# Optimizing a Trainium2 kernel written in Bass

```python
import numpy as np
import jax
import jax.numpy as jnp

def _softmax(x, axis=-1):
    return jax.nn.softmax(x, axis=axis)

def _gelu(x):
    return jax.nn.gelu(x, approximate=True)

def _silu(x):
    return jax.nn.silu(x)

def _sigmoid(x):
    return jax.nn.sigmoid(x)

def _layernorm(x, axis=-1, eps=1e-05):
    m = jnp.mean(x, axis=axis, keepdims=True)
    v = jnp.var(x, axis=axis, keepdims=True)
    return (x - m) / jnp.sqrt(v + eps)

def _scatter_add(tgt, idx, src, axis=0):
    return tgt.at[idx].add(src)

def _segment_sum(src, seg, n):
    return jax.ops.segment_sum(src, seg, n)
kernel_name = 'mk_gnn_ffn_d2_gnn_r32_b489b9'

def setup_inputs(seed: int=0):
    np.random.seed(seed)
    _w = jnp.asarray

    def _rec_inputs():
        import jax
        import jax.numpy as jnp
        _gk = jax.random.key(seed)
        x = -0.0003713 + 1 * jax.random.normal(jax.random.fold_in(_gk, 1), (3125, 256), jnp.float32)
        src = jax.random.randint(jax.random.fold_in(_gk, 2), (50000,), 0, 3125, jnp.int32)
        dst = jnp.minimum((3125 * jax.random.uniform(jax.random.fold_in(_gk, 3), (50000,)) ** 2.0).astype(jnp.int32), 99999)
        _o = jnp.argsort(dst, stable=True)
        src = src[_o]
        dst = dst[_o]
        return (x, src, dst)
    x, src, dst = _rec_inputs()

    def _L0_gnn_setup():
        import jax, jax.numpy as jnp
        import numpy as np
        N_NODES = 50000
        N_EDGES = 25000
        IN_DIM = 256
        OUT_DIM = 32
        NUM_HEADS = 8
        key = jax.random.key(seed)
        ks = jax.random.split(key, 9)
        h = jax.random.normal(ks[0], (N_NODES, IN_DIM), dtype=jnp.float32)
        src = jax.random.randint(ks[1], (N_EDGES,), 0, N_NODES, dtype=jnp.int32)
        dst = jax.random.randint(ks[2], (N_EDGES,), 0, N_NODES, dtype=jnp.int32)
        s = 1.0 / np.sqrt(IN_DIM)
        W_lin = jax.random.uniform(ks[3], (IN_DIM, IN_DIM), jnp.float32, -s, s)
        b_lin = jax.random.uniform(ks[4], (IN_DIM,), jnp.float32, -s, s)
        W_gat = jax.random.normal(ks[5], (IN_DIM, NUM_HEADS * OUT_DIM), dtype=jnp.float32) * s
        attn_l = jax.random.normal(ks[6], (NUM_HEADS, OUT_DIM), dtype=jnp.float32) * 0.1
        attn_r = jax.random.normal(ks[7], (NUM_HEADS, OUT_DIM), dtype=jnp.float32) * 0.1
        gat_bias = jnp.zeros((NUM_HEADS * OUT_DIM,), dtype=jnp.float32)
        return {'h': h, 'src': src, 'dst': dst, 'W_lin': W_lin, 'b_lin': b_lin, 'W_gat': W_gat, 'attn_l': attn_l, 'attn_r': attn_r, 'gat_bias': gat_bias}
    _L0_gnn_all = _L0_gnn_setup()
    _L0_gnn_in = {k: v for k, v in _L0_gnn_all.items() if k in ('W_lin', 'b_lin', 'W_gat', 'attn_l', 'attn_r', 'gat_bias')}
    del _L0_gnn_all

    def _L0_ffn_setup():
        import jax, jax.numpy as jnp
        import numpy as np
        DIM = 256
        H = 8
        D = 64
        G = 64
        INNER = H * D
        SCALE = D ** (-0.5)
        key = jax.random.key(seed)
        ks = jax.random.split(key, 12)
        B, N = (4, 512)
        x = jax.random.normal(ks[0], (B, N, DIM), dtype=jnp.float32)
        s = lambda fan_in: 1.0 / np.sqrt(fan_in)
        W_fx = jax.random.normal(ks[1], (DIM, INNER), dtype=jnp.float32) * s(DIM)
        b_fx = jnp.zeros((INNER,), dtype=jnp.float32)
        W_x = jax.random.normal(ks[2], (DIM, INNER), dtype=jnp.float32) * s(DIM)
        b_x = jnp.zeros((INNER,), dtype=jnp.float32)
        A = jax.random.normal(ks[3], (G, D), dtype=jnp.float32)
        Q, _ = jnp.linalg.qr(A.T)
        W_slice = Q[:, :G].astype(jnp.float32)
        b_slice = jnp.zeros((G,), dtype=jnp.float32)
        W_q = jax.random.normal(ks[4], (D, D), dtype=jnp.float32) * s(D)
        W_k = jax.random.normal(ks[5], (D, D), dtype=jnp.float32) * s(D)
        W_v = jax.random.normal(ks[6], (D, D), dtype=jnp.float32) * s(D)
        W_out = jax.random.normal(ks[7], (INNER, DIM), dtype=jnp.float32) * s(INNER)
        b_out = jnp.zeros((DIM,), dtype=jnp.float32)
        temperature = jnp.ones((1, H, 1, 1), dtype=jnp.float32) * 0.5
        return {'x': x, 'W_fx': W_fx, 'b_fx': b_fx, 'W_x': W_x, 'b_x': b_x, 'W_slice': W_slice, 'b_slice': b_slice, 'W_q': W_q, 'W_k': W_k, 'W_v': W_v, 'W_out': W_out, 'b_out': b_out, 'temperature': temperature}
    _L0_ffn_all = _L0_ffn_setup()
    _L0_ffn_in = {k: v for k, v in _L0_ffn_all.items() if k in ('W_fx', 'b_fx', 'W_x', 'b_x', 'W_slice', 'b_slice', 'W_q', 'W_k', 'W_v', 'W_out', 'b_out', 'temperature')}
    del _L0_ffn_all

    def _L1_gnn_setup():
        import jax, jax.numpy as jnp
        import numpy as np
        N = 50000
        E = 15625
        D = 256
        key = jax.random.key(seed)
        ks = jax.random.split(key, 12)
        s = 0.02
        x = jax.random.normal(ks[0], (N, D), dtype=jnp.float32)
        edge_index = jax.random.randint(ks[1], (2, E), 0, N, dtype=jnp.int64)
        W1 = jax.random.normal(ks[2], (D, 2 * D), dtype=jnp.float32) * s
        b1 = jax.random.normal(ks[3], (D,), dtype=jnp.float32) * s
        W2 = jax.random.normal(ks[4], (D, D), dtype=jnp.float32) * s
        b2 = jax.random.normal(ks[5], (D,), dtype=jnp.float32) * s
        w_ih = jax.random.normal(ks[6], (3 * D, D), dtype=jnp.float32) * s
        w_hh = jax.random.normal(ks[7], (3 * D, D), dtype=jnp.float32) * s
        b_ih = jax.random.normal(ks[8], (3 * D,), dtype=jnp.float32) * s
        b_hh = jax.random.normal(ks[9], (3 * D,), dtype=jnp.float32) * s
        gamma = jnp.ones((D,), dtype=jnp.float32)
        beta = jnp.zeros((D,), dtype=jnp.float32)
        return {'x': x, 'edge_index': edge_index, 'W1': W1, 'b1': b1, 'W2': W2, 'b2': b2, 'w_ih': w_ih, 'w_hh': w_hh, 'b_ih': b_ih, 'b_hh': b_hh, 'gamma': gamma, 'beta': beta}
    _L1_gnn_all = _L1_gnn_setup()
    _L1_gnn_in = {k: v for k, v in _L1_gnn_all.items() if k in ('W1', 'b1', 'W2', 'b2', 'w_ih', 'w_hh', 'b_ih', 'b_hh', 'gamma', 'beta')}
    del _L1_gnn_all

    def _L1_ffn_setup():
        import jax, jax.numpy as jnp
        import numpy as np
        D_MODEL = 256
        EXPERT_DIM = 512
        NUM_EXPERTS = 8
        TOP_K = 2
        SEQ_LEN = 64
        BATCH = 2
        key = jax.random.key(seed)
        ks = jax.random.split(key, 8)
        s = 0.02
        x = jax.random.normal(ks[0], (SEQ_LEN, BATCH, D_MODEL), dtype=jnp.float32)
        Wg = jax.random.normal(ks[1], (D_MODEL, NUM_EXPERTS), dtype=jnp.float32) * s
        bg = jax.random.normal(ks[2], (NUM_EXPERTS,), dtype=jnp.float32) * s
        bias = jnp.zeros((NUM_EXPERTS,), dtype=jnp.float32)
        W1 = jax.random.normal(ks[3], (NUM_EXPERTS, D_MODEL, EXPERT_DIM), dtype=jnp.float32) * s
        b1 = jax.random.normal(ks[4], (NUM_EXPERTS, EXPERT_DIM), dtype=jnp.float32) * s
        W2 = jax.random.normal(ks[5], (NUM_EXPERTS, EXPERT_DIM, D_MODEL), dtype=jnp.float32) * s
        b2 = jax.random.normal(ks[6], (NUM_EXPERTS, D_MODEL), dtype=jnp.float32) * s
        return {'x': x, 'Wg': Wg, 'bg': bg, 'bias': bias, 'W1': W1, 'b1': b1, 'W2': W2, 'b2': b2}
    _L1_ffn_all = _L1_ffn_setup()
    _L1_ffn_in = {k: v for k, v in _L1_ffn_all.items() if k in ('Wg', 'bg', 'bias', 'W1', 'b1', 'W2', 'b2')}
    del _L1_ffn_all
    return {'x': x, 'src': src, 'dst': dst, 'L0_gnn_W_lin': _L0_gnn_in['W_lin'], 'L0_gnn_b_lin': _L0_gnn_in['b_lin'], 'L0_gnn_W_gat': _L0_gnn_in['W_gat'], 'L0_gnn_attn_l': _L0_gnn_in['attn_l'], 'L0_gnn_attn_r': _L0_gnn_in['attn_r'], 'L0_gnn_gat_bias': _L0_gnn_in['gat_bias'], 'L0_ffn_W_fx': _L0_ffn_in['W_fx'], 'L0_ffn_b_fx': _L0_ffn_in['b_fx'], 'L0_ffn_W_x': _L0_ffn_in['W_x'], 'L0_ffn_b_x': _L0_ffn_in['b_x'], 'L0_ffn_W_slice': _L0_ffn_in['W_slice'], 'L0_ffn_b_slice': _L0_ffn_in['b_slice'], 'L0_ffn_W_q': _L0_ffn_in['W_q'], 'L0_ffn_W_k': _L0_ffn_in['W_k'], 'L0_ffn_W_v': _L0_ffn_in['W_v'], 'L0_ffn_W_out': _L0_ffn_in['W_out'], 'L0_ffn_b_out': _L0_ffn_in['b_out'], 'L0_ffn_temperature': _L0_ffn_in['temperature'], 'L1_gnn_W1': _L1_gnn_in['W1'], 'L1_gnn_b1': _L1_gnn_in['b1'], 'L1_gnn_W2': _L1_gnn_in['W2'], 'L1_gnn_b2': _L1_gnn_in['b2'], 'L1_gnn_w_ih': _L1_gnn_in['w_ih'], 'L1_gnn_w_hh': _L1_gnn_in['w_hh'], 'L1_gnn_b_ih': _L1_gnn_in['b_ih'], 'L1_gnn_b_hh': _L1_gnn_in['b_hh'], 'L1_gnn_gamma': _L1_gnn_in['gamma'], 'L1_gnn_beta': _L1_gnn_in['beta'], 'L1_ffn_Wg': _L1_ffn_in['Wg'], 'L1_ffn_bg': _L1_ffn_in['bg'], 'L1_ffn_bias': _L1_ffn_in['bias'], 'L1_ffn_W1': _L1_ffn_in['W1'], 'L1_ffn_b1': _L1_ffn_in['b1'], 'L1_ffn_W2': _L1_ffn_in['W2'], 'L1_ffn_b2': _L1_ffn_in['b2']}

def reference(x, src, dst, L0_gnn_W_lin, L0_gnn_b_lin, L0_gnn_W_gat, L0_gnn_attn_l, L0_gnn_attn_r, L0_gnn_gat_bias, L0_ffn_W_fx, L0_ffn_b_fx, L0_ffn_W_x, L0_ffn_b_x, L0_ffn_W_slice, L0_ffn_b_slice, L0_ffn_W_q, L0_ffn_W_k, L0_ffn_W_v, L0_ffn_W_out, L0_ffn_b_out, L0_ffn_temperature, L1_gnn_W1, L1_gnn_b1, L1_gnn_W2, L1_gnn_b2, L1_gnn_w_ih, L1_gnn_w_hh, L1_gnn_b_ih, L1_gnn_b_hh, L1_gnn_gamma, L1_gnn_beta, L1_ffn_Wg, L1_ffn_bg, L1_ffn_bias, L1_ffn_W1, L1_ffn_b1, L1_ffn_W2, L1_ffn_b2):
    import jax
    import jax.numpy as jnp

    def _L0_gnn_ref(h, src, dst, W_lin, b_lin, W_gat, attn_l, attn_r, gat_bias):
        import jax, jax.numpy as jnp
        import numpy as np
        N_NODES = 50000
        N_EDGES = 25000
        IN_DIM = 256
        OUT_DIM = 32
        NUM_HEADS = 8
        N = h.shape[0]
        h = h @ W_lin + b_lin
        h_in = h
        feat = (h @ W_gat).reshape(N, NUM_HEADS, OUT_DIM)
        el = jnp.sum(feat * attn_l, axis=-1)
        er = jnp.sum(feat * attn_r, axis=-1)
        e = jax.nn.leaky_relu(el[src] + er[dst], 0.2)
        m = jax.ops.segment_max(e, dst, num_segments=N)
        m = jnp.where(jnp.isfinite(m), m, 0.0)
        e = jnp.exp(e - m[dst])
        s = jax.ops.segment_sum(e, dst, num_segments=N)
        a = e / s[dst]
        msg = feat[src] * a[:, :, None]
        out = jax.ops.segment_sum(msg, dst, num_segments=N)
        out = out.reshape(N, NUM_HEADS * OUT_DIM) + gat_bias
        out = jax.nn.leaky_relu(out, 0.01)
        return h_in + out

    def _L0_ffn_ref(x, W_fx, b_fx, W_x, b_x, W_slice, b_slice, W_q, W_k, W_v, W_out, b_out, temperature):
        import jax, jax.numpy as jnp
        import numpy as np
        DIM = 256
        H = 8
        D = 64
        G = 64
        INNER = H * D
        SCALE = D ** (-0.5)
        B, N, _ = x.shape
        fx_mid = (x @ W_fx + b_fx).reshape(B, N, H, D).transpose(0, 2, 1, 3)
        x_mid = (x @ W_x + b_x).reshape(B, N, H, D).transpose(0, 2, 1, 3)
        temp = jnp.clip(temperature, 0.1, 5.0)
        slice_weights = jax.nn.softmax((x_mid @ W_slice + b_slice) / temp, axis=-1)
        slice_norm = slice_weights.sum(axis=2)
        slice_token = jnp.einsum('bhnc,bhng->bhgc', fx_mid, slice_weights)
        slice_token = slice_token / (slice_norm[..., None] + 1e-05)
        q = slice_token @ W_q
        k = slice_token @ W_k
        v = slice_token @ W_v
        attn = jax.nn.softmax(jnp.einsum('bhgc,bhkc->bhgk', q, k) * SCALE, axis=-1)
        out_slice = jnp.einsum('bhgk,bhkc->bhgc', attn, v)
        out_x = jnp.einsum('bhgc,bhng->bhnc', out_slice, slice_weights)
        out_x = out_x.transpose(0, 2, 1, 3).reshape(B, N, INNER)
        return out_x @ W_out + b_out

    def _L1_gnn_ref(x, edge_index, W1, b1, W2, b2, w_ih, w_hh, b_ih, b_hh, gamma, beta):
        import jax, jax.numpy as jnp
        import numpy as np
        N = 50000
        E = 15625
        D = 256
        n_nodes = x.shape[0]
        row, col = (edge_index[0], edge_index[1])
        h = jnp.concatenate([x[row], x[col]], axis=-1)
        msgs = jax.nn.silu(h @ W1.T + b1) @ W2.T + b2
        agg = jax.ops.segment_sum(msgs, row, num_segments=n_nodes)
        cnt = jax.ops.segment_sum(jnp.ones((row.shape[0], 1), x.dtype), row, num_segments=n_nodes)
        agg = agg / (cnt + 1e-08)
        gi = agg @ w_ih.T + b_ih
        gh = x @ w_hh.T + b_hh
        i_r, i_z, i_n = jnp.split(gi, 3, axis=-1)
        h_r, h_z, h_n = jnp.split(gh, 3, axis=-1)
        r = jax.nn.sigmoid(i_r + h_r)
        z = jax.nn.sigmoid(i_z + h_z)
        n = jnp.tanh(i_n + r * h_n)
        x_new = (1.0 - z) * n + z * x
        mu = jnp.mean(x_new, axis=-1, keepdims=True)
        var = jnp.var(x_new, axis=-1, keepdims=True)
        return gamma * (x_new - mu) / jnp.sqrt(var + 1e-05) + beta

    def _L1_ffn_ref(x, Wg, bg, bias, W1, b1, W2, b2):
        import jax, jax.numpy as jnp
        import numpy as np
        D_MODEL = 256
        EXPERT_DIM = 512
        NUM_EXPERTS = 8
        TOP_K = 2
        SEQ_LEN = 64
        BATCH = 2
        x_flat = x.reshape(-1, D_MODEL)
        gate_logits = x_flat @ Wg + bg + bias
        topk_vals, topk_idx = jax.lax.top_k(gate_logits, TOP_K)
        topk_w = jax.nn.softmax(topk_vals, axis=-1)
        combine = (jax.nn.one_hot(topk_idx, NUM_EXPERTS, dtype=x.dtype) * topk_w[..., None]).sum(axis=1)
        h = jax.nn.relu(jnp.einsum('td,edh->teh', x_flat, W1) + b1)
        y = jnp.einsum('teh,ehd->ted', h, W2) + b2
        out = jnp.einsum('ted,te->td', y, combine)
        return out.reshape(x.shape)
    edge_index = jnp.stack([src, dst])
    x = x + _L0_gnn_ref(_layernorm(x, axis=-1), src, dst, L0_gnn_W_lin, L0_gnn_b_lin, L0_gnn_W_gat, L0_gnn_attn_l, L0_gnn_attn_r, L0_gnn_gat_bias)
    x = x + _L0_ffn_ref(_layernorm(x, axis=-1)[None], L0_ffn_W_fx, L0_ffn_b_fx, L0_ffn_W_x, L0_ffn_b_x, L0_ffn_W_slice, L0_ffn_b_slice, L0_ffn_W_q, L0_ffn_W_k, L0_ffn_W_v, L0_ffn_W_out, L0_ffn_b_out, L0_ffn_temperature)[0]
    x = x + _L1_gnn_ref(_layernorm(x, axis=-1), edge_index, L1_gnn_W1, L1_gnn_b1, L1_gnn_W2, L1_gnn_b2, L1_gnn_w_ih, L1_gnn_w_hh, L1_gnn_b_ih, L1_gnn_b_hh, L1_gnn_gamma, L1_gnn_beta)
    x = x + _L1_ffn_ref(_layernorm(x, axis=-1)[None], L1_ffn_Wg, L1_ffn_bg, L1_ffn_bias, L1_ffn_W1, L1_ffn_b1, L1_ffn_W2, L1_ffn_b2)[0]
    return x

_drawn_inputs = setup_inputs


def setup_inputs(seed=0):
    import zlib

    import numpy as np

    out = dict(_drawn_inputs(seed))
    spreads = {'L0_gnn_gat_bias': (0.0, 0.1),
     'L0_ffn_b_fx': (0.0, 0.1),
     'L0_ffn_b_x': (0.0, 0.8),
     'L0_ffn_b_slice': (0.0, 0.8),
     'L0_ffn_b_out': (0.0, 0.1),
     'L0_ffn_temperature': (0.5, 0.6),
     'L1_gnn_gamma': (1.0, 0.2),
     'L1_gnn_beta': (0.0, 0.1),
     'L1_ffn_bias': (0.0, 0.556)}
    factors = {'L0_gnn_attn_r': 5.389,
     'L0_ffn_W_x': 8.0,
     'L0_ffn_W_slice': 8.0,
     'L0_ffn_W_q': 8.0,
     'L0_ffn_W_k': 8.0,
     'L1_gnn_W1': 6.111,
     'L1_gnn_b1': 8.0,
     'L1_gnn_W2': 5.877,
     'L1_gnn_b2': 8.0,
     'L1_gnn_w_ih': 5.47,
     'L1_gnn_b_ih': 17.026,
     'L1_gnn_b_hh': 21.813,
     'L1_ffn_bg': 8.0,
     'L1_ffn_b1': 25.748,
     'L1_ffn_b2': 8.0}
    for name, (base, spread) in spreads.items():
        noise = np.random.default_rng([zlib.crc32(name.encode()), seed]).standard_normal(out[name].shape)
        drawn = base * np.exp(spread * noise) if base else spread * noise
        out[name] = jnp.asarray(drawn.astype(out[name].dtype))
    for name, factor in factors.items():
        out[name] = (out[name] * factor).astype(out[name].dtype)
    return out
```

```python
from contextlib import ExitStack

import concourse.bass as bass
from concourse import mybir
from concourse.alu_op_type import AluOpType as ALU

ACT = mybir.ActivationFunctionType
F32 = mybir.dt.float32
I32 = mybir.dt.int32
AX = mybir.AxisListType.X
DVE, SP = mybir.EngineType.DVE, mybir.EngineType.SP
PE = mybir.EngineType.PE

P = 128
N = 3125
NT = -(-N // P)
NP = NT * P
TAIL = N - (NT - 1) * P
D = 256
KC = D // P
E = 50000
EC = 392
EP = P * EC
EFULL = E // EC
EREST = E - EFULL * EC
ST = (EP + NT * (P - 1)) // P
ER = EP + P
H1 = 8
HD = D // H1
SH, SD = 8, 64
SI = SH * SD
PAIRS = SH // 2
NE, ED = 8, 512
EK = ED // P
U = 5
GROUPS = NT // U
BIG = 1.0e30
EPS = 1e-5
RSLOTS = 8
VSLOTS = 4
assert NT % U == 0 and ST % RSLOTS == 0 and EC % 28 == 0 and EREST < EC


class Kept:

    def __init__(self, nc, tables):
        self.nc, self.t, self.count, self.semaphores = nc, tables, 0, []


class Steps:

    def __init__(self, engine, semaphore, start=0):
        self.engine, self.semaphore, self.n = engine, semaphore, start

    def __call__(self, instruction):
        instruction.then_inc(self.semaphore, 1)
        self.n = self.n + 1
        self.engine.wait_ge(self.semaphore, self.n)


def phase(k):
    ctx = ExitStack()
    nc = k.nc
    k.count += 1
    tag = f"p{k.count}_"

    def sb(name, shape, dtype=F32):
        return ctx.enter_context(nc.sbuf_tensor(tag + name, shape, dtype))

    def sem(name):
        handle = nc.alloc_semaphore(name=tag + name)
        k.semaphores.append(handle)
        return handle

    return ctx, sb, sem


def emit_norm(k, dve, st, mv, stats_ready, sqrt_ready, steps):
    nc = k.nc
    with dve.Fori(0, GROUPS) as g:
        for u in range(U):
            last = nc.vector.bn_stats(st[:, bass.ts(g * U + u, 6)], k.xs[:, bass.ts(g * U + u, D)])
        last.then_inc(steps.semaphore, 1)
    steps.n += GROUPS
    dve.wait_ge(steps.semaphore, steps.n)
    emit_moments(k, dve, st, mv, stats_ready, sqrt_ready, steps)


def emit_moments(k, dve, st, mv, stats_ready, sqrt_ready, steps):
    nc = k.nc
    s = st[:].rearrange("p (i c) -> p i c", c=6)
    mean, var, dif = mv[:, 0, :], mv[:, 1, :], mv[:, 2, :]
    steps(nc.vector.tensor_tensor(dif, s[:, :, 1], s[:, :, 4], ALU.subtract))
    steps(nc.vector.tensor_tensor(var, s[:, :, 2], s[:, :, 5], ALU.add))
    steps(nc.vector.tensor_tensor(dif, dif, dif, ALU.mult))
    steps(nc.vector.tensor_scalar(dif, dif, 0.25, None, ALU.mult))
    steps(nc.vector.scalar_tensor_tensor(out=var, in0=var, scalar=1.0 / D, in1=dif, op0=ALU.mult, op1=ALU.add))
    steps(nc.vector.tensor_tensor(mean, s[:, :, 1], s[:, :, 4], ALU.add))
    steps(nc.vector.tensor_scalar(mean, mean, 0.5, None, ALU.mult))
    nc.vector.tensor_scalar(mv[:, 3, :], var, EPS, None, ALU.add).then_inc(stats_ready, 1)
    rstd = mv[:, 4, :]
    dve.wait_ge(sqrt_ready, 1)
    steps(nc.vector.reciprocal(rstd, rstd))
    steps(nc.vector.tensor_tensor(dif, rstd, rstd, ALU.mult))
    steps(nc.vector.tensor_tensor(dif, dif, mv[:, 3, :], ALU.mult))
    steps(nc.vector.tensor_scalar(dif, dif, -0.5, 1.5, ALU.mult, ALU.add))
    steps(nc.vector.tensor_tensor(rstd, rstd, dif, ALU.mult))


def emit_sqrt(k, act, mv, stats_ready, sqrt_ready):
    act.wait_ge(stats_ready, 1)
    k.nc.scalar.activation(mv[:, 4, :], mv[:, 3, :], ACT.Sqrt).then_inc(sqrt_ready, 1)


def load_weights(k, sp, sem, pairs):
    for dst, src in pairs:
        sp.dma_start(dst, src).then_inc(sem, 16)
    return 16 * len(pairs)


def row(v):
    return v.rearrange("(a d) -> a d", a=1)


def across(v):
    return row(v).to_broadcast([P, v.shape[0]])


def chunks(w):
    return w.rearrange("(c p) n -> p c n", p=P)


def setup(k):
    nc, t = k.nc, k.t
    ctx, sb, sem = phase(k)
    with ctx:
        loaded, made, made2 = sem("loaded"), sem("made"), sem("made2")
        dve_step = sem("dve_step")
        bkt_i, bkt = sb("bucket_i", [P, EC], I32), sb("bucket", [P, EC])
        junk, scan, part = sb("junk", [P, EC]), sb("scan", [P, EC]), sb("part", [P, EC])
        ones_e = sb("ones_e", [P, EC])
        pos = sb("pos", [P, EC])
        counts = sb("counts", [P, NT])
        src_f = sb("src_f", [P, EC])
        small = sb("small", [P, 8])
        small_i = sb("small_i", [P, 8], I32)
        tot, off = sb("tot", [P, NT]), sb("off", [P, NT])
        grid, vrow = sb("grid", [NT, ST]), sb("vrow", [NT, P])
        starts = sb("starts", [P, ST])
        iota_q = sb("iota_q", [P, ST])
        pad10, pad2 = sb("pad10", [P, 10], I32), sb("pad2", [P, 2], I32)
        pad_f = sb("pad_f", [P, 1])
        counted, summed, tiles_ready, cum_ready, grid_ready, table_ready = (
            sem(s) for s in ("counted", "summed", "tiles_ready", "cum_ready", "grid_ready", "table_ready"))
        pads_made, pads_stored = sem("pads_made"), sem("pads_stored")
        edges_filled, x_filled = sem("edges_filled"), sem("x_filled")

        with nc.Block() as block:
            @block.sync
            def _(sp):
                sp.wait_ge(x_filled, 1)
                sp.dma_start(k.xs[:, 0:(NT - 1) * D].rearrange("p (i d) -> p i d", d=D),
                             t["x"][0:(NT - 1) * P, :].rearrange("(i p) d -> p i d", p=P)).then_inc(loaded, 16)
                sp.dma_start(k.xs[0:TAIL, (NT - 1) * D:NT * D], t["x"][(NT - 1) * P:N, :]).then_inc(loaded, 16)
                sp.wait_ge(edges_filled, 2)
                for dst, src in ((k.dst_i, t["dst"]), (k.src_i, t["src"])):
                    sp.dma_start(dst[0:EFULL, :], src[0:EFULL * EC].rearrange("(p j) -> p j", j=EC)).then_inc(loaded, 16)
                    sp.dma_start(dst[EFULL:EFULL + 1, 0:EREST], row(src[EFULL * EC:E])).then_inc(loaded, 16)
                sp.wait_ge(pads_made, 5)
                sp.dma_start(t["rec_gat"][EP:ER, :], pad10[:]).then_inc(pads_stored, 16)
                sp.dma_start(t["rec_src"][EP:ER, :], pad2[:]).then_inc(pads_stored, 16)
                sp.wait_ge(pads_stored, 32)

            @block.gpsimd
            def _(pool):
                nc.gpsimd.memset(k.xs[:, (NT - 1) * D:NT * D], 0.0).then_inc(x_filled, 1)
                nc.gpsimd.memset(k.dst_i[:], NP - 1).then_inc(edges_filled, 1)
                nc.gpsimd.memset(k.src_i[:], NP - 1).then_inc(edges_filled, 1)
                nc.gpsimd.memset(pad_f[:], float(NP - 1)).then_inc(pads_made, 1)
                nc.gpsimd.memset(pad10[:], 0).then_inc(pads_made, 1)
                pool.wait_ge(pads_made, 2)
                nc.gpsimd.memset(pad10[:, 0:1], NP - 1).then_inc(pads_made, 1)
                nc.gpsimd.memset(pad2[:, 0:1], NP - 1).then_inc(pads_made, 1)
                nc.gpsimd.memset(k.ident[:], 0.0).then_inc(made, 1)
                nc.gpsimd.memset(k.ones[:], 1.0).then_inc(made, 1)
                nc.gpsimd.memset(k.tri_incl[:], 1.0).then_inc(made, 1)
                nc.gpsimd.memset(k.tri_strict[:], 1.0).then_inc(made, 1)
                nc.gpsimd.memset(k.mask[:], 1.0).then_inc(made, 1)
                nc.gpsimd.iota(k.iota[:], pattern=[[1, P]], base=0, channel_multiplier=0,
                               allow_small_or_imprecise_dtypes=True).then_inc(made, 1)
                nc.gpsimd.iota(iota_q[:], pattern=[[1, ST]], base=0, channel_multiplier=0,
                               allow_small_or_imprecise_dtypes=True).then_inc(made, 1)
                pool.wait_ge(made, 7)
                nc.gpsimd.affine_select(out=k.ident[:], in_=k.ident[:], compare_op=ALU.not_equal, fill=1.0,
                                        base=0, pattern=[[-1, P]], channel_multiplier=1).then_inc(made2, 1)
                nc.gpsimd.affine_select(out=k.tri_incl[:], in_=k.tri_incl[:], compare_op=ALU.is_ge, fill=0.0,
                                        base=0, pattern=[[1, P]], channel_multiplier=-1).then_inc(made2, 1)
                nc.gpsimd.affine_select(out=k.tri_strict[:], in_=k.tri_strict[:], compare_op=ALU.is_ge, fill=0.0,
                                        base=-1, pattern=[[1, P]], channel_multiplier=-1).then_inc(made2, 1)
                nc.gpsimd.affine_select(out=k.mask[:, NT - 1:NT], in_=k.mask[:, NT - 1:NT], compare_op=ALU.is_ge,
                                        fill=0.0, base=TAIL - 1, pattern=[[0, 1]],
                                        channel_multiplier=-1).then_inc(made2, 1)

            @block.vector
            def _(dve):
                step = Steps(dve, dve_step)
                dve.wait_ge(pads_made, 4)
                step(nc.vector.tensor_copy(pad10[:, 1:2].bitcast(F32), pad_f[:]))
                nc.vector.tensor_copy(pad2[:, 1:2].bitcast(F32), pad_f[:]).then_inc(pads_made, 1)
                step(nc.vector.memset(ones_e[:], 1.0))
                dve.wait_ge(made2, 4)
                dve.wait_ge(loaded, 96)
                step(nc.vector.tensor_copy(k.dst_f[:], k.dst_i[:]))
                step(nc.vector.tensor_copy(src_f[:], k.src_i[:]))
                for n, (key, base, start, tile) in enumerate(((k.dst_i, k.base_dst, k.start_dst, k.tile_dst),
                                                              (k.src_i, k.base_src, k.start_src, k.tile_src))):
                    step(nc.vector.tensor_scalar(bkt_i[:], key[:], 7, None, ALU.arith_shift_right))
                    step(nc.vector.tensor_copy(bkt[:], bkt_i[:]))
                    for b in range(NT):
                        last = nc.vector.tensor_scalar(junk[:], bkt[:], float(b), 0.0, ALU.is_equal, ALU.add,
                                                       accum_out=counts[:, b:b + 1])
                        if b < NT - 1:
                            step(last)
                    last.then_inc(counted, 1)
                    dve.wait_ge(summed, n + 1)
                    step(nc.vector.tensor_scalar(small[0:NT, 0:1], k.ps[0:NT, 0, 0:1], float(P - 1), None, ALU.add))
                    step(nc.vector.tensor_copy(small_i[0:NT, 0:1], small[0:NT, 0:1]))
                    step(nc.vector.tensor_scalar(small_i[0:NT, 1:2], small_i[0:NT, 0:1], 7, None,
                                                 ALU.arith_shift_right))
                    step(nc.vector.tensor_copy(small[0:NT, 1:2], small_i[0:NT, 1:2]))
                    step(nc.vector.scalar_tensor_tensor(out=small[0:NT, 2:3], in0=small[0:NT, 1:2], scalar=-float(P),
                                                        in1=k.ps[0:NT, 0, 0:1], op0=ALU.mult, op1=ALU.add))
                    nc.vector.tensor_scalar(vrow[:], k.ones[0:NT, :], small[0:NT, 2:3], None,
                                            ALU.mult).then_inc(tiles_ready, 1)
                    dve.wait_ge(cum_ready, n + 1)
                    nc.vector.tensor_scalar(grid[:], iota_q[0:NT, :], k.ps[0:NT, 3, 0:1], None,
                                            ALU.is_ge).then_inc(grid_ready, 1)
                    dve.wait_ge(table_ready, n + 1)
                    step(nc.vector.tensor_scalar(base[:], k.ps[:, 4, 0:ST], float(NT - 1), None, ALU.min))
                    step(nc.vector.tensor_copy(tile[:], base[0:1, :]))
                    step(nc.vector.tensor_scalar(base[:], base[:], float(P), None, ALU.mult))
                    step(nc.vector.scalar_tensor_tensor(out=starts[:], in0=iota_q[:], scalar=float(P),
                                                        in1=k.ps[:, 5, 0:ST], op0=ALU.mult, op1=ALU.add))
                    step(nc.vector.tensor_scalar(starts[:], starts[:], float(EP), None, ALU.min))
                    step(nc.vector.tensor_copy(start[:], starts[0:1, :]))
                step(nc.vector.tensor_copy(tot[:], k.ps[:, 1, 0:NT]))
                step(nc.vector.tensor_tensor_scan(off[:], ones_e[:, 0:NT], tot[:], -1.0, ALU.mult, ALU.add))
                step(nc.vector.tensor_tensor(off[:], off[:], tot[:], ALU.subtract))
                step(nc.vector.tensor_tensor(off[:], off[:], k.ps[:, 2, 0:NT], ALU.add))
                step(nc.vector.memset(pos[:], 0.0))
                for b in range(NT):
                    step(nc.vector.tensor_scalar(part[:], bkt[:], float(b), None, ALU.is_equal))
                    step(nc.vector.tensor_tensor_scan(scan[:], ones_e[:], part[:], off[:, b:b + 1], ALU.mult, ALU.add))
                    step(nc.vector.tensor_tensor(part[:], part[:], scan[:], ALU.mult))
                    step(nc.vector.tensor_tensor(pos[:], pos[:], part[:], ALU.add))
                step(nc.vector.tensor_copy(k.pos_i[:], pos[:]))
                rec = k.edge_rec[:].rearrange("p (j c) -> p j c", c=2)
                step(nc.vector.tensor_copy(rec[:, :, 0], k.dst_i[:]))
                step(nc.vector.tensor_copy(rec[:, :, 1].bitcast(F32), src_f[:]))

            @block.tensor
            def _(pe):
                pe.wait_ge(made2, 4)
                for n in range(2):
                    pe.wait_ge(counted, n + 1)
                    if n:
                        pe.wait_ge(table_ready, 1)
                    nc.tensor.matmul(k.ps[0:NT, 0, 0:1], counts[:], k.ones[:, 0:1], start=True, stop=True)
                    nc.tensor.matmul(k.ps[:, 1, 0:NT], k.ones[:], counts[:], start=True, stop=True)
                    nc.tensor.matmul(k.ps[:, 2, 0:NT], k.tri_strict[:], counts[:], start=True,
                                     stop=True).then_inc(summed, 1)
                    pe.wait_ge(tiles_ready, n + 1)
                    nc.tensor.matmul(k.ps[0:NT, 3, 0:1], k.tri_incl[0:NT, 0:NT], small[0:NT, 1:2], start=True,
                                     stop=True).then_inc(cum_ready, 1)
                    pe.wait_ge(grid_ready, n + 1)
                    nc.tensor.matmul(k.ps[:, 4, 0:ST], k.ones[0:NT, :], grid[:], start=True, stop=True)
                    nc.tensor.matmul(k.ps[:, 5, 0:ST], vrow[:], grid[:], start=True,
                                     stop=True).then_inc(table_ready, 1)


def gat_tables(k):
    nc, t = k.nc, k.t
    ctx, sb, sem = phase(k)
    C = 2 * D + 2 * H1
    with ctx:
        w_lin_t, w_gat = sb("w_lin_t", [P, KC, D]), sb("w_gat", [P, KC, D])
        b_col = sb("b_col", [P, KC])
        att = sb("att", [P, KC, 2 * H1])
        fused_t = sb("fused_t", [P, KC, D])
        w_all = sb("w_all", [P, KC, C])
        bias_row = sb("bias_row", [1, C])
        bias_col = sb("bias_col", [P, KC])
        bias = sb("bias", [P, C])
        st, mv = sb("st", [P, NT * 6]), sb("mv", [P, 5, NT])
        xn, xt = sb("xn", [P, U, D]), sb("xt", [P, U, D])
        out = sb("out", [P, U, D + 2 * H1])
        loaded, zeroed = sem("loaded"), sem("zeroed")
        dve_step, stats_ready, sqrt_ready = sem("dve_step"), sem("stats_ready"), sem("sqrt_ready")
        fused, copied, w_ready = sem("fused"), sem("copied"), sem("w_ready")
        normed, turned, turned_copied, product, added = (
            sem(s) for s in ("normed", "turned", "turned_copied", "product", "added"))
        stored = [sem(f"stored{u}") for u in range(U)]
        hbm = sem("loaded_lin")

        with nc.Block() as block:
            @block.sync
            def _(sp):
                load_weights(k, sp, loaded, [
                    (w_lin_t[:], chunks(t["w_lin_t"])), (w_gat[:], chunks(t["w_gat"])),
                    (b_col[:], t["b_lin_cols"]),
                    (w_all[:, :, 0:D], chunks(t["w_lin"])), (bias_row[:, 0:D], row(t["b_lin"]))])
                sp.wait_ge(zeroed, 1)
                for n, a in enumerate((t["attn_l"], t["attn_r"])):
                    for h in range(H1):
                        p0 = (h * HD) % P
                        sp.dma_start(att[p0:p0 + HD, h * HD // P, n * H1 + h:n * H1 + h + 1],
                                     a[h, :].rearrange("(d a) -> d a", a=1)).then_inc(loaded, 16)
                with sp.Fori(0, GROUPS) as g:
                    for u in range(U):
                        i = g * U + u
                        sp.wait_ge(added, i + 1)
                        sp.dma_start(t["gat_rows"][bass.ts(i, P), :], out[:, u, 0:D]).then_inc(stored[u], 16)
                        sp.dma_start(t["el_rows"][bass.ts(i, P), :], out[:, u, D:D + H1]).then_inc(stored[u], 16)
                        sp.dma_start(t["er_rows"][bass.ts(i, P), :], out[:, u, D + H1:]).then_inc(stored[u], 16)
                for u in range(U):
                    sp.wait_ge(stored[u], 48 * GROUPS)

            @block.gpsimd
            def _(pool):
                nc.gpsimd.memset(att[:], 0.0).then_inc(zeroed, 1)

            @block.vector
            def _(dve):
                step = Steps(dve, dve_step)
                emit_norm(k, dve, st, mv, stats_ready, sqrt_ready, step)
                dve.wait_ge(fused, 1)
                nc.vector.tensor_copy(fused_t[:], k.ps[:, 0:KC, 0:D]).then_inc(copied, 1)
                nc.vector.tensor_copy(w_all[:, :, D:2 * D], k.ps[:, 2:2 + KC, 0:D]).then_inc(copied, 1)
                nc.vector.tensor_copy(bias_row[:, D:2 * D], k.ps[0:1, 4, 0:D]).then_inc(copied, 1)
                nc.vector.tensor_copy(bias_col[:], k.ps[:, 5:5 + KC, 0]).then_inc(copied, 1)
                dve.wait_ge(fused, 2)
                nc.vector.tensor_copy(w_all[:, :, 2 * D:], k.ps[:, 0:KC, 0:2 * H1]).then_inc(copied, 1)
                nc.vector.tensor_copy(bias_row[:, 2 * D:], k.ps[0:1, 4, 0:2 * H1]).then_inc(copied, 1)
                dve.wait_ge(fused, 3)
                nc.vector.tensor_copy(bias[:, 0:ED], k.ps[:, 0, :]).then_inc(copied, 1)
                nc.vector.tensor_copy(bias[:, ED:C], k.ps[:, 1, 0:C - ED]).then_inc(w_ready, 1)
                dve.wait_ge(w_ready, 1)
                dve.wait_ge(copied, 7)
                with dve.Fori(0, GROUPS) as g:
                    for u in range(U):
                        i = g * U + u
                        dve.wait_ge(turned, i + 1)
                        nc.vector.tensor_scalar(xn[:, u, :], k.xs[:, bass.ts(i, D)], mv[:, 0, bass.ds(i, 1)],
                                                mv[:, 4, bass.ds(i, 1)], ALU.subtract,
                                                ALU.mult).then_inc(normed, 1)
                    for u in range(U):
                        i = g * U + u
                        bank = 2 + 2 * (u % 2)
                        dve.wait_ge(product, i + 1)
                        dve.wait_ge(stored[u], 48 * g)
                        nc.vector.tensor_tensor(out[:, u, 0:D], k.ps[:, bank, D:2 * D], bias[:, D:2 * D],
                                                ALU.add)
                        nc.vector.tensor_tensor(out[:, u, D:], k.ps[:, bank + 1, 0:2 * H1], bias[:, 2 * D:],
                                                ALU.add)
                        xsl = k.xs[:, bass.ts(i, D)]
                        nc.vector.tensor_tensor(xsl, xsl, k.ps[:, bank, 0:D], ALU.add).then_inc(dve_step, 1)
                        dve.wait_ge(dve_step, step.n + 1 + i)
                        nc.vector.tensor_tensor(xsl, xsl, bias[:, 0:D], ALU.add).then_inc(added, 1)

            @block.scalar
            def _(act):
                emit_sqrt(k, act, mv, stats_ready, sqrt_ready)
                with act.Fori(0, GROUPS) as g:
                    for u in range(U):
                        i = g * U + u
                        act.wait_ge(turned, i + U + 1)
                        nc.scalar.copy(xt[:, u, :], k.ps[:, u % 2, 0:D]).then_inc(turned_copied, 1)

            @block.tensor
            def _(pe):
                pe.sem_inc(turned, U)
                pe.wait_ge(loaded, 16 * (5 + 2 * H1))
                for m in range(KC):
                    for c in range(KC):
                        nc.tensor.matmul(k.ps[:, m, 0:D], w_gat[:, c, bass.ts(m, P)], w_lin_t[:, c, :],
                                         start=c == 0, stop=c == KC - 1)
                for m in range(KC):
                    for c in range(KC):
                        nc.tensor.matmul(k.ps[:, 2 + m, 0:D], w_lin_t[:, c, bass.ts(m, P)], w_gat[:, c, :],
                                         start=c == 0, stop=c == KC - 1)
                for c in range(KC):
                    nc.tensor.matmul(k.ps[0:1, 4, 0:D], b_col[:, c:c + 1], w_gat[:, c, :],
                                     start=c == 0, stop=c == KC - 1)
                for m in range(KC):
                    for c in range(KC):
                        last = nc.tensor.matmul(k.ps[:, 5 + m, 0:1], w_gat[:, c, bass.ts(m, P)], b_col[:, c:c + 1],
                                                start=c == 0, stop=c == KC - 1)
                last.then_inc(fused, 1)
                pe.wait_ge(copied, 4)
                for m in range(KC):
                    for c in range(KC):
                        nc.tensor.matmul(k.ps[:, m, 0:2 * H1], fused_t[:, c, bass.ts(m, P)], att[:, c, :],
                                         start=c == 0, stop=c == KC - 1)
                for c in range(KC):
                    last = nc.tensor.matmul(k.ps[0:1, 4, 0:2 * H1], bias_col[:, c:c + 1], att[:, c, :],
                                            start=c == 0, stop=c == KC - 1)
                last.then_inc(fused, 1)
                pe.wait_ge(copied, 6)
                nc.tensor.matmul(k.ps[:, 0, :], k.ones[0:1, :], bias_row[:, 0:ED], start=True, stop=True)
                nc.tensor.matmul(k.ps[:, 1, 0:C - ED], k.ones[0:1, :], bias_row[:, ED:C], start=True,
                                 stop=True).then_inc(fused, 1)
                pe.wait_ge(w_ready, 1)
                with pe.Fori(0, GROUPS) as g:
                    for u in range(U):
                        i = g * U + u
                        pe.wait_ge(normed, i + 1)
                        if u >= 2:
                            pe.wait_ge(turned_copied, i - 1)
                        else:
                            pe.wait_ge(turned_copied, g * U)
                        for c in range(KC):
                            last = nc.tensor.transpose(k.ps[:, u % 2, bass.ts(c, P)], xn[:, u, bass.ts(c, P)],
                                                       k.ident[:])
                        last.then_inc(turned, 1)
                    for u in range(U):
                        i = g * U + u
                        bank = 2 + 2 * (u % 2)
                        pe.wait_ge(turned_copied, i + 1)
                        if u >= 2:
                            pe.wait_ge(added, i - 1)
                        else:
                            pe.wait_ge(added, g * U)
                        for c in range(KC):
                            nc.tensor.matmul(k.ps[:, bank, :], xt[:, u, bass.ts(c, P)], w_all[:, c, 0:2 * D],
                                             start=c == 0, stop=c == KC - 1)
                        for c in range(KC):
                            last = nc.tensor.matmul(k.ps[:, bank + 1, 0:2 * H1], xt[:, u, bass.ts(c, P)],
                                                    w_all[:, c, 2 * D:], start=c == 0, stop=c == KC - 1)
                        last.then_inc(product, 1)


def gat_scores(k):
    nc, t = k.nc, k.t
    ctx, sb, sem = phase(k)
    W = 14
    with ctx:
        el, er = sb("el", [P, EC * H1]), sb("er", [P, EC * H1])
        fwd, bwd = sb("fwd", [P, EC * H1]), sb("bwd", [P, EC * H1])
        rec = sb("rec", [P, EC * (2 + H1)], I32)
        cut = sb("cut", [P, EC + 1])
        index, got = sb("index", [P, 2, 2, W], I32), sb("got", [P, 2, 2, W, H1])
        ends = sb("ends", [P, 4, H1])
        turned = sb("turned", [H1, 4, P])
        line = sb("line", [H1, 6, P])
        carry = sb("carry", [P, 2, H1])
        staged, unloaded, step_sem, started = sem("staged"), sem("unloaded"), sem("step"), sem("started")
        landed = [sem("landed0"), sem("landed1")]
        ends_ready, ends_turned, line_ready, line_turned = (
            sem(s) for s in ("ends_ready", "ends_turned", "line_ready", "line_turned"))
        shifted, weighted, rec_ready, stored = sem("shifted"), sem("weighted"), sem("rec_ready"), sem("stored")

        with nc.Block() as block:
            @block.gpsimd
            def _(pool):
                with pool.Fori(0, EC // W // 2) as g:
                    for s in range(2):
                        c = 2 * g + s
                        pool.wait_ge(unloaded, c + 1)
                        nc.gpsimd.tensor_copy(index[:, s, 0, :], k.src_i[:, bass.ts(c, W)]).then_inc(staged, 1)
                        nc.gpsimd.tensor_copy(index[:, s, 1, :], k.dst_i[:, bass.ts(c, W)]).then_inc(staged, 1)
                        pool.wait_ge(staged, 2 * c + 2)
                        pool.sem_inc(started, 1)
                        for n, rows in enumerate((t["el_rows"], t["er_rows"])):
                            for j in range(W):
                                nc.gpsimd.indirect_dma_start(
                                    got[:, s, n, j, :], None, rows[:, :],
                                    bass.IndirectOffsetOnAxis(ap=index[:, s, n, j:j + 1], axis=0)
                                ).then_inc(landed[s], 16)

            @block.scalar
            def _(act):
                act.sem_inc(unloaded, 2)
                with act.Fori(0, EC // W // 2) as g:
                    for s in range(2):
                        c = 2 * g + s
                        act.wait_ge(landed[s], 16 * 2 * W * (g + 1))
                        nc.scalar.copy(el[:, bass.ts(c, W * H1)], got[:, s, 0, :, :].rearrange("p j h -> p (j h)"))
                        nc.scalar.copy(er[:, bass.ts(c, W * H1)],
                                       got[:, s, 1, :, :].rearrange("p j h -> p (j h)")).then_inc(unloaded, 1)
                act.wait_ge(shifted, 1)
                nc.scalar.activation(rec[:].rearrange("p (j c) -> p j c", c=2 + H1)[:, :, 2:].bitcast(F32),
                                     el[:].rearrange("p (j h) -> p j h", h=H1), ACT.Exp).then_inc(rec_ready, 1)

            @block.vector
            def _(dve):
                step = Steps(dve, step_sem)
                rec3 = rec[:].rearrange("p (j c) -> p j c", c=2 + H1)
                nc.vector.tensor_copy(rec3[:, :, 0], k.src_i[:]).then_inc(rec_ready, 1)
                nc.vector.tensor_copy(rec3[:, :, 1].bitcast(F32), k.dst_f[:]).then_inc(rec_ready, 1)
                step(nc.vector.memset(cut[:], 0.0))
                step(nc.vector.tensor_tensor(cut[:, 1:EC], k.dst_f[:, 1:EC], k.dst_f[:, 0:EC - 1], ALU.is_equal))
                step(nc.vector.tensor_scalar(cut[:], cut[:], -1.0, BIG, ALU.add, ALU.mult))
                for n, j in ((2, 0), (3, EC - 1)):
                    step(nc.vector.tensor_scalar(ends[:, n, :], k.ones[:, 0:H1], k.dst_f[:, j:j + 1], None, ALU.mult))
                dve.wait_ge(unloaded, 2 + EC // W)
                f3, b3, e3 = (a[:].rearrange("p (j h) -> p j h", h=H1) for a in (fwd, bwd, el))

                def scans(first, second):
                    for h in range(H1):
                        nc.vector.tensor_tensor_scan(f3[:, :, h], cut[:, 0:EC], e3[:, :, h], first(h), ALU.add, ALU.max)
                        last = nc.vector.tensor_tensor_scan(b3[:, ::-1, h], cut[:, 1:EC + 1][:, ::-1],
                                                            e3[:, ::-1, h], second(h), ALU.add, ALU.max)
                    step(last)

                scans(lambda h: -BIG, lambda h: -BIG)
                nc.vector.tensor_copy(ends[:, 0, :], f3[:, EC - 1, :])
                nc.vector.tensor_copy(ends[:, 1, :], b3[:, 0, :]).then_inc(ends_ready, 1)
                dve.wait_ge(ends_turned, 1)
                step(nc.vector.tensor_copy(turned[:], k.ps[0:H1, 0:4, 0:P]))
                tail, head, first, final = (turned[:, n, :] for n in range(4))
                linked, reach, back, run, cin, cout = (line[:, n, :] for n in range(6))
                step(nc.vector.memset(line[:], 0.0))
                step(nc.vector.tensor_tensor(linked[:, 1:P], final[:, 0:P - 1], first[:, 1:P], ALU.is_equal))
                step(nc.vector.tensor_tensor(run, first, final, ALU.is_equal))
                step(nc.vector.tensor_tensor(reach, run, linked, ALU.mult))
                step(nc.vector.tensor_tensor(back[:, 0:P - 1], run[:, 0:P - 1], linked[:, 1:P], ALU.mult))
                step(nc.vector.tensor_scalar(line[:, 0:3, :], line[:, 0:3, :], -1.0, BIG, ALU.add, ALU.mult))
                step(nc.vector.tensor_tensor_scan(run, reach, tail, -BIG, ALU.add, ALU.max))
                step(nc.vector.memset(cin, -BIG))
                step(nc.vector.tensor_tensor(cin[:, 1:P], run[:, 0:P - 1], linked[:, 1:P], ALU.add))
                step(nc.vector.tensor_tensor_scan(run[:, ::-1], back[:, ::-1], head[:, ::-1], -BIG, ALU.add, ALU.max))
                step(nc.vector.memset(cout, -BIG))
                nc.vector.tensor_tensor(cout[:, 0:P - 1], run[:, 1:P], linked[:, 1:P], ALU.add).then_inc(line_ready, 1)
                dve.wait_ge(line_turned, 1)
                step(nc.vector.tensor_copy(carry[:], k.ps[:, 4:6, 0:H1]))
                step(nc.vector.memset(cut[:, 0:1], 0.0))
                step(nc.vector.memset(cut[:, EC:EC + 1], 0.0))
                scans(lambda h: carry[:, 0, h:h + 1], lambda h: carry[:, 1, h:h + 1])
                step(nc.vector.tensor_tensor(fwd[:], fwd[:], bwd[:], ALU.max))
                step(nc.vector.tensor_tensor(el[:], el[:], er[:], ALU.add))
                step(nc.vector.tensor_tensor(fwd[:], fwd[:], er[:], ALU.add))
                step(nc.vector.scalar_tensor_tensor(out=el[:], in0=el[:], scalar=0.2, in1=el[:],
                                                    op0=ALU.mult, op1=ALU.max))
                step(nc.vector.scalar_tensor_tensor(out=fwd[:], in0=fwd[:], scalar=0.2, in1=fwd[:],
                                                    op0=ALU.mult, op1=ALU.max))
                nc.vector.tensor_tensor(el[:], el[:], fwd[:], ALU.subtract).then_inc(shifted, 1)

            @block.tensor
            def _(pe):
                pe.wait_ge(ends_ready, 1)
                for n in range(4):
                    last = nc.tensor.transpose(k.ps[0:H1, n, 0:P], ends[:, n, :], k.ident[:])
                last.then_inc(ends_turned, 1)
                pe.wait_ge(line_ready, 1)
                for n in range(2):
                    last = nc.tensor.transpose(k.ps[:, 4 + n, 0:H1], line[:, 4 + n, :], k.ident[0:H1, 0:H1])
                last.then_inc(line_turned, 1)

            @block.sync
            def _(sp):
                sp.wait_ge(rec_ready, 3)
                sp.dma_start(t["rec_gat"][0:EP, :].rearrange("(p j) c -> p (j c)", p=P), rec[:]).then_inc(stored, 16)
                sp.wait_ge(stored, 16)


def gat_edges(k):
    nc, t = k.nc, k.t
    ctx, sb, sem = phase(k)
    W = D + H1
    with ctx:
        acc = sb("acc", [P, NT * W])
        rec, rows = sb("rec", [P, RSLOTS, 2 + H1], I32), sb("rows", [P, RSLOTS, D])
        hot, msg = sb("hot", [P, VSLOTS, P]), sb("msg", [P, VSLOTS, D])
        bias, top = sb("bias", [P, D]), sb("top", [P, 2, D])
        den = sb("den", [P, NT * H1])
        rec_landed = [sem(f"rec_landed{s}") for s in range(RSLOTS)]
        row_landed = [sem(f"row_landed{s}") for s in range(RSLOTS)]
        weighted, multiplied, added, step_sem, loaded, started = (
            sem(s) for s in ("weighted", "multiplied", "added", "step", "loaded", "started"))

        with nc.Block() as block:
            @block.sync
            def _(sp):
                sp.dma_start(bias[:], across(t["gat_bias"])).then_inc(loaded, 16)
                with sp.Fori(0, ST // RSLOTS) as g:
                    _, start = nc.values_load_multi_w_load_instructions(
                        k.start_dst[0:1, bass.ts(g, RSLOTS)], engines=(SP,), min_val=0, max_val=EP)
                    for s in range(RSLOTS):
                        sp.wait_ge(multiplied, g * RSLOTS + s + 1)
                        sp.dma_start(rec[:, s, :], t["rec_gat"][bass.ds(start[s], P), :]).then_inc(rec_landed[s], 16)

            @block.gpsimd
            def _(pool):
                with pool.Fori(0, ST // RSLOTS) as g:
                    for s in range(RSLOTS):
                        pool.wait_ge(rec_landed[s], 16 * (g + 1))
                        pool.sem_inc(started, 1)
                        nc.gpsimd.indirect_dma_start(
                            rows[:, s, :], None, t["gat_rows"][:, :],
                            bass.IndirectOffsetOnAxis(ap=rec[:, s, 0:1], axis=0)).then_inc(row_landed[s], 16)

            @block.vector
            def _(dve):
                step = Steps(dve, step_sem)
                step(nc.vector.memset(acc[:], 0.0))
                with dve.Fori(0, ST // RSLOTS) as g:
                    _, tile = nc.values_load_multi_w_load_instructions(
                        k.tile_dst[0:1, bass.ts(g, RSLOTS)], engines=(DVE,), min_val=0, max_val=NT - 1)
                    for half in range(RSLOTS // VSLOTS):
                        for v in range(VSLOTS):
                            s = half * VSLOTS + v
                            q = g * RSLOTS + s
                            dve.wait_ge(multiplied, q + 1 + RSLOTS - VSLOTS)
                            dve.wait_ge(rec_landed[s], 16 * (g + 1))
                            nc.vector.tensor_scalar(hot[:, v, :], k.iota[:], k.base_dst[:, bass.ds(q, 1)],
                                                    rec[:, s, 1:2].bitcast(F32), ALU.add, ALU.is_equal)
                            dve.wait_ge(row_landed[s], 16 * (g + 1))
                            nc.vector.tensor_tensor(
                                msg[:, v, :].rearrange("p (h d) -> p h d", d=HD),
                                rows[:, s, :].rearrange("p (h d) -> p h d", d=HD),
                                rec[:, s, 2:].bitcast(F32).unsqueeze(2).to_broadcast([P, H1, HD]),
                                ALU.mult).then_inc(weighted, 1)
                        for v in range(VSLOTS):
                            s = half * VSLOTS + v
                            q = g * RSLOTS + s
                            dve.wait_ge(multiplied, q + 1 + RSLOTS)
                            dve.wait_ge(added, q)
                            sums = acc[:, bass.ds(tile[s] * W, W)]
                            nc.vector.tensor_tensor(sums, sums, k.ps[:, v, 0:W], ALU.add).then_inc(added, 1)
                dve.wait_ge(added, ST)
                dve.wait_ge(loaded, 16)
                acc3 = acc[:].rearrange("p (i c) -> p i c", c=W)
                den3 = den[:].rearrange("p (i h) -> p i h", h=H1)
                step(nc.vector.tensor_scalar(den3, acc3[:, :, D:], 1e-30, None, ALU.max))
                step(nc.vector.reciprocal(den[:], den[:]))
                base = step.n
                for i in range(NT):
                    a, xsl, y = acc3[:, i, 0:D], k.xs[:, bass.ts(i, D)], top[:, i % 2, :]
                    step(nc.vector.tensor_tensor(
                        a.rearrange("p (h d) -> p h d", d=HD), a.rearrange("p (h d) -> p h d", d=HD),
                        den3[:, i, :].unsqueeze(2).to_broadcast([P, H1, HD]), ALU.mult))
                    step(nc.vector.tensor_tensor(a, a, bias[:], ALU.add))
                    step(nc.vector.scalar_tensor_tensor(out=y, in0=a, scalar=0.01, in1=a, op0=ALU.mult, op1=ALU.max))
                    step(nc.vector.tensor_tensor(xsl, xsl, y, ALU.add))

            @block.tensor
            def _(pe):
                pe.sem_inc(multiplied, RSLOTS)
                with pe.Fori(0, ST // RSLOTS) as g:
                    for s in range(RSLOTS):
                        v = s % VSLOTS
                        q = g * RSLOTS + s
                        pe.wait_ge(weighted, q + 1)
                        if s >= VSLOTS:
                            pe.wait_ge(added, q + 1 - VSLOTS)
                        else:
                            pe.wait_ge(added, g * RSLOTS)
                        nc.tensor.matmul(k.ps[:, v, 0:D], hot[:, v, :], msg[:, v, :], start=True, stop=True)
                        nc.tensor.matmul(k.ps[:, v, D:W], hot[:, v, :], rec[:, s, 2:].bitcast(F32), start=True,
                                         stop=True).then_inc(multiplied, 1)


def slice_attention(k):
    nc, t = k.nc, k.t
    ctx, sb, sem = phase(k)
    W = 14
    PD = 2 * SD
    with ctx:
        w_fx, w_sl = sb("w_fx", [P, KC, SI]), sb("w_sl", [P, KC, SI])
        w_x_t = sb("w_x_t", [SD, SH, D])
        w_slice, b_x = sb("w_slice", [SD, SD]), sb("b_x", [SD, SH])
        w_two = [sb(f"w_{n}2", [PD, PD]) for n in ("q", "k", "v")]
        w_out, fold = sb("w_out", [PD, PAIRS, D]), sb("fold", [PD, PAIRS, D])
        b_fx, b_out, b_sl = sb("b_fx", [P, SI]), sb("b_out", [P, D]), sb("b_sl", [P, SI])
        b_slice = sb("b_slice", [SH, SD])
        sl_row = sb("sl_row", [SH, SD])
        temp = sb("temp", [P, SH])
        st, mv = sb("st", [P, NT * 6]), sb("mv", [P, 5, NT])
        xn, xt = sb("xn", [P, U, D]), sb("xt", [P, U, D])
        soft, fx = sb("soft", [P, 2, SI]), sb("fx", [P, 2, PAIRS, PD + 1])
        peak, total = sb("peak", [P, 2, SH]), sb("total", [P, 2, SH])
        soft_t = k.large[:, 0:PAIRS * NP].rearrange("p (a n) -> p a n", n=NP)
        piece = sb("piece", [P, U, SI])
        zero = sb("zero", [1, PD + 1])
        token, norm = sb("token", [PD, PAIRS, PD]), sb("norm", [PD, PAIRS])
        token_t, q_t, k_t, v = (sb(n, [PD, PAIRS, PD]) for n in ("token_t", "q_t", "k_t", "v"))
        att, att_t, mix_t = (sb(n, [PD, PAIRS, PD]) for n in ("att", "att_t", "mix_t"))
        high, mass = sb("high", [PD, PAIRS]), sb("mass", [PD, PAIRS])
        place, pair = sb("place", [P, 2, W], I32), sb("pair", [P, 2, W, 2], I32)
        S = {n: sem(n) for n in (
            "loaded", "zeroed", "dve_step", "act_step", "stats_ready", "sqrt_ready", "fused", "copied", "bias_out",
            "bias_in", "w_ready", "normed", "turned", "turned_copied", "product", "scored", "raised", "weighed",
            "tokens", "soft_turned", "soft_kept", "fixed", "mid_pe", "mid_dve", "mid_act", "cut", "result",
            "added", "placed", "started")}
        sent = [sem("sent0"), sem("sent1")]
        HALVES = ((0, SD), (SD, PD))

        with nc.Block() as block:
            @block.sync
            def _(sp):
                n = load_weights(k, sp, S["loaded"], [
                    (w_fx[:], chunks(t["w_fx"])), (w_x_t[:], t["w_x_t"].rearrange("(h c) n -> c h n", c=SD)),
                    (w_slice[:], t["w_slice"]), (b_x[:], t["b_x_cols"]), (w_out[:], chunks(t["w_out"])),
                    (b_fx[:], across(t["b_fx"])), (b_out[:], across(t["b_out"])),
                    (b_slice[:], row(t["b_slice"]).to_broadcast([SH, SD])), (temp[:], across(t["temp"]))])
                sp.wait_ge(S["zeroed"], 4)
                for w2, w in zip(w_two, (t["w_q"], t["w_k"], t["w_v"])):
                    for a, b in HALVES:
                        sp.dma_start(w2[a:b, a:b], w).then_inc(S["loaded"], 16)
                sp.wait_ge(S["copied"], 1)
                sp.dma_start(t["slice_bias"], sl_row[:]).then_inc(S["bias_out"], 16)
                sp.wait_ge(S["bias_out"], 16)
                sp.dma_start(b_sl[:], row(t["slice_bias"].rearrange("h g -> (h g)")).to_broadcast(
                    [P, SI])).then_inc(S["bias_in"], 16)

            @block.gpsimd
            def _(pool):
                for w2 in w_two:
                    nc.gpsimd.memset(w2[:], 0.0).then_inc(S["zeroed"], 1)
                nc.gpsimd.memset(zero[:], 0.0).then_inc(S["zeroed"], 1)
                rec3 = k.edge_rec[:].rearrange("p (j c) -> p j c", c=2)
                with pool.Fori(0, EC // W // 2) as g:
                    for s in range(2):
                        c = 2 * g + s
                        pool.wait_ge(sent[s], 16 * W * g)
                        nc.gpsimd.tensor_copy(place[:, s, :], k.pos_i[:, bass.ts(c, W)]).then_inc(S["placed"], 1)
                        nc.gpsimd.tensor_copy(pair[:, s, :, :].rearrange("p j c -> p (j c)"),
                                              k.edge_rec[:, bass.ts(c, 2 * W)]).then_inc(S["placed"], 1)
                        pool.wait_ge(S["placed"], 2 * c + 2)
                        pool.sem_inc(S["started"], 1)
                        for j in range(W):
                            nc.gpsimd.indirect_dma_start(
                                t["rec_src"][0:EP, :], bass.IndirectOffsetOnAxis(ap=place[:, s, j:j + 1], axis=0),
                                pair[:, s, j, :], None).then_inc(sent[s], 16)
                for s in range(2):
                    pool.wait_ge(sent[s], 16 * EC // 2)

            @block.vector
            def _(dve):
                step = Steps(dve, S["dve_step"])
                emit_norm(k, dve, st, mv, S["stats_ready"], S["sqrt_ready"], step)
                dve.wait_ge(S["loaded"], 16 * 15)
                step(nc.vector.tensor_scalar(temp[:], temp[:], 0.1, 5.0, ALU.max, ALU.min))
                step(nc.vector.reciprocal(temp[:], temp[:]))
                dve.wait_ge(S["fused"], 1)
                nc.vector.tensor_tensor(sl_row[:], k.ps[0:SH, 2, 0:SD], b_slice[:], ALU.add).then_inc(S["copied"], 1)
                for c in range(KC):
                    last = nc.vector.tensor_tensor(
                        w_sl[:, c, :].rearrange("p (h g) -> p h g", g=SD),
                        k.ps[:, c, :].rearrange("p (h g) -> p h g", g=SD),
                        temp[:].unsqueeze(2).to_broadcast([P, SH, SD]), ALU.mult)
                last.then_inc(S["w_ready"], 1)
                nc.vector.memset(fx[:, :, :, PD:], 1.0).then_inc(S["fixed"], 1)
                nc.vector.memset(token[:], 0.0).then_inc(S["fixed"], 1)
                nc.vector.memset(att[:], 0.0).then_inc(S["fixed"], 1)
                dve.wait_ge(S["fixed"], 3)
                dve.wait_ge(S["bias_in"], 16)
                step(nc.vector.tensor_tensor(
                    b_sl[:].rearrange("p (h g) -> p h g", g=SD), b_sl[:].rearrange("p (h g) -> p h g", g=SD),
                    temp[:].unsqueeze(2).to_broadcast([P, SH, SD]), ALU.mult))
                before = step.n
                with dve.Fori(0, GROUPS) as g:
                    for u in range(U):
                        i = g * U + u
                        dve.wait_ge(S["turned"], i + 1)
                        nc.vector.tensor_scalar(xn[:, u, :], k.xs[:, bass.ts(i, D)], mv[:, 0, bass.ds(i, 1)],
                                                mv[:, 4, bass.ds(i, 1)], ALU.subtract, ALU.mult).then_inc(S["normed"], 1)
                    for u in range(U):
                        i = g * U + u
                        o = u % 2
                        s3 = soft[:, o, :].rearrange("p (h g) -> p h g", g=SD)

                        dve.wait_ge(S["product"], i + 1)
                        dve.wait_ge(S["tokens"], i)
                        nc.vector.tensor_tensor(fx[:, o, :, 0:PD],
                                                k.ps[:, 2, :].rearrange("p (a b) -> p a b", b=PD),
                                                b_fx[:].rearrange("p (a b) -> p a b", b=PD), ALU.add)
                        nc.vector.tensor_tensor(soft[:, o, :], k.ps[:, 3, :], b_sl[:], ALU.add).then_inc(S["scored"], 1)
                        dve.wait_ge(S["scored"], i + 1)
                        nc.vector.tensor_reduce(peak[:, o, :], s3, AX, ALU.max).then_inc(S["dve_step"], 1)
                        dve.wait_ge(S["dve_step"], before + 3 * i + 1)
                        nc.vector.tensor_tensor(s3, s3, peak[:, o, :].unsqueeze(2).to_broadcast([P, SH, SD]),
                                                ALU.subtract).then_inc(S["raised"], 1)
                        dve.wait_ge(S["weighed"], i + 1)
                        nc.vector.tensor_reduce(total[:, o, :], s3, AX, ALU.add).then_inc(S["dve_step"], 1)
                        dve.wait_ge(S["dve_step"], before + 3 * i + 2)
                        nc.vector.reciprocal(total[:, o, :], total[:, o, :]).then_inc(S["dve_step"], 1)
                        dve.wait_ge(S["dve_step"], before + 3 * i + 3)
                        nc.vector.scalar_tensor_tensor(
                            out=s3, in0=s3, scalar=k.mask[:, bass.ds(i, 1)],
                            in1=total[:, o, :].unsqueeze(2).to_broadcast([P, SH, SD]),
                            op0=ALU.mult, op1=ALU.mult).then_inc(S["cut"], 1)
                step = Steps(dve, S["mid_dve"])
                dve.wait_ge(S["tokens"], NT)
                step(nc.vector.tensor_scalar(norm[:], k.ps[:, 4:8, PD], 1e-5, None, ALU.add))
                step(nc.vector.reciprocal(norm[:], norm[:]))
                for r in range(PAIRS):
                    for a, b in HALVES:
                        last = nc.vector.tensor_scalar(token[a:b, r, a:b], k.ps[a:b, 4 + r, a:b],
                                                       norm[a:b, r:r + 1], None, ALU.mult)
                step(last)

                def leave(n, out, bank):
                    dve.wait_ge(S["mid_pe"], n)
                    step(nc.vector.tensor_copy(out[:].rearrange("p a b -> p (a b)"), k.ps[:, bank, :]))

                leave(1, token_t, 0)
                dve.wait_ge(S["mid_pe"], 2)
                for out, bank in ((q_t, 1), (k_t, 2), (v, 3)):
                    step(nc.vector.tensor_copy(out[:].rearrange("p a b -> p (a b)"), k.ps[:, bank, :]))
                dve.wait_ge(S["mid_pe"], 3)
                scale = float(SD) ** -0.5
                for a, b in HALVES:
                    last = nc.vector.tensor_reduce(high[a:b, :], k.ps[a:b, 0, :].rearrange(
                        "p (r c) -> p r c", c=PD)[:, :, a:b], AX, ALU.max)
                step(last)
                for a, b in HALVES:
                    last = nc.vector.tensor_tensor(
                        att[a:b, :, a:b], k.ps[a:b, 0, :].rearrange("p (r c) -> p r c", c=PD)[:, :, a:b],
                        high[a:b, :].unsqueeze(2).to_broadcast([SD, PAIRS, SD]), ALU.subtract)
                step(last)
                dve.wait_ge(S["mid_act"], 1)
                for a, b in HALVES:
                    last = nc.vector.tensor_reduce(mass[a:b, :], att[a:b, :, a:b], AX, ALU.add)
                step(last)
                step(nc.vector.reciprocal(mass[:], mass[:]))
                step(nc.vector.tensor_tensor(att[:], att[:], mass[:].unsqueeze(2).to_broadcast([PD, PAIRS, PD]),
                                             ALU.mult))
                leave(4, att_t, 1)
                leave(5, mix_t, 2)
                dve.wait_ge(S["mid_pe"], 6)
                step(nc.vector.tensor_copy(fold[:, 0:2, :].rearrange("p a b -> p (a b)"), k.ps[:, 4, :]))
                step(nc.vector.tensor_copy(fold[:, 2:4, :].rearrange("p a b -> p (a b)"), k.ps[:, 5, :]))
                with dve.Fori(0, GROUPS) as g:
                    for u in range(U):
                        i = g * U + u
                        dve.wait_ge(S["result"], i + 1)
                        xsl = k.xs[:, bass.ts(i, D)]
                        nc.vector.tensor_tensor(xsl, xsl, k.ps[:, u % 2, 0:D], ALU.add).then_inc(S["cut"], 1)
                        dve.wait_ge(S["cut"], NT + i + 1)
                        nc.vector.tensor_tensor(xsl, xsl, b_out[:], ALU.add).then_inc(S["added"], 1)

            @block.scalar
            def _(act):
                emit_sqrt(k, act, mv, S["stats_ready"], S["sqrt_ready"])
                with act.Fori(0, GROUPS) as g:
                    for u in range(U):
                        i = g * U + u
                        act.wait_ge(S["turned"], i + U + 1)
                        nc.scalar.copy(xt[:, u, :], k.ps[:, 0, 0:D]).then_inc(S["turned_copied"], 1)
                    for u in range(U):
                        i = g * U + u
                        act.wait_ge(S["raised"], i + 1)
                        nc.scalar.activation(soft[:, u % 2, :], soft[:, u % 2, :], ACT.Exp).then_inc(S["weighed"], 1)
                        act.wait_ge(S["soft_turned"], i + 1)
                        nc.scalar.copy(soft_t[:, :, bass.ts(i, P)],
                                       k.ps[:, 1, :].rearrange("p (a b) -> p a b", b=P)).then_inc(S["soft_kept"], 1)
                act.wait_ge(S["mid_dve"], 9)
                for a, b in HALVES:
                    last = nc.scalar.activation(att[a:b, :, a:b], att[a:b, :, a:b], ACT.Exp, scale=float(SD) ** -0.5)
                last.then_inc(S["mid_act"], 1)
                act.wait_ge(S["soft_kept"], NT)
                with act.Fori(0, GROUPS) as g:
                    for u in range(U):
                        i = g * U + u
                        act.wait_ge(S["result"], g * U)
                        nc.scalar.copy(piece[:, u, :].rearrange("p (a b) -> p a b", b=P),
                                       soft_t[:, :, bass.ts(i, P)]).then_inc(S["act_step"], 1)

            @block.tensor
            def _(pe):
                pe.sem_inc(S["turned"], U)
                pe.wait_ge(S["loaded"], 16 * 15)
                pe.wait_ge(S["zeroed"], 4)
                for c in range(KC):
                    for h in range(SH):
                        nc.tensor.matmul(k.ps[:, c, bass.ts(h, SD)], w_x_t[:, h, bass.ts(c, P)], w_slice[:],
                                         start=True, stop=True)
                nc.tensor.matmul(k.ps[0:SH, 2, 0:SD], b_x[:], w_slice[:], start=True, stop=True).then_inc(S["fused"], 1)
                pe.wait_ge(S["w_ready"], 1)
                for r in range(PAIRS):
                    nc.tensor.matmul(k.ps[:, 4 + r, 0:PD + 1], k.ones[0:1, :], zero[:], start=True, stop=False,
                                     skip_group_check=True)
                with pe.Fori(0, GROUPS) as g:
                    for u in range(U):
                        i = g * U + u
                        pe.wait_ge(S["normed"], i + 1)
                        pe.wait_ge(S["turned_copied"], i)
                        for c in range(KC):
                            last = nc.tensor.transpose(k.ps[:, 0, bass.ts(c, P)],
                                                       xn[:, u, bass.ts(c, P)], k.ident[:])
                        last.then_inc(S["turned"], 1)
                    for u in range(U):
                        i = g * U + u
                        pe.wait_ge(S["turned_copied"], i + 1)
                        pe.wait_ge(S["scored"], i)
                        for bank, w in ((2, w_fx), (3, w_sl)):
                            for c in range(KC):
                                last = nc.tensor.matmul(k.ps[:, bank, :], xt[:, u, bass.ts(c, P)], w[:, c, :],
                                                        start=c == 0, stop=c == KC - 1)
                        last.then_inc(S["product"], 1)
                        pe.wait_ge(S["cut"], i + 1)
                        pe.wait_ge(S["soft_kept"], i)
                        for r in range(PAIRS):
                            last = nc.tensor.transpose(k.ps[:, 1, bass.ts(r, P)], soft[:, u % 2, bass.ts(r, P)],
                                                       k.ident[:])
                        last.then_inc(S["soft_turned"], 1)
                        for r in range(PAIRS):
                            last = nc.tensor.matmul(k.ps[:, 4 + r, 0:PD + 1], soft[:, u % 2, bass.ts(r, PD)],
                                                    fx[:, u % 2, r, :], start=False, stop=False,
                                                    skip_group_check=True)
                        last.then_inc(S["tokens"], 1)
                pe.wait_ge(S["soft_kept"], NT)
                pe.wait_ge(S["mid_dve"], 3)
                for r in range(PAIRS):
                    last = nc.tensor.transpose(k.ps[:, 0, bass.ts(r, PD)], token[:, r, :], k.ident[:])
                last.then_inc(S["mid_pe"], 1)
                pe.wait_ge(S["mid_dve"], 4)
                for r in range(PAIRS):
                    nc.tensor.matmul(k.ps[:, 1, bass.ts(r, PD)], w_two[0][:], token_t[:, r, :], start=True, stop=True)
                    nc.tensor.matmul(k.ps[:, 2, bass.ts(r, PD)], w_two[1][:], token_t[:, r, :], start=True, stop=True)
                    last = nc.tensor.matmul(k.ps[:, 3, bass.ts(r, PD)], token_t[:, r, :], w_two[2][:], start=True,
                                            stop=True)
                last.then_inc(S["mid_pe"], 1)
                pe.wait_ge(S["mid_dve"], 7)
                for r in range(PAIRS):
                    last = nc.tensor.matmul(k.ps[:, 0, bass.ts(r, PD)], q_t[:, r, :], k_t[:, r, :], start=True,
                                            stop=True)
                last.then_inc(S["mid_pe"], 1)
                pe.wait_ge(S["mid_dve"], 12)
                for r in range(PAIRS):
                    last = nc.tensor.transpose(k.ps[:, 1, bass.ts(r, PD)], att[:, r, :], k.ident[:])
                last.then_inc(S["mid_pe"], 1)
                pe.wait_ge(S["mid_dve"], 13)
                for r in range(PAIRS):
                    last = nc.tensor.matmul(k.ps[:, 2, bass.ts(r, PD)], v[:, r, :], att_t[:, r, :], start=True,
                                            stop=True)
                last.then_inc(S["mid_pe"], 1)
                pe.wait_ge(S["mid_dve"], 14)
                for r in range(PAIRS):
                    last = nc.tensor.matmul(k.ps[:, 4 + r // 2, bass.ts(r % 2, D)], mix_t[:, r, :], w_out[:, r, :],
                                            start=True, stop=True)
                last.then_inc(S["mid_pe"], 1)
                pe.wait_ge(S["mid_dve"], 16)
                with pe.Fori(0, GROUPS) as g:
                    for u in range(U):
                        i = g * U + u
                        pe.wait_ge(S["act_step"], i + 1)
                        pe.wait_ge(S["added"], i - 1 if u >= 2 else g * U)
                        for r in range(PAIRS):
                            last = nc.tensor.matmul(k.ps[:, u % 2, 0:D], piece[:, u, bass.ts(r, P)], fold[:, r, :],
                                                    start=r == 0, stop=r == PAIRS - 1)
                        last.then_inc(S["result"], 1)


def message_tables(k):
    nc, t = k.nc, k.t
    ctx, sb, sem = phase(k)
    with ctx:
        w, b1 = sb("w", [P, KC, 2 * D]), sb("b1", [P, D])
        st, mv = sb("st", [P, NT * 6]), sb("mv", [P, 5, NT])
        xn, xt, out = sb("xn", [P, U, D]), sb("xt", [P, U, D]), sb("out", [P, U, D])
        loaded, dve_step, stats_ready, sqrt_ready = (sem(s) for s in ("loaded", "dve_step", "stats_ready", "sqrt_ready"))
        normed, turned, turned_copied, product, left = (
            sem(s) for s in ("normed", "turned", "turned_copied", "product", "left"))
        stored = [sem(f"stored{u}") for u in range(U)]

        with nc.Block() as block:
            @block.sync
            def _(sp):
                load_weights(k, sp, loaded, [(w[:, :, 0:D], chunks(t["w1_t"][0:D, :])),
                                             (w[:, :, D:], chunks(t["w1_t"][D:, :])), (b1[:], across(t["b1"]))])
                with sp.Fori(0, GROUPS) as g:
                    for u in range(U):
                        i = g * U + u
                        sp.wait_ge(left, i + 1)
                        sp.dma_start(t["msg_rows"][bass.ts(i, P), :], out[:, u, :]).then_inc(stored[u], 16)
                for u in range(U):
                    sp.wait_ge(stored[u], 16 * GROUPS)

            @block.vector
            def _(dve):
                step = Steps(dve, dve_step)
                emit_norm(k, dve, st, mv, stats_ready, sqrt_ready, step)
                dve.wait_ge(loaded, 48)
                with dve.Fori(0, GROUPS) as g:
                    for u in range(U):
                        i = g * U + u
                        dve.wait_ge(turned, i + 1)
                        nc.vector.tensor_scalar(xn[:, u, :], k.xs[:, bass.ts(i, D)], mv[:, 0, bass.ds(i, 1)],
                                                mv[:, 4, bass.ds(i, 1)], ALU.subtract, ALU.mult).then_inc(normed, 1)
                    for u in range(U):
                        i = g * U + u
                        dve.wait_ge(product, i + 1)
                        dve.wait_ge(stored[u], 16 * g)
                        nc.vector.tensor_tensor(k.source_part[:, bass.ts(i, D)], k.ps[:, 2 + u % 2, 0:D], b1[:], ALU.add)
                        nc.vector.tensor_copy(out[:, u, :], k.ps[:, 2 + u % 2, D:]).then_inc(left, 1)

            @block.scalar
            def _(act):
                emit_sqrt(k, act, mv, stats_ready, sqrt_ready)
                with act.Fori(0, GROUPS) as g:
                    for u in range(U):
                        i = g * U + u
                        act.wait_ge(turned, i + U + 1)
                        nc.scalar.copy(xt[:, u, :], k.ps[:, u % 2, 0:D]).then_inc(turned_copied, 1)

            @block.tensor
            def _(pe):
                pe.sem_inc(turned, U)
                pe.wait_ge(loaded, 48)
                with pe.Fori(0, GROUPS) as g:
                    for u in range(U):
                        i = g * U + u
                        pe.wait_ge(normed, i + 1)
                        pe.wait_ge(turned_copied, i - 1 if u >= 2 else g * U)
                        for c in range(KC):
                            last = nc.tensor.transpose(k.ps[:, u % 2, bass.ts(c, P)], xn[:, u, bass.ts(c, P)],
                                                       k.ident[:])
                        last.then_inc(turned, 1)
                    for u in range(U):
                        i = g * U + u
                        pe.wait_ge(turned_copied, i + 1)
                        pe.wait_ge(left, i - 1 if u >= 2 else g * U)
                        for c in range(KC):
                            last = nc.tensor.matmul(k.ps[:, 2 + u % 2, :], xt[:, u, bass.ts(c, P)], w[:, c, :],
                                                    start=c == 0, stop=c == KC - 1)
                        last.then_inc(product, 1)


BATCH = 4
BSETS = 4
BODIES = ST // (BATCH * BSETS)
assert BODIES * BATCH * BSETS == ST and BODIES > 2


def message_edges(k):
    nc, t = k.nc, k.t
    ctx, sb, sem = phase(k)
    W = D + 1
    SLOTS = BATCH * BSETS
    with ctx:
        acc = k.sums
        rec, rows = sb("rec", [P, SLOTS, 2], I32), sb("rows", [P, SLOTS, D])
        hot, hot_t = sb("hot", [P, SLOTS, P]), sb("hot_t", [P, 2, BATCH, P])
        msg = sb("msg", [P, 2, BATCH, W])
        started = sem("started")
        rec_landed = [sem(f"rec_landed{s}") for s in range(SLOTS)]
        row_landed = [sem(f"row_landed{s}") for s in range(SLOTS)]
        hot_made, hot_turned, hot_copied, expanded, raised, silu_done, multiplied, added, prepared = (
            sem(s) for s in ("hot_made", "hot_turned", "hot_copied", "expanded", "raised", "silu_done", "multiplied",
                             "added", "prepared"))

        def bodies(engine, body):
            body(0, True, False)
            with engine.Fori(1, BODIES - 1) as g:
                body(g, False, False)
            body(BODIES - 1, False, True)

        with nc.Block() as block:
            @block.sync
            def _(sp):
                with sp.Fori(0, BODIES) as g:
                    for half in range(2):
                        _, start = nc.values_load_multi_w_load_instructions(
                            k.start_src[0:1, bass.ds(g * SLOTS + half * 8, 8)], engines=(SP,), min_val=0, max_val=EP)
                        for n in range(8):
                            s = half * 8 + n
                            sp.wait_ge(raised, g * BSETS + s // BATCH + 1)
                            sp.dma_start(rec[:, s, :], t["rec_src"][bass.ds(start[n], P), :]).then_inc(rec_landed[s], 16)

            @block.gpsimd
            def _(pool):
                with pool.Fori(0, BODIES) as g:
                    for s in range(SLOTS):
                        pool.wait_ge(rec_landed[s], 16 * (g + 1))
                        pool.sem_inc(started, 1)
                        nc.gpsimd.indirect_dma_start(
                            rows[:, s, :], None, t["msg_rows"][:, :],
                            bass.IndirectOffsetOnAxis(ap=rec[:, s, 0:1], axis=0)).then_inc(row_landed[s], 16)

            @block.vector
            def _(dve):
                dve.sem_inc(raised, BSETS)
                nc.vector.memset(msg[:, :, :, D:], 1.0).then_inc(prepared, 1)
                nc.vector.memset(acc[:], 0.0).then_inc(prepared, 1)
                dve.wait_ge(prepared, 2)

                def one_hots(g, c):
                    for n in range(BATCH):
                        s = c * BATCH + n
                        q = g * SLOTS + s
                        if not (isinstance(g, int) and g == 0):
                            dve.wait_ge(multiplied, q - SLOTS + 1)
                        dve.wait_ge(rec_landed[s], 16 * (g + 1))
                        last = nc.vector.tensor_scalar(hot[:, s, :], k.iota[:], k.base_src[:, bass.ds(q, 1)],
                                                       rec[:, s, 1:2].bitcast(F32), ALU.add, ALU.is_equal)
                    last.then_inc(hot_made, 1)

                def add_rows(g, c):
                    B = g * BSETS + c
                    dve.wait_ge(expanded, B + 1)
                    if not (isinstance(g, int) and g == 0 and c < 2):
                        dve.wait_ge(multiplied, (B - 1) * BATCH)
                    for h in range(2):
                        s0 = c * BATCH + 2 * h
                        for s in (s0, s0 + 1):
                            dve.wait_ge(row_landed[s], 16 * (g + 1))
                        last = nc.vector.tensor_tensor(
                            msg[:, c % 2, 2 * h:2 * h + 2, 0:D], k.ps[:, 2 + h, :].rearrange("p (a b) -> p a b", b=D),
                            rows[:, s0:s0 + 2, :], ALU.add)
                    last.then_inc(raised, 1)

                def add_sums(g, c, tile):
                    for n in range(BATCH):
                        q = g * SLOTS + c * BATCH + n
                        dve.wait_ge(multiplied, q + 1)
                        dve.wait_ge(added, q)
                        sums = acc[:, bass.ds(tile[n] * W, W)]
                        nc.vector.tensor_tensor(sums, sums, k.ps[:, 4 + n, 0:W], ALU.add).then_inc(added, 1)

                def tiles(q):
                    return nc.values_load_multi_w_load_instructions(
                        k.tile_src[0:1, bass.ds(q, BATCH)], engines=(DVE,), min_val=0, max_val=NT - 1)[1]

                def body(g, first, last):
                    if first:
                        one_hots(0, 0)
                        one_hots(0, 1)
                    for c in range(BSETS):
                        if c < BSETS - 2:
                            one_hots(g, c + 2)
                        elif not last:
                            one_hots(g + 1, c + 2 - BSETS)
                        add_rows(g, c)
                        if c:
                            add_sums(g, c - 1, tiles(g * SLOTS + (c - 1) * BATCH))
                        elif not first:
                            add_sums(g - 1, BSETS - 1, tiles(g * SLOTS - BATCH))
                    if last:
                        add_sums(g, BSETS - 1, tiles(g * SLOTS + (BSETS - 1) * BATCH))

                bodies(dve, body)

            @block.scalar
            def _(act):
                def copy_turned(g, c):
                    B = g * BSETS + c
                    act.wait_ge(hot_turned, B + 1)
                    if not (isinstance(g, int) and g == 0 and c < 2):
                        act.wait_ge(expanded, B - 1)
                    nc.scalar.copy(hot_t[:, c % 2, :, :], k.ps[:, c % 2, :].rearrange(
                        "p (a b) -> p a b", b=P)).then_inc(hot_copied, 1)

                def body(g, first, last):
                    if first:
                        copy_turned(0, 0)
                    for c in range(BSETS):
                        if c < BSETS - 1:
                            copy_turned(g, c + 1)
                        elif not last:
                            copy_turned(g + 1, 0)
                        act.wait_ge(raised, g * BSETS + c + 1 + BSETS)
                        nc.scalar.activation(msg[:, c % 2, :, 0:D], msg[:, c % 2, :, 0:D],
                                             ACT.Silu).then_inc(silu_done, 1)

                bodies(act, body)

            @block.tensor
            def _(pe):
                pe.wait_ge(prepared, 1)

                def turn(g, c):
                    B = g * BSETS + c
                    pe.wait_ge(hot_made, B + 1)
                    if not (isinstance(g, int) and g == 0 and c < 2):
                        pe.wait_ge(hot_copied, B - 1)
                    for n in range(BATCH):
                        last = nc.tensor.transpose(k.ps[:, c % 2, bass.ts(n, P)], hot[:, c * BATCH + n, :], k.ident[:])
                    last.then_inc(hot_turned, 1)

                def expand(g, c, tile):
                    B = g * BSETS + c
                    pe.wait_ge(hot_copied, B + 1)
                    pe.wait_ge(raised, B + BSETS)
                    for n in range(BATCH):
                        last = nc.tensor.matmul(k.ps[:, 2 + n // 2, bass.ts(n % 2, D)], hot_t[:, c % 2, n, :],
                                                k.source_part[:, bass.ds(tile[n] * D, D)], start=True, stop=True)
                    last.then_inc(expanded, 1)

                def multiply(g, c):
                    B = g * BSETS + c
                    pe.wait_ge(silu_done, B + 1)
                    for n in range(BATCH):
                        if not (isinstance(g, int) and g == 0 and c == 0):
                            pe.wait_ge(added, (B - 1) * BATCH + n + 1)
                        nc.tensor.matmul(k.ps[:, 4 + n, 0:W], hot[:, c * BATCH + n, :], msg[:, c % 2, n, :],
                                         start=True, stop=True).then_inc(multiplied, 1)

                def tiles(q):
                    return nc.values_load_multi_w_load_instructions(
                        k.tile_src[0:1, bass.ds(q, BATCH)], engines=(PE,), min_val=0, max_val=NT - 1)[1]

                def body(g, first, last):
                    if first:
                        turn(0, 0)
                    for c in range(BSETS):
                        if c < BSETS - 1:
                            turn(g, c + 1)
                        elif not last:
                            turn(g + 1, 0)
                        expand(g, c, tiles(g * SLOTS + c * BATCH))
                        if c:
                            multiply(g, c - 1)
                        elif not first:
                            multiply(g - 1, BSETS - 1)
                    if last:
                        multiply(g, BSETS - 1)

                bodies(pe, body)


def gated_update(k):
    nc, t = k.nc, k.t
    ctx, sb, sem = phase(k)
    W, G = D + 1, 3 * D
    with ctx:
        w_hh, w_ih = sb("w_hh", [P, KC, G]), sb("w_ih", [P, KC, G])
        w2, b2 = sb("w2", [P, KC, D]), sb("b2", [P, KC])
        w_in = sb("w_in", [P, KC, G])
        bias = sb("bias", [3, 4 * D])
        gamma, beta = sb("gamma", [P, D]), sb("beta", [P, D])
        inv, full = sb("inv", [P, NT]), sb("full", [P, NT])
        st, mv = sb("st", [P, NT * 6]), sb("mv", [P, 5, NT])
        both = sb("both", [P, 2, 2 * D + 3])
        both_t = sb("both_t", [P, 2, 4, P])
        ones_t = sb("ones_t", [3, 2, P])
        rz, new = sb("rz", [P, 2, 2 * D]), sb("new", [P, 2, D])
        nst = sb("nst", [P, 2, 6])
        names = ("loaded", "zeroed", "dve_step", "stats_ready", "sqrt_ready", "fused", "w_ready", "normed", "turned",
                 "turned_copied", "product", "gates", "candidate", "tanh_done", "chain", "tile_var", "tile_sqrt",
                 "finished")
        S = {n: sem(n) for n in names}
        sums3 = k.sums[:].rearrange("p (i c) -> p i c", c=W)
        outv = k.new_rows

        with nc.Block() as block:
            @block.sync
            def _(sp):
                sp.wait_ge(S["zeroed"], 1)
                load_weights(k, sp, S["loaded"], [
                    (w_hh[:], chunks(t["w_hh_t"])), (w_ih[:], chunks(t["w_ih_t"])), (w2[:], chunks(t["w2"])),
                    (b2[:], t["b2_cols"]), (gamma[:], across(t["gamma"])), (beta[:], across(t["beta"])),
                    (bias[1:2, 0:3 * D], row(t["b_ih"])), (bias[2:3, 0:2 * D], row(t["b_hh"][0:2 * D])),
                    (bias[2:3, 3 * D:], row(t["b_hh"][2 * D:]))])

            @block.gpsimd
            def _(pool):
                nc.gpsimd.memset(bias[:], 0.0).then_inc(S["zeroed"], 1)
                nc.gpsimd.memset(both[:, :, 2 * D + 1:], 1.0).then_inc(S["zeroed"], 1)

            @block.vector
            def _(dve):
                step = Steps(dve, S["dve_step"])
                emit_norm(k, dve, st, mv, S["stats_ready"], S["sqrt_ready"], step)
                step(nc.vector.tensor_scalar(inv[:], sums3[:, :, D], 1e-8, None, ALU.add))
                step(nc.vector.reciprocal(inv[:], inv[:]))
                step(nc.vector.tensor_tensor(full[:], sums3[:, :, D], inv[:], ALU.mult))
                dve.wait_ge(S["fused"], 1)
                for m in range(KC):
                    step(nc.vector.tensor_copy(w_in[:, m, 0:2 * D], k.ps[:, 2 * m, :]))
                    step(nc.vector.tensor_copy(w_in[:, m, 2 * D:], k.ps[:, 2 * m + 1, 0:D]))
                dve.wait_ge(S["loaded"], 16 * 9)
                step(nc.vector.tensor_copy(bias[0:1, 0:2 * D], k.ps[0:1, 4, :]))
                nc.vector.tensor_copy(bias[0:1, 2 * D:3 * D], k.ps[0:1, 5, 0:D]).then_inc(S["w_ready"], 1)
                dve.wait_ge(S["zeroed"], 2)
                dve.wait_ge(S["w_ready"], 1)
                CH = 5

                def tile(i, o, first):
                    def link(n, ins):
                        ins.then_inc(S["chain"], 1)
                        dve.wait_ge(S["chain"], i * CH + n)

                    if not first:
                        dve.wait_ge(S["turned"], i - 1)
                    nc.vector.tensor_scalar(both[:, o, 0:D], k.xs[:, bass.ts(i, D)], mv[:, 0, bass.ds(i, 1)],
                                            mv[:, 4, bass.ds(i, 1)], ALU.subtract, ALU.mult)
                    nc.vector.tensor_copy(both[:, o, 2 * D:2 * D + 1], full[:, bass.ds(i, 1)])
                    nc.vector.tensor_scalar(both[:, o, D:2 * D], k.sums[:, bass.ds(i * W, D)], inv[:, bass.ds(i, 1)],
                                            None, ALU.mult).then_inc(S["normed"], 1)
                    dve.wait_ge(S["normed"], i + 1)
                    dve.wait_ge(S["gates"], i + 1)
                    link(1, nc.vector.tensor_tensor(new[:, o, :], rz[:, o, 0:D], k.ps[:, 4 + o, D:], ALU.mult))
                    nc.vector.tensor_tensor(new[:, o, :], new[:, o, :], k.ps[:, 4 + o, 0:D],
                                            ALU.add).then_inc(S["candidate"], 1)
                    dve.wait_ge(S["tanh_done"], i + 1)
                    link(2, nc.vector.tensor_tensor(both[:, o, 0:D], both[:, o, 0:D], new[:, o, :], ALU.subtract))
                    link(3, nc.vector.tensor_tensor(both[:, o, 0:D], both[:, o, 0:D], rz[:, o, D:], ALU.mult))
                    link(4, nc.vector.tensor_tensor(new[:, o, :], new[:, o, :], both[:, o, 0:D], ALU.add))
                    link(5, nc.vector.bn_stats(nst[:, o, :], new[:, o, :]))
                    nc.vector.tensor_scalar(st[:, bass.ts(i, 6)], nst[:, o, :], 1.0, None, ALU.mult)
                    nc.vector.tensor_scalar(outv[:, bass.ts(i, D)], new[:, o, :], 1.0, None,
                                            ALU.mult).then_inc(S["finished"], 1)

                tile(0, 0, True)
                tile(1, 1, True)
                with dve.Fori(0, (NT - 3) // 2) as g:
                    tile(g * 2 + 2, 0, False)
                    tile(g * 2 + 3, 1, False)
                tile(NT - 1, 0, False)
                dve.wait_ge(S["finished"], NT)
                emit_moments(k, dve, st, mv, S["tile_var"], S["tile_sqrt"], step)
                start = step.n
                with dve.Fori(0, GROUPS) as g:
                    for n in range(4):
                        for u in range(U):
                            i = g * U + u
                            y, xsl = outv[:, bass.ts(i, D)], k.xs[:, bass.ts(i, D)]
                            if n == 0:
                                last = nc.vector.tensor_scalar(y, y, mv[:, 0, bass.ds(i, 1)],
                                                               mv[:, 4, bass.ds(i, 1)], ALU.subtract, ALU.mult)
                            elif n == 1:
                                last = nc.vector.tensor_tensor(y, y, gamma[:], ALU.mult)
                            elif n == 2:
                                last = nc.vector.tensor_tensor(xsl, xsl, beta[:], ALU.add)
                            else:
                                last = nc.vector.tensor_tensor(xsl, xsl, y, ALU.add)
                        last.then_inc(S["dve_step"], 1)
                        dve.wait_ge(S["dve_step"], start + 4 * g + n + 1)

            @block.scalar
            def _(act):
                emit_sqrt(k, act, mv, S["stats_ready"], S["sqrt_ready"])

                def tile(i, o, first):
                    act.wait_ge(S["turned"], i + 1)
                    if not first:
                        act.wait_ge(S["product"], i - 1)
                    nc.scalar.copy(both_t[:, o, :, :], k.ps[:, o, :].rearrange("p (a b) -> p a b", b=P))
                    nc.scalar.copy(ones_t[:, o, :], k.ps[0:3, 6, 0:P]).then_inc(S["turned_copied"], 1)
                    act.wait_ge(S["product"], i + 1)
                    nc.scalar.activation(rz[:, o, :], k.ps[:, 2 + o, :], ACT.Sigmoid).then_inc(S["gates"], 1)
                    act.wait_ge(S["candidate"], i + 1)
                    nc.scalar.activation(new[:, o, :], new[:, o, :], ACT.Tanh).then_inc(S["tanh_done"], 1)

                tile(0, 0, True)
                tile(1, 1, True)
                with act.Fori(0, (NT - 3) // 2) as g:
                    tile(g * 2 + 2, 0, False)
                    tile(g * 2 + 3, 1, False)
                tile(NT - 1, 0, False)
                emit_sqrt(k, act, mv, S["tile_var"], S["tile_sqrt"])

            @block.tensor
            def _(pe):
                pe.wait_ge(S["loaded"], 16 * 9)
                for m in range(KC):
                    for c in range(KC):
                        nc.tensor.matmul(k.ps[:, 2 * m, :], w2[:, c, bass.ts(m, P)], w_ih[:, c, 0:2 * D],
                                         start=c == 0, stop=c == KC - 1)
                    for c in range(KC):
                        nc.tensor.matmul(k.ps[:, 2 * m + 1, 0:D], w2[:, c, bass.ts(m, P)], w_ih[:, c, 2 * D:],
                                         start=c == 0, stop=c == KC - 1)
                for c in range(KC):
                    nc.tensor.matmul(k.ps[0:1, 4, :], b2[:, c:c + 1], w_ih[:, c, 0:2 * D], start=c == 0,
                                     stop=c == KC - 1)
                for c in range(KC):
                    last = nc.tensor.matmul(k.ps[0:1, 5, 0:D], b2[:, c:c + 1], w_ih[:, c, 2 * D:], start=c == 0,
                                            stop=c == KC - 1)
                last.then_inc(S["fused"], 1)
                pe.wait_ge(S["w_ready"], 1)

                def tile(i, o, first):
                    pe.wait_ge(S["normed"], i + 1)
                    pe.wait_ge(S["turned_copied"], i)
                    for c in range(4):
                        nc.tensor.transpose(k.ps[:, o, bass.ts(c, P)], both[:, o, bass.ts(c, P)], k.ident[:])
                    nc.tensor.transpose(k.ps[0:3, 6, 0:P], both[:, o, 2 * D:], k.ident[:]).then_inc(S["turned"], 1)
                    pe.wait_ge(S["turned_copied"], i + 1)
                    if not first:
                        pe.wait_ge(S["candidate"], i - 1)
                    rz_p, i_n, h_n = k.ps[:, 2 + o, :], k.ps[:, 4 + o, 0:D], k.ps[:, 4 + o, D:]
                    x_t, m_t, one = both_t[:, o, 0:2, :], both_t[:, o, 2:4, :], ones_t[:, o, :]
                    for c in range(KC):
                        nc.tensor.matmul(rz_p, x_t[:, c, :], w_hh[:, c, 0:2 * D], start=c == 0, stop=False)
                    for c in range(KC):
                        nc.tensor.matmul(rz_p, m_t[:, c, :], w_in[:, c, 0:2 * D], start=False, stop=False)
                    nc.tensor.matmul(rz_p, one, bias[:, 0:2 * D], start=False, stop=True)
                    for c in range(KC):
                        nc.tensor.matmul(i_n, m_t[:, c, :], w_in[:, c, 2 * D:], start=c == 0, stop=False)
                    nc.tensor.matmul(i_n, one, bias[:, 2 * D:3 * D], start=False, stop=True)
                    for c in range(KC):
                        nc.tensor.matmul(h_n, x_t[:, c, :], w_hh[:, c, 2 * D:], start=c == 0, stop=False)
                    nc.tensor.matmul(h_n, one, bias[:, 3 * D:], start=False, stop=True).then_inc(S["product"], 1)

                tile(0, 0, True)
                tile(1, 1, True)
                with pe.Fori(0, (NT - 3) // 2) as g:
                    tile(g * 2 + 2, 0, False)
                    tile(g * 2 + 3, 1, False)
                tile(NT - 1, 0, False)


def experts(k):
    nc, t = k.nc, k.t
    ctx, sb, sem = phase(k)
    TOK = U * P
    HALF = TOK // 2
    with ctx:
        w1, w2 = sb("w1", [P, NE, KC, ED]), sb("w2", [P, NE, EK, D])
        b1, b2 = sb("b1", [P, NE, EK]), sb("b2", [NE, D])
        w_gate, b_gate, g_bias = sb("w_gate", [P, KC, NE]), sb("b_gate", [P, NE]), sb("g_bias", [P, NE])
        rank = sb("rank", [P, U, NE])
        st, mv = sb("st", [P, NT * 6]), sb("mv", [P, 5, NT])
        xn, xt = sb("xn", [P, U, D]), sb("xt", [P, KC, TOK])
        hid = sb("hid", [P, 2, EK, TOK])
        y = sb("y", [P, U, D])
        logit, eq, one, two, mix = (sb(n, [P, U, NE]) for n in ("logit", "eq", "one", "two", "mix"))
        best = sb("best", [P, 6, U])
        mix_t = sb("mix_t", [NE, U, P])
        names = ("loaded", "gate_loaded", "dve_step", "stats_ready", "sqrt_ready", "ranked", "normed", "turned",
                 "turned_copied", "gated", "chain", "gap", "gap_exp", "mix_ready", "mix_turned", "mix_copied", "based",
                 "filled", "based_mix", "hidden", "active", "projected", "mixed")
        S = {n: sem(n) for n in names}
        stored = [sem(f"stored{u}") for u in range(U)]

        def groups(engine, group):
            with engine.Fori(0, GROUPS - 1) as g:
                group(g, False)
            group(GROUPS - 1, True)

        with nc.Block() as block:
            @block.sync
            def _(sp):
                load_weights(k, sp, S["gate_loaded"], [
                    (w_gate[:], chunks(t["w_gate"])), (b_gate[:], across(t["b_gate"])), (g_bias[:], across(t["gate_bias"]))])
                load_weights(k, sp, S["loaded"], [(b1[:], t["e_b1_cols"]), (b2[:], t["e_b2"])])
                for e in range(NE):
                    sp.dma_start(w1[:, e, :, :], chunks(t["e_w1"][e])).then_inc(S["loaded"], 16)
                    sp.dma_start(w2[:, e, :, :], chunks(t["e_w2"][e])).then_inc(S["loaded"], 16)

                def group(g, last):
                    for u in range(U):
                        i = g * U + u
                        sp.wait_ge(S["mixed"], (g * NE + NE - 1) * U + u + 1)
                        if last and u == U - 1:
                            sp.dma_start(t["out"][(NT - 1) * P:N, :], y[0:TAIL, u, :]).then_inc(stored[u], 16)
                        else:
                            sp.dma_start(t["out"][bass.ts(i, P), :], y[:, u, :]).then_inc(stored[u], 16)

                groups(sp, group)
                for u in range(U):
                    sp.wait_ge(stored[u], 16 * GROUPS)

            @block.vector
            def _(dve):
                step = Steps(dve, S["dve_step"])
                emit_norm(k, dve, st, mv, S["stats_ready"], S["sqrt_ready"], step)
                for u in range(U):
                    last = nc.vector.tensor_scalar(rank[:, u, :], k.iota[:, 0:NE], -1.0, float(NE), ALU.mult, ALU.add)
                step(last)
                dve.wait_ge(S["gate_loaded"], 48)
                CH = 18

                def group(g, final):
                    def link(n, ins):
                        ins.then_inc(S["chain"], 1)
                        dve.wait_ge(S["chain"], g * CH + n)

                    for u in range(U):
                        i = g * U + u
                        dve.wait_ge(S["turned"], i + 1)
                        nc.vector.tensor_scalar(xn[:, u, :], k.xs[:, bass.ts(i, D)], mv[:, 0, bass.ds(i, 1)],
                                                mv[:, 4, bass.ds(i, 1)], ALU.subtract, ALU.mult).then_inc(S["normed"], 1)
                    for u in range(U):
                        i = g * U + u
                        dve.wait_ge(stored[u], 16 * g)
                        last = nc.vector.tensor_scalar(y[:, u, :], k.xs[:, bass.ts(i, D)], 1.0, None, ALU.mult)
                    last.then_inc(S["filled"], 1)
                    dve.wait_ge(S["gated"], g + 1)

                    def spread(v):
                        return v.unsqueeze(2).to_broadcast([P, U, NE])

                    def same(v):
                        return v[:].unsqueeze(1).to_broadcast([P, U, NE])

                    link(1, nc.vector.tensor_tensor(logit[:], k.ps[:, 7, 0:U * NE].rearrange(
                        "p (u e) -> p u e", e=NE), same(b_gate), ALU.add))
                    link(2, nc.vector.tensor_tensor(logit[:], logit[:], same(g_bias), ALU.add))
                    n = 2
                    for hot, top in ((one, best[:, 0, :]), (two, best[:, 1, :])):
                        link(n + 1, nc.vector.tensor_reduce(top, logit[:], AX, ALU.max))
                        link(n + 2, nc.vector.tensor_tensor(eq[:], logit[:], spread(top), ALU.is_equal))
                        link(n + 3, nc.vector.tensor_tensor(eq[:], eq[:], rank[:], ALU.mult))
                        link(n + 4, nc.vector.tensor_reduce(best[:, 2, :], eq[:], AX, ALU.max))
                        link(n + 5, nc.vector.tensor_tensor(hot[:], eq[:], spread(best[:, 2, :]), ALU.is_equal))
                        if hot is one:
                            link(n + 6, nc.vector.scalar_tensor_tensor(out=logit[:], in0=one[:], scalar=-BIG,
                                                                       in1=logit[:], op0=ALU.mult, op1=ALU.add))
                            n += 6
                    nc.vector.tensor_tensor(best[:, 3, :], best[:, 1, :], best[:, 0, :], ALU.subtract).then_inc(S["gap"], 1)
                    dve.wait_ge(S["gap_exp"], g + 1)
                    link(14, nc.vector.tensor_scalar(best[:, 4, :], best[:, 3, :], 1.0, None, ALU.add))
                    link(15, nc.vector.reciprocal(best[:, 4, :], best[:, 4, :]))
                    link(16, nc.vector.tensor_tensor(best[:, 5, :], best[:, 3, :], best[:, 4, :], ALU.mult))
                    link(17, nc.vector.tensor_tensor(one[:], one[:], spread(best[:, 4, :]), ALU.mult))
                    link(18, nc.vector.tensor_tensor(two[:], two[:], spread(best[:, 5, :]), ALU.mult))
                    nc.vector.tensor_tensor(mix[:], one[:], two[:], ALU.add).then_inc(S["mix_ready"], 1)
                    dve.wait_ge(S["mix_ready"], g + 1)
                    dve.wait_ge(S["filled"], g + 1)
                    for u in range(U):
                        i = g * U + u
                        dve.wait_ge(S["based"], i + 1)
                        nc.vector.tensor_tensor(y[:, u, :], y[:, u, :], k.ps[:, 4 + u % 2, 0:D],
                                                ALU.add).then_inc(S["based_mix"], 1)
                    for e in range(NE):
                        for u in range(U):
                            n = (g * NE + e) * U + u
                            dve.wait_ge(S["projected"], n + 1)
                            if e:
                                dve.wait_ge(S["mixed"], n - U + 1)
                            else:
                                dve.wait_ge(S["based_mix"], g * U + u + 1)
                            nc.vector.scalar_tensor_tensor(
                                out=y[:, u, :], in0=k.ps[:, 4 + u % 2, 0:D], scalar=mix[:, u, e:e + 1],
                                in1=y[:, u, :], op0=ALU.mult, op1=ALU.add).then_inc(S["mixed"], 1)

                groups(dve, group)

            @block.scalar
            def _(act):
                emit_sqrt(k, act, mv, S["stats_ready"], S["sqrt_ready"])
                act.wait_ge(S["loaded"], 16 * (2 + 2 * NE))

                def relu(g, e):
                    for m in range(EK):
                        n = (g * NE + e) * EK + m
                        act.wait_ge(S["hidden"], n + 1)
                        if e >= 2:
                            act.wait_ge(S["projected"], (g * NE + e - 1) * U)
                        else:
                            act.wait_ge(S["projected"], g * NE * U)
                        nc.scalar.activation(
                            hid[:, e % 2, m, :].rearrange("p (a b) -> p a b", b=HALF),
                            k.ps[:, 2 * (m % 2):2 * (m % 2) + 2, 0:HALF], ACT.Relu,
                            bias=b1[:, e, m:m + 1]).then_inc(S["active"], 1)

                def group(g, last):
                    act.wait_ge(S["hidden"], g * NE * EK)
                    for u in range(U):
                        i = g * U + u
                        act.wait_ge(S["turned"], i + U + 1)
                        nc.scalar.copy(xt[:, :, bass.ts(u, P)],
                                       k.ps[:, 6, 0:D].rearrange("p (c n) -> p c n", n=P)).then_inc(S["turned_copied"], 1)
                    act.wait_ge(S["gap"], g + 1)
                    nc.scalar.activation(best[:, 3, :], best[:, 3, :], ACT.Exp).then_inc(S["gap_exp"], 1)
                    relu(g, 0)
                    act.wait_ge(S["mix_turned"], g + 1)
                    nc.scalar.copy(mix_t[:], k.ps[0:NE, 6:8, :].rearrange("p a b -> p (a b)")[:, 0:TOK].rearrange(
                        "p (u n) -> p u n", n=P)).then_inc(S["mix_copied"], 1)
                    for e in range(1, NE):
                        relu(g, e)

                groups(act, group)

            @block.tensor
            def _(pe):
                pe.sem_inc(S["turned"], U)

                def hidden(g, e):
                    for m in range(EK):
                        n = (g * NE + e) * EK + m
                        if e or m >= 2:
                            pe.wait_ge(S["active"], n - 1)
                        else:
                            pe.wait_ge(S["active"], g * NE * EK)
                        for h in range(2):
                            for c in range(KC):
                                last = nc.tensor.matmul(k.ps[:, 2 * (m % 2) + h, 0:HALF], w1[:, e, c, bass.ts(m, P)],
                                                        xt[:, c, bass.ts(h, HALF)], start=c == 0, stop=c == KC - 1)
                        last.then_inc(S["hidden"], 1)

                def project(g, e):
                    pe.wait_ge(S["active"], (g * NE + e + 1) * EK)
                    for u in range(U):
                        n = (g * NE + e) * U + u
                        if u >= 2:
                            pe.wait_ge(S["mixed"], n - 1)
                        elif e:
                            pe.wait_ge(S["mixed"], n - u)
                        else:
                            pe.wait_ge(S["based_mix"], (g + 1) * U)
                        for m in range(EK):
                            last = nc.tensor.matmul(k.ps[:, 4 + u % 2, 0:D], hid[:, e % 2, m, bass.ts(u, P)],
                                                    w2[:, e, m, :], start=m == 0, stop=m == EK - 1)
                        last.then_inc(S["projected"], 1)

                def group(g, last_group):
                    for u in range(U):
                        i = g * U + u
                        pe.wait_ge(S["normed"], i + 1)
                        pe.wait_ge(S["turned_copied"], i)
                        pe.wait_ge(S["mix_copied"], g)
                        for c in range(KC):
                            last = nc.tensor.transpose(k.ps[:, 6, bass.ts(c, P)], xn[:, u, bass.ts(c, P)], k.ident[:])
                        last.then_inc(S["turned"], 1)
                    pe.wait_ge(S["turned_copied"], (g + 1) * U)
                    pe.wait_ge(S["gate_loaded"], 48)
                    for u in range(U):
                        for c in range(KC):
                            last = nc.tensor.matmul(k.ps[:, 7, bass.ts(u, NE)], xt[:, c, bass.ts(u, P)],
                                                    w_gate[:, c, :], start=c == 0, stop=c == KC - 1)
                    last.then_inc(S["gated"], 1)
                    pe.wait_ge(S["loaded"], 16 * (2 + 2 * NE))
                    hidden(g, 0)
                    pe.wait_ge(S["mix_ready"], g + 1)
                    for u in range(U):
                        bank, at = 6 + u // 4, (u % 4) * P
                        last = nc.tensor.transpose(k.ps[0:NE, bank, at:at + P], mix[:, u, :], k.ident[:])
                    last.then_inc(S["mix_turned"], 1)
                    hidden(g, 1)
                    pe.wait_ge(S["mix_copied"], g + 1)
                    for u in range(U):
                        i = g * U + u
                        if u >= 2:
                            pe.wait_ge(S["based_mix"], i - 1)
                        else:
                            pe.wait_ge(S["mixed"], g * NE * U)
                        nc.tensor.matmul(k.ps[:, 4 + u % 2, 0:D], mix_t[:, u, :], b2[:], start=True,
                                         stop=True).then_inc(S["based"], 1)
                    project(g, 0)
                    for e in range(2, NE):
                        hidden(g, e)
                        project(g, e - 1)
                    project(g, NE - 1)

                groups(pe, group)


def build(nc, t):
    ctx = ExitStack()
    with ctx:
        def sb(name, shape, dtype=F32):
            return ctx.enter_context(nc.sbuf_tensor(name, shape, dtype))

        k = Kept(nc, t)
        k.ps = ctx.enter_context(nc.psum_tensor("banks", [P, 8, 512], F32))
        k.xs = sb("xs", [P, NT * D])
        k.ident, k.ones = sb("ident", [P, P]), sb("ones", [P, P])
        k.tri_incl, k.tri_strict = sb("tri_incl", [P, P]), sb("tri_strict", [P, P])
        k.iota, k.mask = sb("iota", [P, P]), sb("mask", [P, NT])
        k.dst_i, k.src_i = sb("dst_i", [P, EC], I32), sb("src_i", [P, EC], I32)
        k.dst_f = sb("dst_f", [P, EC])
        k.pos_i, k.edge_rec = sb("pos_i", [P, EC], I32), sb("edge_rec", [P, EC * 2], I32)
        k.base_dst, k.base_src = sb("base_dst", [P, ST]), sb("base_src", [P, ST])
        k.start_dst, k.start_src = sb("start_dst", [1, ST], I32), sb("start_src", [1, ST], I32)
        k.tile_dst, k.tile_src = sb("tile_dst", [1, ST], I32), sb("tile_src", [1, ST], I32)
        k.large = sb("large", [P, NT * (2 * D + 1)])
        k.source_part, k.sums = k.large[:, 0:NT * D], k.large[:, NT * D:]
        k.new_rows = k.source_part
        phases = [setup, gat_tables, gat_scores, gat_edges, slice_attention, message_tables, message_edges, gated_update, experts]
        for f in phases:
            f(k)
            nc.clear_and_free_semaphores(k.semaphores)
            k.semaphores = []
            nc.all_engine_barrier()


_LAYOUT = {
    "x": ("x", lambda a: a), "src": ("src", lambda a: a), "dst": ("dst", lambda a: a),
    "w_lin": ("L0_gnn_W_lin", lambda a: a), "w_lin_t": ("L0_gnn_W_lin", lambda a: a.T),
    "b_lin": ("L0_gnn_b_lin", lambda a: a), "b_lin_cols": ("L0_gnn_b_lin", lambda a: a.reshape(KC, P).T),
    "w_gat": ("L0_gnn_W_gat", lambda a: a),
    "attn_l": ("L0_gnn_attn_l", lambda a: a), "attn_r": ("L0_gnn_attn_r", lambda a: a),
    "gat_bias": ("L0_gnn_gat_bias", lambda a: a),
    "w_fx": ("L0_ffn_W_fx", lambda a: a), "b_fx": ("L0_ffn_b_fx", lambda a: a),
    "w_x_t": ("L0_ffn_W_x", lambda a: a.T), "b_x_cols": ("L0_ffn_b_x", lambda a: a.reshape(SH, SD).T),
    "w_slice": ("L0_ffn_W_slice", lambda a: a), "b_slice": ("L0_ffn_b_slice", lambda a: a),
    "w_q": ("L0_ffn_W_q", lambda a: a), "w_k": ("L0_ffn_W_k", lambda a: a), "w_v": ("L0_ffn_W_v", lambda a: a),
    "w_out": ("L0_ffn_W_out", lambda a: a), "b_out": ("L0_ffn_b_out", lambda a: a),
    "temp": ("L0_ffn_temperature", lambda a: a.reshape(-1)),
    "w1_t": ("L1_gnn_W1", lambda a: a.T), "b1": ("L1_gnn_b1", lambda a: a),
    "w2": ("L1_gnn_W2", lambda a: a), "b2_cols": ("L1_gnn_b2", lambda a: a.reshape(KC, P).T),
    "w_ih_t": ("L1_gnn_w_ih", lambda a: a.T), "w_hh_t": ("L1_gnn_w_hh", lambda a: a.T),
    "b_ih": ("L1_gnn_b_ih", lambda a: a), "b_hh": ("L1_gnn_b_hh", lambda a: a),
    "gamma": ("L1_gnn_gamma", lambda a: a), "beta": ("L1_gnn_beta", lambda a: a),
    "w_gate": ("L1_ffn_Wg", lambda a: a), "b_gate": ("L1_ffn_bg", lambda a: a),
    "gate_bias": ("L1_ffn_bias", lambda a: a),
    "e_w1": ("L1_ffn_W1", lambda a: a), "e_b1_cols": ("L1_ffn_b1", lambda a: a.reshape(NE, EK, P).transpose(2, 0, 1)),
    "e_w2": ("L1_ffn_W2", lambda a: a), "e_b2": ("L1_ffn_b2", lambda a: a),
}
_TABLES = {
    "gat_rows": ((NP, D), F32), "el_rows": ((NP, H1), F32), "er_rows": ((NP, H1), F32),
    "rec_gat": ((ER, 2 + H1), I32), "rec_src": ((ER, 2), I32), "msg_rows": ((NP, D), F32),
    "slice_bias": ((SH, SD), F32),
}


def kernel(**inputs):
    import numpy as np
    import concourse.bacc as bacc
    from concourse.bass_utils import run_bass_kernel_spmd as run

    nc = bacc.Bacc("TRN2", target_bir_lowering=False, num_devices=1)
    tables, arrays = {}, {}
    for name, (source, lay) in _LAYOUT.items():
        a = np.ascontiguousarray(lay(np.asarray(inputs[source])))
        arrays["in_" + name] = a
        tables[name] = nc.dram_tensor("in_" + name, a.shape, mybir.dt.from_np(a.dtype), kind="ExternalInput").ap()
    for name, (shape, dtype) in _TABLES.items():
        tables[name] = nc.dram_tensor("tab_" + name, list(shape), dtype, kind="Internal").ap()
    tables["out"] = nc.dram_tensor("out_0_dram", (N, D), F32, kind="ExternalOutput").ap()
    build(nc, tables)
    return run(nc, [arrays], core_ids=[0]).results[0]["out_0_dram"]
```

```python
from contextlib import ExitStack

import concourse.bass as bass
from concourse import mybir
from concourse.alu_op_type import AluOpType as ALU

ACT = mybir.ActivationFunctionType
F32 = mybir.dt.float32
I32 = mybir.dt.int32
AX = mybir.AxisListType.X
DVE, SP = mybir.EngineType.DVE, mybir.EngineType.SP
PE = mybir.EngineType.PE

P = 128
N = 3125
NT = -(-N // P)
NP = NT * P
TAIL = N - (NT - 1) * P
D = 256
KC = D // P
E = 50000
EC = 392
EP = P * EC
EFULL = E // EC
EREST = E - EFULL * EC
ST = (EP + NT * (P - 1)) // P
ER = EP + P
H1 = 8
HD = D // H1
SH, SD = 8, 64
SI = SH * SD
PAIRS = SH // 2
NE, ED = 8, 512
EK = ED // P
U = 5
GROUPS = NT // U
BIG = 1.0e30
EPS = 1e-5
RW = 2 + 2 * H1
SEND = 7
SENT_BY_TABLES, SENT_BY_SLICES, SENT_BY_MESSAGES = (0, 14), (14, 44), (44, EC // SEND)
assert EC % SEND == 0 and all(a % 2 == 0 == b % 2 for a, b in (SENT_BY_TABLES, SENT_BY_SLICES, SENT_BY_MESSAGES))
assert NT % U == 0 and EC % 28 == 0 and EREST < EC


class Kept:

    def __init__(self, nc, tables):
        self.nc, self.t, self.count, self.semaphores = nc, tables, 0, []


class Steps:

    def __init__(self, engine, semaphore, start=0):
        self.engine, self.semaphore, self.n = engine, semaphore, start

    def __call__(self, instruction):
        instruction.then_inc(self.semaphore, 1)
        self.n = self.n + 1
        self.engine.wait_ge(self.semaphore, self.n)


def phase(k):
    ctx = ExitStack()
    nc = k.nc
    k.count += 1
    tag = f"p{k.count}_"

    def sb(name, shape, dtype=F32):
        return ctx.enter_context(nc.sbuf_tensor(tag + name, shape, dtype))

    def sem(name):
        handle = nc.alloc_semaphore(name=tag + name)
        k.semaphores.append(handle)
        return handle

    return ctx, sb, sem


def emit_norm(k, dve, st, mv, stats_ready, sqrt_ready, steps):
    nc = k.nc
    with dve.Fori(0, GROUPS) as g:
        for u in range(U):
            last = nc.vector.bn_stats(st[:, bass.ts(g * U + u, 6)], k.xs[:, bass.ts(g * U + u, D)])
        last.then_inc(steps.semaphore, 1)
    steps.n += GROUPS
    dve.wait_ge(steps.semaphore, steps.n)
    emit_moments(k, dve, st, mv, stats_ready, sqrt_ready, steps)


def emit_moments(k, dve, st, mv, stats_ready, sqrt_ready, steps):
    nc = k.nc
    s = st[:].rearrange("p (i c) -> p i c", c=6)
    mean, var, dif = mv[:, 0, :], mv[:, 1, :], mv[:, 2, :]
    steps(nc.vector.tensor_tensor(dif, s[:, :, 1], s[:, :, 4], ALU.subtract))
    steps(nc.vector.tensor_tensor(var, s[:, :, 2], s[:, :, 5], ALU.add))
    steps(nc.vector.tensor_tensor(dif, dif, dif, ALU.mult))
    steps(nc.vector.tensor_scalar(dif, dif, 0.25, None, ALU.mult))
    steps(nc.vector.scalar_tensor_tensor(out=var, in0=var, scalar=1.0 / D, in1=dif, op0=ALU.mult, op1=ALU.add))
    steps(nc.vector.tensor_tensor(mean, s[:, :, 1], s[:, :, 4], ALU.add))
    steps(nc.vector.tensor_scalar(mean, mean, 0.5, None, ALU.mult))
    nc.vector.tensor_scalar(mv[:, 3, :], var, EPS, None, ALU.add).then_inc(stats_ready, 1)
    rstd = mv[:, 4, :]
    dve.wait_ge(sqrt_ready, 1)
    steps(nc.vector.reciprocal(rstd, rstd))
    steps(nc.vector.tensor_tensor(dif, rstd, rstd, ALU.mult))
    steps(nc.vector.tensor_tensor(dif, dif, mv[:, 3, :], ALU.mult))
    steps(nc.vector.tensor_scalar(dif, dif, -0.5, 1.5, ALU.mult, ALU.add))
    steps(nc.vector.tensor_tensor(rstd, rstd, dif, ALU.mult))


def emit_sqrt(k, act, mv, stats_ready, sqrt_ready):
    act.wait_ge(stats_ready, 1)
    k.nc.scalar.activation(mv[:, 4, :], mv[:, 3, :], ACT.Sqrt).then_inc(sqrt_ready, 1)


def load_weights(k, sp, sem, pairs):
    for dst, src in pairs:
        sp.dma_start(dst, src).then_inc(sem, 16)
    return 16 * len(pairs)


class Sender:

    def __init__(self, k, sb, sem):
        self.k = k
        self.place, self.pair = sb("place", [P, 2, SEND], I32), sb("pair", [P, 2, SEND, 2], I32)
        self.placed, self.scattering, self.sent = sem("placed"), sem("scattering"), [sem("sent0"), sem("sent1")]


def send_edges(pool, sender, first, last):
    nc, k, placed, sent = sender.k.nc, sender.k, sender.placed, sender.sent
    place, pair = sender.place, sender.pair
    with pool.Fori(0, (last - first) // 2) as g:
        for s in range(2):
            c = 2 * g + (first + s)
            pool.wait_ge(sent[s], 16 * SEND * g)
            nc.gpsimd.tensor_copy(place[:, s, :], k.pos_i[:, bass.ts(c, SEND)]).then_inc(placed, 1)
            nc.gpsimd.tensor_copy(pair[:, s, :, :].rearrange("p j c -> p (j c)"),
                                  k.edge_rec[:, bass.ts(c, 2 * SEND)]).then_inc(placed, 1)
            pool.wait_ge(placed, 4 * g + (2 * s + 2))
            pool.sem_inc(sender.scattering, 1)
            for j in range(SEND):
                nc.gpsimd.indirect_dma_start(
                    k.t["rec_src"][0:EP, :], bass.IndirectOffsetOnAxis(ap=place[:, s, j:j + 1], axis=0),
                    pair[:, s, j, :], None).then_inc(sent[s], 16)
    for s in range(2):
        pool.wait_ge(sent[s], 16 * SEND * (last - first) // 2)


def staggered(engine, stages):
    deepest = max(lag for _, lag in stages)
    first = deepest + 4 + (NT - deepest) % 4

    def one(base, n):
        for stage, lag in stages:
            if not (isinstance(base, int) and (n < lag or n - lag >= NT)):
                stage(base + (n - lag), (n - lag) % 4)

    for n in range(first):
        one(0, n)
    with engine.Fori(0, (NT - first) // 4) as g:
        for n in range(4):
            one(g * 4, first + n)
    for n in range(NT, NT + deepest):
        one(0, n)


def row(v):
    return v.rearrange("(a d) -> a d", a=1)


def across(v):
    return row(v).to_broadcast([P, v.shape[0]])


def chunks(w):
    return w.rearrange("(c p) n -> p c n", p=P)


def setup(k):
    nc, t = k.nc, k.t
    ctx, sb, sem = phase(k)
    with ctx:
        loaded, made, made2 = sem("loaded"), sem("made"), sem("made2")
        dve_step = sem("dve_step")
        bkt_i, bkt = sb("bucket_i", [P, EC], I32), sb("bucket", [P, EC])
        junk, scan, part = sb("junk", [P, EC]), sb("scan", [P, EC]), sb("part", [P, EC])
        ones_e = sb("ones_e", [P, EC])
        pos = sb("pos", [P, EC])
        counts = sb("counts", [P, NT])
        src_f = sb("src_f", [P, EC])
        small = sb("small", [P, 8])
        small_i = sb("small_i", [P, 8], I32)
        tot, off = sb("tot", [P, NT]), sb("off", [P, NT])
        grid, vrow = sb("grid", [NT, ST]), sb("vrow", [NT, P])
        starts = sb("starts", [P, ST])
        iota_q = sb("iota_q", [P, ST])
        pad_gat, pad2 = sb("pad_gat", [P, RW], I32), sb("pad2", [P, 2], I32)
        pad_f = sb("pad_f", [P, 1])
        counted, summed, tiles_ready, cum_ready, grid_ready, table_ready = (
            sem(s) for s in ("counted", "summed", "tiles_ready", "cum_ready", "grid_ready", "table_ready"))
        pads_made, pads_stored = sem("pads_made"), sem("pads_stored")
        edges_filled, x_filled = sem("edges_filled"), sem("x_filled")

        with nc.Block() as block:
            @block.sync
            def _(sp):
                sp.wait_ge(x_filled, 1)
                sp.dma_start(k.xs[:, 0:(NT - 1) * D].rearrange("p (i d) -> p i d", d=D),
                             t["x"][0:(NT - 1) * P, :].rearrange("(i p) d -> p i d", p=P)).then_inc(loaded, 16)
                sp.dma_start(k.xs[0:TAIL, (NT - 1) * D:NT * D], t["x"][(NT - 1) * P:N, :]).then_inc(loaded, 16)
                sp.wait_ge(edges_filled, 2)
                for dst, src in ((k.dst_i, t["dst"]), (k.src_i, t["src"])):
                    sp.dma_start(dst[0:EFULL, :], src[0:EFULL * EC].rearrange("(p j) -> p j", j=EC)).then_inc(loaded, 16)
                    sp.dma_start(dst[EFULL:EFULL + 1, 0:EREST], row(src[EFULL * EC:E])).then_inc(loaded, 16)
                sp.wait_ge(pads_made, 5)
                sp.dma_start(t["rec_gat"][EP:ER, :], pad_gat[:]).then_inc(pads_stored, 16)
                sp.dma_start(t["rec_src"][EP:ER, :], pad2[:]).then_inc(pads_stored, 16)
                sp.wait_ge(pads_stored, 32)

            @block.gpsimd
            def _(pool):
                nc.gpsimd.memset(k.xs[:, (NT - 1) * D:NT * D], 0.0).then_inc(x_filled, 1)
                nc.gpsimd.memset(k.dst_i[:], NP - 1).then_inc(edges_filled, 1)
                nc.gpsimd.memset(k.src_i[:], NP - 1).then_inc(edges_filled, 1)
                nc.gpsimd.memset(pad_f[:], float(NP - 1)).then_inc(pads_made, 1)
                nc.gpsimd.memset(pad_gat[:], 0).then_inc(pads_made, 1)
                pool.wait_ge(pads_made, 2)
                nc.gpsimd.memset(pad_gat[:, 0:1], NP - 1).then_inc(pads_made, 1)
                nc.gpsimd.memset(pad2[:, 0:1], NP - 1).then_inc(pads_made, 1)
                nc.gpsimd.memset(k.ident[:], 0.0).then_inc(made, 1)
                nc.gpsimd.memset(k.ones[:], 1.0).then_inc(made, 1)
                nc.gpsimd.memset(k.tri_incl[:], 1.0).then_inc(made, 1)
                nc.gpsimd.memset(k.tri_strict[:], 1.0).then_inc(made, 1)
                nc.gpsimd.memset(k.mask[:], 1.0).then_inc(made, 1)
                nc.gpsimd.iota(k.iota[:], pattern=[[1, P]], base=0, channel_multiplier=0,
                               allow_small_or_imprecise_dtypes=True).then_inc(made, 1)
                nc.gpsimd.iota(iota_q[:], pattern=[[1, ST]], base=0, channel_multiplier=0,
                               allow_small_or_imprecise_dtypes=True).then_inc(made, 1)
                pool.wait_ge(made, 7)
                nc.gpsimd.affine_select(out=k.ident[:], in_=k.ident[:], compare_op=ALU.not_equal, fill=1.0,
                                        base=0, pattern=[[-1, P]], channel_multiplier=1).then_inc(made2, 1)
                nc.gpsimd.affine_select(out=k.tri_incl[:], in_=k.tri_incl[:], compare_op=ALU.is_ge, fill=0.0,
                                        base=0, pattern=[[1, P]], channel_multiplier=-1).then_inc(made2, 1)
                nc.gpsimd.affine_select(out=k.tri_strict[:], in_=k.tri_strict[:], compare_op=ALU.is_ge, fill=0.0,
                                        base=-1, pattern=[[1, P]], channel_multiplier=-1).then_inc(made2, 1)
                nc.gpsimd.affine_select(out=k.mask[:, NT - 1:NT], in_=k.mask[:, NT - 1:NT], compare_op=ALU.is_ge,
                                        fill=0.0, base=TAIL - 1, pattern=[[0, 1]],
                                        channel_multiplier=-1).then_inc(made2, 1)

            @block.vector
            def _(dve):
                step = Steps(dve, dve_step)
                dve.wait_ge(pads_made, 4)
                step(nc.vector.tensor_copy(pad_gat[:, 1:2].bitcast(F32), pad_f[:]))
                nc.vector.tensor_copy(pad2[:, 1:2].bitcast(F32), pad_f[:]).then_inc(pads_made, 1)
                step(nc.vector.memset(ones_e[:], 1.0))
                dve.wait_ge(made2, 4)
                dve.wait_ge(loaded, 96)
                step(nc.vector.tensor_copy(k.dst_f[:], k.dst_i[:]))
                step(nc.vector.tensor_copy(src_f[:], k.src_i[:]))
                for n, (key, base, start, tile) in enumerate(((k.dst_i, k.base_dst, k.start_dst, k.tile_dst),
                                                              (k.src_i, k.base_src, k.start_src, k.tile_src))):
                    step(nc.vector.tensor_scalar(bkt_i[:], key[:], 7, None, ALU.arith_shift_right))
                    step(nc.vector.tensor_copy(bkt[:], bkt_i[:]))
                    for b in range(NT):
                        last = nc.vector.tensor_scalar(junk[:], bkt[:], float(b), 0.0, ALU.is_equal, ALU.add,
                                                       accum_out=counts[:, b:b + 1])
                        if b < NT - 1:
                            step(last)
                    last.then_inc(counted, 1)
                    dve.wait_ge(summed, n + 1)
                    step(nc.vector.tensor_scalar(small[0:NT, 0:1], k.ps[0:NT, 0, 0:1], float(P - 1), None, ALU.add))
                    step(nc.vector.tensor_copy(small_i[0:NT, 0:1], small[0:NT, 0:1]))
                    step(nc.vector.tensor_scalar(small_i[0:NT, 1:2], small_i[0:NT, 0:1], 7, None,
                                                 ALU.arith_shift_right))
                    step(nc.vector.tensor_copy(small[0:NT, 1:2], small_i[0:NT, 1:2]))
                    step(nc.vector.scalar_tensor_tensor(out=small[0:NT, 2:3], in0=small[0:NT, 1:2], scalar=-float(P),
                                                        in1=k.ps[0:NT, 0, 0:1], op0=ALU.mult, op1=ALU.add))
                    nc.vector.tensor_scalar(vrow[:], k.ones[0:NT, :], small[0:NT, 2:3], None,
                                            ALU.mult).then_inc(tiles_ready, 1)
                    dve.wait_ge(cum_ready, n + 1)
                    nc.vector.tensor_scalar(grid[:], iota_q[0:NT, :], k.ps[0:NT, 3, 0:1], None,
                                            ALU.is_ge).then_inc(grid_ready, 1)
                    dve.wait_ge(table_ready, n + 1)
                    step(nc.vector.tensor_scalar(base[:], k.ps[:, 4, 0:ST], float(NT - 1), None, ALU.min))
                    step(nc.vector.tensor_copy(tile[:], base[0:1, :]))
                    step(nc.vector.tensor_scalar(base[:], base[:], float(P), None, ALU.mult))
                    step(nc.vector.scalar_tensor_tensor(out=starts[:], in0=iota_q[:], scalar=float(P),
                                                        in1=k.ps[:, 5, 0:ST], op0=ALU.mult, op1=ALU.add))
                    step(nc.vector.tensor_scalar(starts[:], starts[:], float(EP), None, ALU.min))
                    step(nc.vector.tensor_copy(start[:], starts[0:1, :]))
                step(nc.vector.tensor_copy(tot[:], k.ps[:, 1, 0:NT]))
                step(nc.vector.tensor_tensor_scan(off[:], ones_e[:, 0:NT], tot[:], -1.0, ALU.mult, ALU.add))
                step(nc.vector.tensor_tensor(off[:], off[:], tot[:], ALU.subtract))
                step(nc.vector.tensor_tensor(off[:], off[:], k.ps[:, 2, 0:NT], ALU.add))
                step(nc.vector.memset(pos[:], 0.0))
                for b in range(NT):
                    step(nc.vector.tensor_scalar(part[:], bkt[:], float(b), None, ALU.is_equal))
                    step(nc.vector.tensor_tensor_scan(scan[:], ones_e[:], part[:], off[:, b:b + 1], ALU.mult, ALU.add))
                    step(nc.vector.tensor_tensor(part[:], part[:], scan[:], ALU.mult))
                    step(nc.vector.tensor_tensor(pos[:], pos[:], part[:], ALU.add))
                step(nc.vector.tensor_copy(k.pos_i[:], pos[:]))
                rec = k.edge_rec[:].rearrange("p (j c) -> p j c", c=2)
                step(nc.vector.tensor_copy(rec[:, :, 0], k.dst_i[:]))
                step(nc.vector.tensor_copy(rec[:, :, 1].bitcast(F32), src_f[:]))

            @block.tensor
            def _(pe):
                pe.wait_ge(made2, 4)
                for n in range(2):
                    pe.wait_ge(counted, n + 1)
                    if n:
                        pe.wait_ge(table_ready, 1)
                    nc.tensor.matmul(k.ps[0:NT, 0, 0:1], counts[:], k.ones[:, 0:1], start=True, stop=True)
                    nc.tensor.matmul(k.ps[:, 1, 0:NT], k.ones[:], counts[:], start=True, stop=True)
                    nc.tensor.matmul(k.ps[:, 2, 0:NT], k.tri_strict[:], counts[:], start=True,
                                     stop=True).then_inc(summed, 1)
                    pe.wait_ge(tiles_ready, n + 1)
                    nc.tensor.matmul(k.ps[0:NT, 3, 0:1], k.tri_incl[0:NT, 0:NT], small[0:NT, 1:2], start=True,
                                     stop=True).then_inc(cum_ready, 1)
                    pe.wait_ge(grid_ready, n + 1)
                    nc.tensor.matmul(k.ps[:, 4, 0:ST], k.ones[0:NT, :], grid[:], start=True, stop=True)
                    nc.tensor.matmul(k.ps[:, 5, 0:ST], vrow[:], grid[:], start=True,
                                     stop=True).then_inc(table_ready, 1)


def gat_tables(k):
    nc, t = k.nc, k.t
    ctx, sb, sem = phase(k)
    C = 2 * D + 2 * H1
    with ctx:
        w_lin_t, w_gat = sb("w_lin_t", [P, KC, D]), sb("w_gat", [P, KC, D])
        b_col = sb("b_col", [P, KC])
        att = sb("att", [P, KC, 2 * H1])
        fused_t = sb("fused_t", [P, KC, D])
        w_all = sb("w_all", [P, KC, C])
        bias_row = sb("bias_row", [1, C])
        bias_col = sb("bias_col", [P, KC])
        bias = sb("bias", [P, C])
        st, mv = sb("st", [P, NT * 6]), sb("mv", [P, 5, NT])
        xn, xt = sb("xn", [P, U, D]), sb("xt", [P, U, D])
        out = sb("out", [P, U, D + H1])
        loaded, zeroed = sem("loaded"), sem("zeroed")
        dve_step, stats_ready, sqrt_ready = sem("dve_step"), sem("stats_ready"), sem("sqrt_ready")
        fused, copied, w_ready = sem("fused"), sem("copied"), sem("w_ready")
        normed, turned, turned_copied, product, added = (
            sem(s) for s in ("normed", "turned", "turned_copied", "product", "added"))
        stored = [sem(f"stored{u}") for u in range(U)]
        sender = Sender(k, sb, sem)

        with nc.Block() as block:
            @block.sync
            def _(sp):
                load_weights(k, sp, loaded, [
                    (w_lin_t[:], chunks(t["w_lin_t"])), (w_gat[:], chunks(t["w_gat"])),
                    (b_col[:], t["b_lin_cols"]),
                    (w_all[:, :, 0:D], chunks(t["w_lin"])), (bias_row[:, 0:D], row(t["b_lin"]))])
                sp.wait_ge(zeroed, 1)
                for n, a in enumerate((t["attn_l"], t["attn_r"])):
                    for h in range(H1):
                        p0 = (h * HD) % P
                        sp.dma_start(att[p0:p0 + HD, h * HD // P, n * H1 + h:n * H1 + h + 1],
                                     a[h, :].rearrange("(d a) -> d a", a=1)).then_inc(loaded, 16)
                with sp.Fori(0, GROUPS) as g:
                    for u in range(U):
                        i = g * U + u
                        sp.wait_ge(added, i + 1)
                        sp.dma_start(t["gat_rows"][bass.ts(i, P), :], out[:, u, 0:D]).then_inc(stored[u], 16)
                        sp.dma_start(t["el_rows"][bass.ts(i, P), :], out[:, u, D:D + H1]).then_inc(stored[u], 16)
                for u in range(U):
                    sp.wait_ge(stored[u], 32 * GROUPS)

            @block.gpsimd
            def _(pool):
                nc.gpsimd.memset(att[:], 0.0).then_inc(zeroed, 1)
                send_edges(pool, sender, *SENT_BY_TABLES)

            @block.vector
            def _(dve):
                step = Steps(dve, dve_step)
                emit_norm(k, dve, st, mv, stats_ready, sqrt_ready, step)
                dve.wait_ge(fused, 1)
                nc.vector.tensor_copy(fused_t[:], k.ps[:, 0:KC, 0:D]).then_inc(copied, 1)
                nc.vector.tensor_copy(w_all[:, :, D:2 * D], k.ps[:, 2:2 + KC, 0:D]).then_inc(copied, 1)
                nc.vector.tensor_copy(bias_row[:, D:2 * D], k.ps[0:1, 4, 0:D]).then_inc(copied, 1)
                nc.vector.tensor_copy(bias_col[:], k.ps[:, 5:5 + KC, 0]).then_inc(copied, 1)
                dve.wait_ge(fused, 2)
                nc.vector.tensor_copy(w_all[:, :, 2 * D:], k.ps[:, 0:KC, 0:2 * H1]).then_inc(copied, 1)
                nc.vector.tensor_copy(bias_row[:, 2 * D:], k.ps[0:1, 4, 0:2 * H1]).then_inc(copied, 1)
                dve.wait_ge(fused, 3)
                nc.vector.tensor_copy(bias[:, 0:ED], k.ps[:, 0, :]).then_inc(copied, 1)
                nc.vector.tensor_copy(bias[:, ED:C], k.ps[:, 1, 0:C - ED]).then_inc(w_ready, 1)
                dve.wait_ge(w_ready, 1)
                dve.wait_ge(copied, 7)
                with dve.Fori(0, GROUPS) as g:
                    for u in range(U):
                        i = g * U + u
                        dve.wait_ge(turned, i + 1)
                        nc.vector.tensor_scalar(xn[:, u, :], k.xs[:, bass.ts(i, D)], mv[:, 0, bass.ds(i, 1)],
                                                mv[:, 4, bass.ds(i, 1)], ALU.subtract,
                                                ALU.mult).then_inc(normed, 1)
                    for u in range(U):
                        i = g * U + u
                        bank = 2 + 2 * (u % 2)
                        dve.wait_ge(product, i + 1)
                        dve.wait_ge(stored[u], 32 * g)
                        nc.vector.tensor_tensor(out[:, u, 0:D], k.ps[:, bank, D:2 * D], bias[:, D:2 * D],
                                                ALU.add)
                        nc.vector.tensor_tensor(out[:, u, D:], k.ps[:, bank + 1, 0:H1], bias[:, 2 * D:2 * D + H1],
                                                ALU.add)
                        nc.vector.tensor_tensor(k.er[:, bass.ts(i, H1)], k.ps[:, bank + 1, H1:2 * H1],
                                                bias[:, 2 * D + H1:], ALU.add)
                        xsl = k.xs[:, bass.ts(i, D)]
                        nc.vector.tensor_tensor(xsl, xsl, k.ps[:, bank, 0:D], ALU.add).then_inc(dve_step, 1)
                        dve.wait_ge(dve_step, step.n + 1 + i)
                        nc.vector.tensor_tensor(xsl, xsl, bias[:, 0:D], ALU.add).then_inc(added, 1)

            @block.scalar
            def _(act):
                emit_sqrt(k, act, mv, stats_ready, sqrt_ready)
                with act.Fori(0, GROUPS) as g:
                    for u in range(U):
                        i = g * U + u
                        act.wait_ge(turned, i + U + 1)
                        nc.scalar.copy(xt[:, u, :], k.ps[:, u % 2, 0:D]).then_inc(turned_copied, 1)

            @block.tensor
            def _(pe):
                pe.sem_inc(turned, U)
                pe.wait_ge(loaded, 16 * (5 + 2 * H1))
                for m in range(KC):
                    for c in range(KC):
                        nc.tensor.matmul(k.ps[:, m, 0:D], w_gat[:, c, bass.ts(m, P)], w_lin_t[:, c, :],
                                         start=c == 0, stop=c == KC - 1)
                for m in range(KC):
                    for c in range(KC):
                        nc.tensor.matmul(k.ps[:, 2 + m, 0:D], w_lin_t[:, c, bass.ts(m, P)], w_gat[:, c, :],
                                         start=c == 0, stop=c == KC - 1)
                for c in range(KC):
                    nc.tensor.matmul(k.ps[0:1, 4, 0:D], b_col[:, c:c + 1], w_gat[:, c, :],
                                     start=c == 0, stop=c == KC - 1)
                for m in range(KC):
                    for c in range(KC):
                        last = nc.tensor.matmul(k.ps[:, 5 + m, 0:1], w_gat[:, c, bass.ts(m, P)], b_col[:, c:c + 1],
                                                start=c == 0, stop=c == KC - 1)
                last.then_inc(fused, 1)
                pe.wait_ge(copied, 4)
                for m in range(KC):
                    for c in range(KC):
                        nc.tensor.matmul(k.ps[:, m, 0:2 * H1], fused_t[:, c, bass.ts(m, P)], att[:, c, :],
                                         start=c == 0, stop=c == KC - 1)
                for c in range(KC):
                    last = nc.tensor.matmul(k.ps[0:1, 4, 0:2 * H1], bias_col[:, c:c + 1], att[:, c, :],
                                            start=c == 0, stop=c == KC - 1)
                last.then_inc(fused, 1)
                pe.wait_ge(copied, 6)
                nc.tensor.matmul(k.ps[:, 0, :], k.ones[0:1, :], bias_row[:, 0:ED], start=True, stop=True)
                nc.tensor.matmul(k.ps[:, 1, 0:C - ED], k.ones[0:1, :], bias_row[:, ED:C], start=True,
                                 stop=True).then_inc(fused, 1)
                pe.wait_ge(w_ready, 1)
                with pe.Fori(0, GROUPS) as g:
                    for u in range(U):
                        i = g * U + u
                        pe.wait_ge(normed, i + 1)
                        if u >= 2:
                            pe.wait_ge(turned_copied, i - 1)
                        else:
                            pe.wait_ge(turned_copied, g * U)
                        for c in range(KC):
                            last = nc.tensor.transpose(k.ps[:, u % 2, bass.ts(c, P)], xn[:, u, bass.ts(c, P)],
                                                       k.ident[:])
                        last.then_inc(turned, 1)
                    for u in range(U):
                        i = g * U + u
                        bank = 2 + 2 * (u % 2)
                        pe.wait_ge(turned_copied, i + 1)
                        if u >= 2:
                            pe.wait_ge(added, i - 1)
                        else:
                            pe.wait_ge(added, g * U)
                        for c in range(KC):
                            nc.tensor.matmul(k.ps[:, bank, :], xt[:, u, bass.ts(c, P)], w_all[:, c, 0:2 * D],
                                             start=c == 0, stop=c == KC - 1)
                        for c in range(KC):
                            last = nc.tensor.matmul(k.ps[:, bank + 1, 0:2 * H1], xt[:, u, bass.ts(c, P)],
                                                    w_all[:, c, 2 * D:], start=c == 0, stop=c == KC - 1)
                        last.then_inc(product, 1)


def gat_scores(k):
    nc, t = k.nc, k.t
    ctx, sb, sem = phase(k)
    W = 14
    with ctx:
        el = sb("el", [P, EC * H1])
        fwd, bwd = sb("fwd", [P, EC * H1]), sb("bwd", [P, EC * H1])
        rec = sb("rec", [P, EC * RW], I32)
        cut = sb("cut", [P, EC + 1])
        index, got = sb("index", [P, 2, W], I32), sb("got", [P, 2, W, H1])
        ends = sb("ends", [P, 4, H1])
        turned = sb("turned", [H1, 4, P])
        line = sb("line", [H1, 6, P])
        carry = sb("carry", [P, 2, H1])
        staged, unloaded, step_sem, started = sem("staged"), sem("unloaded"), sem("step"), sem("started")
        landed = [sem("landed0"), sem("landed1")]
        ends_ready, ends_turned, line_ready, line_turned = (
            sem(s) for s in ("ends_ready", "ends_turned", "line_ready", "line_turned"))
        rec_ready, stored = sem("rec_ready"), sem("stored")

        with nc.Block() as block:
            @block.gpsimd
            def _(pool):
                with pool.Fori(0, EC // W // 2) as g:
                    for s in range(2):
                        c = 2 * g + s
                        pool.wait_ge(unloaded, c + 1)
                        nc.gpsimd.tensor_copy(index[:, s, :], k.src_i[:, bass.ts(c, W)]).then_inc(staged, 1)
                        pool.wait_ge(staged, c + 1)
                        pool.sem_inc(started, 1)
                        for j in range(W):
                            nc.gpsimd.indirect_dma_start(
                                got[:, s, j, :], None, t["el_rows"][:, :],
                                bass.IndirectOffsetOnAxis(ap=index[:, s, j:j + 1], axis=0)).then_inc(landed[s], 16)

            @block.scalar
            def _(act):
                act.sem_inc(unloaded, 2)
                with act.Fori(0, EC // W // 2) as g:
                    for s in range(2):
                        c = 2 * g + s
                        act.wait_ge(landed[s], 16 * W * (g + 1))
                        nc.scalar.copy(el[:, bass.ts(c, W * H1)],
                                       got[:, s, :, :].rearrange("p j h -> p (j h)")).then_inc(unloaded, 1)
                act.wait_ge(unloaded, 2 + EC // W)
                nc.scalar.copy(rec[:].rearrange("p (j c) -> p j c", c=RW)[:, :, 2:2 + H1].bitcast(F32),
                               el[:].rearrange("p (j h) -> p j h", h=H1)).then_inc(rec_ready, 1)

            @block.vector
            def _(dve):
                step = Steps(dve, step_sem)
                rec3 = rec[:].rearrange("p (j c) -> p j c", c=RW)
                nc.vector.tensor_copy(rec3[:, :, 0], k.src_i[:]).then_inc(rec_ready, 1)
                nc.vector.tensor_copy(rec3[:, :, 1].bitcast(F32), k.dst_f[:]).then_inc(rec_ready, 1)
                step(nc.vector.memset(cut[:], 0.0))
                step(nc.vector.tensor_tensor(cut[:, 1:EC], k.dst_f[:, 1:EC], k.dst_f[:, 0:EC - 1], ALU.is_equal))
                step(nc.vector.tensor_scalar(cut[:], cut[:], -1.0, BIG, ALU.add, ALU.mult))
                for n, j in ((2, 0), (3, EC - 1)):
                    step(nc.vector.tensor_scalar(ends[:, n, :], k.ones[:, 0:H1], k.dst_f[:, j:j + 1], None, ALU.mult))
                dve.wait_ge(unloaded, 2 + EC // W)
                f3, b3, e3 = (a[:].rearrange("p (j h) -> p j h", h=H1) for a in (fwd, bwd, el))

                def scans(first, second):
                    for h in range(H1):
                        nc.vector.tensor_tensor_scan(f3[:, :, h], cut[:, 0:EC], e3[:, :, h], first(h), ALU.add, ALU.max)
                        last = nc.vector.tensor_tensor_scan(b3[:, ::-1, h], cut[:, 1:EC + 1][:, ::-1],
                                                            e3[:, ::-1, h], second(h), ALU.add, ALU.max)
                    step(last)

                scans(lambda h: -BIG, lambda h: -BIG)
                nc.vector.tensor_copy(ends[:, 0, :], f3[:, EC - 1, :])
                nc.vector.tensor_copy(ends[:, 1, :], b3[:, 0, :]).then_inc(ends_ready, 1)
                dve.wait_ge(ends_turned, 1)
                step(nc.vector.tensor_copy(turned[:], k.ps[0:H1, 0:4, 0:P]))
                tail, head, first, final = (turned[:, n, :] for n in range(4))
                linked, reach, back, run, cin, cout = (line[:, n, :] for n in range(6))
                step(nc.vector.memset(line[:], 0.0))
                step(nc.vector.tensor_tensor(linked[:, 1:P], final[:, 0:P - 1], first[:, 1:P], ALU.is_equal))
                step(nc.vector.tensor_tensor(run, first, final, ALU.is_equal))
                step(nc.vector.tensor_tensor(reach, run, linked, ALU.mult))
                step(nc.vector.tensor_tensor(back[:, 0:P - 1], run[:, 0:P - 1], linked[:, 1:P], ALU.mult))
                step(nc.vector.tensor_scalar(line[:, 0:3, :], line[:, 0:3, :], -1.0, BIG, ALU.add, ALU.mult))
                step(nc.vector.tensor_tensor_scan(run, reach, tail, -BIG, ALU.add, ALU.max))
                step(nc.vector.memset(cin, -BIG))
                step(nc.vector.tensor_tensor(cin[:, 1:P], run[:, 0:P - 1], linked[:, 1:P], ALU.add))
                step(nc.vector.tensor_tensor_scan(run[:, ::-1], back[:, ::-1], head[:, ::-1], -BIG, ALU.add, ALU.max))
                step(nc.vector.memset(cout, -BIG))
                nc.vector.tensor_tensor(cout[:, 0:P - 1], run[:, 1:P], linked[:, 1:P], ALU.add).then_inc(line_ready, 1)
                dve.wait_ge(line_turned, 1)
                step(nc.vector.tensor_copy(carry[:], k.ps[:, 4:6, 0:H1]))
                step(nc.vector.memset(cut[:, 0:1], 0.0))
                step(nc.vector.memset(cut[:, EC:EC + 1], 0.0))
                scans(lambda h: carry[:, 0, h:h + 1], lambda h: carry[:, 1, h:h + 1])
                nc.vector.tensor_tensor(rec3[:, :, 2 + H1:].bitcast(F32), f3, b3, ALU.max).then_inc(rec_ready, 1)

            @block.tensor
            def _(pe):
                pe.wait_ge(ends_ready, 1)
                for n in range(4):
                    last = nc.tensor.transpose(k.ps[0:H1, n, 0:P], ends[:, n, :], k.ident[:])
                last.then_inc(ends_turned, 1)
                pe.wait_ge(line_ready, 1)
                for n in range(2):
                    last = nc.tensor.transpose(k.ps[:, 4 + n, 0:H1], line[:, 4 + n, :], k.ident[0:H1, 0:H1])
                last.then_inc(line_turned, 1)

            @block.sync
            def _(sp):
                sp.wait_ge(rec_ready, 4)
                sp.dma_start(t["rec_gat"][0:EP, :].rearrange("(p j) c -> p (j c)", p=P), rec[:]).then_inc(stored, 16)
                sp.wait_ge(stored, 16)


BATCH = 4
BSETS = 4
SLOTS = BATCH * BSETS
BODIES = ST // SLOTS
assert BODIES * SLOTS == ST and BODIES > 2


def bodies(engine, body):
    body(0, True, False)
    with engine.Fori(1, BODIES - 1) as g:
        body(g, False, False)
    body(BODIES - 1, False, True)


def gat_edges(k):
    nc, t = k.nc, k.t
    ctx, sb, sem = phase(k)
    W = D + H1
    with ctx:
        acc = sb("acc", [P, NT * W])
        rec, rows = sb("rec", [P, SLOTS, RW], I32), sb("rows", [P, SLOTS, D])
        hot, hot_t = sb("hot", [P, SLOTS, P]), sb("hot_t", [P, 2, BATCH, P])
        score = sb("score", [P, 2, BATCH, 2, H1])
        msg = sb("msg", [P, BSETS, BATCH, W])
        bias, top = sb("bias", [P, D]), sb("top", [P, 2, D])
        den = sb("den", [P, NT * H1])
        rec_landed = [sem(f"rec_landed{s}") for s in range(SLOTS)]
        row_landed = [sem(f"row_landed{s}") for s in range(SLOTS)]
        started, loaded, step_sem = sem("started"), sem("loaded"), sem("step")
        hot_made, hot_turned, hot_copied, expanded, scored, shifted, raised, weighted, exp_done, multiplied, added = (
            sem(s) for s in ("hot_made", "hot_turned", "hot_copied", "expanded", "scored", "shifted", "raised",
                             "weighted", "exp_done", "multiplied", "added"))

        with nc.Block() as block:
            @block.sync
            def _(sp):
                sp.dma_start(bias[:], across(t["gat_bias"])).then_inc(loaded, 16)
                with sp.Fori(0, BODIES) as g:
                    for half in range(2):
                        _, start = nc.values_load_multi_w_load_instructions(
                            k.start_dst[0:1, bass.ds(g * SLOTS + half * 8, 8)], engines=(SP,), min_val=0, max_val=EP)
                        for n in range(8):
                            s = half * 8 + n
                            sp.wait_ge(weighted, g * SLOTS + s + 1)
                            sp.dma_start(rec[:, s, :], t["rec_gat"][bass.ds(start[n], P), :]).then_inc(rec_landed[s], 16)

            @block.gpsimd
            def _(pool):
                with pool.Fori(0, BODIES) as g:
                    for s in range(SLOTS):
                        pool.wait_ge(rec_landed[s], 16 * (g + 1))
                        pool.sem_inc(started, 1)
                        nc.gpsimd.indirect_dma_start(
                            rows[:, s, :], None, t["gat_rows"][:, :],
                            bass.IndirectOffsetOnAxis(ap=rec[:, s, 0:1], axis=0)).then_inc(row_landed[s], 16)

            @block.vector
            def _(dve):
                step = Steps(dve, step_sem)
                dve.sem_inc(weighted, SLOTS)
                step(nc.vector.memset(acc[:], 0.0))

                def one_hot(g, c, n):
                    s = c * BATCH + n
                    q = g * SLOTS + s
                    if not (isinstance(g, int) and g == 0):
                        dve.wait_ge(multiplied, q - SLOTS + 1)
                    dve.wait_ge(rec_landed[s], 16 * (g + 1))
                    nc.vector.tensor_scalar(hot[:, s, :], k.iota[:], k.base_dst[:, bass.ds(q, 1)],
                                            rec[:, s, 1:2].bitcast(F32), ALU.add, ALU.is_equal).then_inc(hot_made, 1)

                def scores(g, c, part):
                    B = g * BSETS + c
                    now, s0 = score[:, c % 2], c * BATCH
                    if part == 0:
                        dve.wait_ge(expanded, B + 1)
                        nc.vector.tensor_tensor(
                            now, rec[:, s0:s0 + BATCH, 2:].bitcast(F32).rearrange("p a (b h) -> p a b h", h=H1),
                            k.ps[:, 2 + c % 2, 0:BATCH * H1].rearrange(
                                "p (a h) -> p a h", h=H1).unsqueeze(2).to_broadcast([P, BATCH, 2, H1]),
                            ALU.add).then_inc(scored, 1)
                    elif part == 1:
                        dve.wait_ge(scored, B + 1)
                        nc.vector.scalar_tensor_tensor(out=now, in0=now, scalar=0.2, in1=now, op0=ALU.mult,
                                                       op1=ALU.max).then_inc(raised, 1)
                    elif part == 2:
                        dve.wait_ge(raised, B + 1)
                        nc.vector.tensor_tensor(now[:, :, 0, :], now[:, :, 0, :], now[:, :, 1, :],
                                                ALU.subtract).then_inc(shifted, 1)

                def weigh_row(g, c, n):
                    s = c * BATCH + n
                    if n == 0:
                        dve.wait_ge(exp_done, g * BSETS + c + 1)
                    dve.wait_ge(row_landed[s], 16 * (g + 1))
                    nc.vector.tensor_tensor(
                        msg[:, c, n, 0:D].rearrange("p (h d) -> p h d", d=HD),
                        rows[:, s, :].rearrange("p (h d) -> p h d", d=HD),
                        msg[:, c, n, D:].unsqueeze(2).to_broadcast([P, H1, HD]), ALU.mult).then_inc(weighted, 1)

                def add_sum(g, c, n, tile):
                    q = g * SLOTS + c * BATCH + n
                    dve.wait_ge(multiplied, q + 1)
                    dve.wait_ge(added, q)
                    sums = acc[:, bass.ds(tile[n] * W, W)]
                    nc.vector.tensor_tensor(sums, sums, k.ps[:, 4 + n, 0:W], ALU.add).then_inc(added, 1)

                def tiles(q):
                    return nc.values_load_multi_w_load_instructions(
                        k.tile_dst[0:1, bass.ds(q, BATCH)], engines=(DVE,), min_val=0, max_val=NT - 1)[1]

                def body(g, first, last):
                    if first:
                        for c in range(2):
                            for n in range(BATCH):
                                one_hot(0, c, n)
                        for part in range(3):
                            scores(0, 0, part)
                    for c in range(BSETS):
                        before = (g, c - 2) if c >= 2 else None if first else (g - 1, c + 2)
                        ahead = (g, c + 2) if c < 2 else None if last else (g + 1, c - 2)
                        if before:
                            tile = tiles(before[0] * SLOTS + before[1] * BATCH)
                        for n in range(BATCH):
                            if before:
                                add_sum(*before, n, tile)
                            if ahead:
                                one_hot(*ahead, n)
                        scored_next = (g, c + 1) if c < BSETS - 1 else None if last else (g + 1, 0)
                        for n in range(BATCH):
                            if scored_next:
                                scores(*scored_next, n)
                            weigh_row(g, c, n)
                    if last:
                        for c in (BSETS - 2, BSETS - 1):
                            tile = tiles(g * SLOTS + c * BATCH)
                            for n in range(BATCH):
                                add_sum(g, c, n, tile)

                bodies(dve, body)
                dve.wait_ge(added, ST)
                dve.wait_ge(loaded, 16)
                acc3 = acc[:].rearrange("p (i c) -> p i c", c=W)
                den3 = den[:].rearrange("p (i h) -> p i h", h=H1)
                step(nc.vector.tensor_scalar(den3, acc3[:, :, D:], 1e-30, None, ALU.max))
                step(nc.vector.reciprocal(den[:], den[:]))
                base = step.n
                for i in range(NT):
                    a, xsl, y = acc3[:, i, 0:D], k.xs[:, bass.ts(i, D)], top[:, i % 2, :]
                    step(nc.vector.tensor_tensor(
                        a.rearrange("p (h d) -> p h d", d=HD), a.rearrange("p (h d) -> p h d", d=HD),
                        den3[:, i, :].unsqueeze(2).to_broadcast([P, H1, HD]), ALU.mult))
                    step(nc.vector.tensor_tensor(a, a, bias[:], ALU.add))
                    step(nc.vector.scalar_tensor_tensor(out=y, in0=a, scalar=0.01, in1=a, op0=ALU.mult, op1=ALU.max))
                    step(nc.vector.tensor_tensor(xsl, xsl, y, ALU.add))

            @block.scalar
            def _(act):
                def copy_turned(g, c):
                    B = g * BSETS + c
                    act.wait_ge(hot_turned, B + 1)
                    if not (isinstance(g, int) and g == 0 and c < 2):
                        act.wait_ge(expanded, B - 1)
                    nc.scalar.copy(hot_t[:, c % 2, :, :], k.ps[:, c % 2, :].rearrange(
                        "p (a b) -> p a b", b=P)).then_inc(hot_copied, 1)

                def weights(g, c):
                    B = g * BSETS + c
                    act.wait_ge(shifted, B + 1)
                    if not (isinstance(g, int) and g == 0):
                        act.wait_ge(multiplied, (B - BSETS + 1) * BATCH)
                    nc.scalar.activation(msg[:, c, :, D:], score[:, c % 2, :, 0, :], ACT.Exp).then_inc(exp_done, 1)

                def body(g, first, last):
                    if first:
                        copy_turned(0, 0)
                        copy_turned(0, 1)
                        weights(0, 0)
                    for c in range(BSETS):
                        if c < BSETS - 2:
                            copy_turned(g, c + 2)
                        elif not last:
                            copy_turned(g + 1, c + 2 - BSETS)
                        if c < BSETS - 1:
                            weights(g, c + 1)
                        elif not last:
                            weights(g + 1, 0)

                bodies(act, body)

            @block.tensor
            def _(pe):
                def turn(g, c):
                    B = g * BSETS + c
                    pe.wait_ge(hot_made, (B + 1) * BATCH)
                    if not (isinstance(g, int) and g == 0 and c < 2):
                        pe.wait_ge(hot_copied, B - 1)
                    for n in range(BATCH):
                        last = nc.tensor.transpose(k.ps[:, c % 2, bass.ts(n, P)], hot[:, c * BATCH + n, :], k.ident[:])
                    last.then_inc(hot_turned, 1)

                def expand(g, c, tile):
                    B = g * BSETS + c
                    pe.wait_ge(hot_copied, B + 1)
                    if not (isinstance(g, int) and g == 0 and c < 2):
                        pe.wait_ge(scored, B - 1)
                    for n in range(BATCH):
                        last = nc.tensor.matmul(k.ps[:, 2 + c % 2, bass.ts(n, H1)], hot_t[:, c % 2, n, :],
                                                k.er[:, bass.ds(tile[n] * H1, H1)], start=True, stop=True)
                    last.then_inc(expanded, 1)

                def multiply(g, c):
                    B = g * BSETS + c
                    pe.wait_ge(weighted, (B + 1) * BATCH + SLOTS)
                    for n in range(BATCH):
                        if not (isinstance(g, int) and g == 0 and c == 0):
                            pe.wait_ge(added, (B - 1) * BATCH + n + 1)
                        nc.tensor.matmul(k.ps[:, 4 + n, 0:W], hot[:, c * BATCH + n, :], msg[:, c, n, :],
                                         start=True, stop=True).then_inc(multiplied, 1)

                def tiles(q):
                    return nc.values_load_multi_w_load_instructions(
                        k.tile_dst[0:1, bass.ds(q, BATCH)], engines=(PE,), min_val=0, max_val=NT - 1)[1]

                def body(g, first, last):
                    if first:
                        turn(0, 0)
                        turn(0, 1)
                        expand(0, 0, tiles(0))
                    for c in range(BSETS):
                        if c < BSETS - 1:
                            expand(g, c + 1, tiles(g * SLOTS + (c + 1) * BATCH))
                        elif not last:
                            expand(g + 1, 0, tiles(g * SLOTS + SLOTS))
                        if c < BSETS - 2:
                            turn(g, c + 2)
                        elif not last:
                            turn(g + 1, c + 2 - BSETS)
                        if c:
                            multiply(g, c - 1)
                        elif not first:
                            multiply(g - 1, BSETS - 1)
                    if last:
                        multiply(g, BSETS - 1)

                bodies(pe, body)


def slice_attention(k):
    nc, t = k.nc, k.t
    ctx, sb, sem = phase(k)
    PD = 2 * SD
    with ctx:
        w_fx, w_sl = sb("w_fx", [P, KC, SI]), sb("w_sl", [P, KC, SI])
        w_x_t = sb("w_x_t", [SD, SH, D])
        w_slice, b_x = sb("w_slice", [SD, SD]), sb("b_x", [SD, SH])
        w_two = [sb(f"w_{n}2", [PD, PD]) for n in ("q", "k", "v")]
        w_out, fold = sb("w_out", [PD, PAIRS, D]), sb("fold", [PD, PAIRS, D])
        b_fx, b_out, b_sl = sb("b_fx", [P, SI]), sb("b_out", [P, D]), sb("b_sl", [P, SI])
        b_slice = sb("b_slice", [SH, SD])
        sl_row = sb("sl_row", [SH, SD])
        temp = sb("temp", [P, SH])
        st, mv = sb("st", [P, NT * 6]), sb("mv", [P, 5, NT])
        xn, xt = sb("xn", [P, 4, D]), sb("xt", [P, 4, D])
        soft, fx = sb("soft", [P, 4, SI]), sb("fx", [P, 4, PAIRS, PD + 1])
        peak, total = sb("peak", [P, 4, SH]), sb("total", [P, 4, SH])
        soft_t = k.large[:, 0:PAIRS * NP].rearrange("p (a n) -> p a n", n=NP)
        piece = sb("piece", [P, U, SI])
        zero = sb("zero", [1, 2 * (PD + 1)])
        token, norm = sb("token", [PD, PAIRS, PD]), sb("norm", [PD, PAIRS])
        token_t, q_t, k_t, v = (sb(n, [PD, PAIRS, PD]) for n in ("token_t", "q_t", "k_t", "v"))
        att, att_t, mix_t = (sb(n, [PD, PAIRS, PD]) for n in ("att", "att_t", "mix_t"))
        high, mass = sb("high", [PD, PAIRS]), sb("mass", [PD, PAIRS])
        sender = Sender(k, sb, sem)
        S = {n: sem(n) for n in (
            "loaded", "zeroed", "dve_step", "act_step", "stats_ready", "sqrt_ready", "fused", "copied", "bias_out",
            "bias_in", "w_ready", "normed", "turned", "turned_copied", "product", "scored", "raised", "weighed",
            "tokens", "soft_turned", "soft_kept", "fixed", "mid_pe", "mid_dve", "mid_act", "cut", "result",
            "added", "peaked", "summed")}
        HALVES = ((0, SD), (SD, PD))

        with nc.Block() as block:
            @block.sync
            def _(sp):
                n = load_weights(k, sp, S["loaded"], [
                    (w_fx[:], chunks(t["w_fx"])), (w_x_t[:], t["w_x_t"].rearrange("(h c) n -> c h n", c=SD)),
                    (w_slice[:], t["w_slice"]), (b_x[:], t["b_x_cols"]), (w_out[:], chunks(t["w_out"])),
                    (b_fx[:], across(t["b_fx"])), (b_out[:], across(t["b_out"])),
                    (b_slice[:], row(t["b_slice"]).to_broadcast([SH, SD])), (temp[:], across(t["temp"]))])
                sp.wait_ge(S["zeroed"], 4)
                for w2, w in zip(w_two, (t["w_q"], t["w_k"], t["w_v"])):
                    for a, b in HALVES:
                        sp.dma_start(w2[a:b, a:b], w).then_inc(S["loaded"], 16)
                sp.wait_ge(S["copied"], 1)
                sp.dma_start(t["slice_bias"], sl_row[:]).then_inc(S["bias_out"], 16)
                sp.wait_ge(S["bias_out"], 16)
                sp.dma_start(b_sl[:], row(t["slice_bias"].rearrange("h g -> (h g)")).to_broadcast(
                    [P, SI])).then_inc(S["bias_in"], 16)

            @block.gpsimd
            def _(pool):
                for w2 in w_two:
                    nc.gpsimd.memset(w2[:], 0.0).then_inc(S["zeroed"], 1)
                nc.gpsimd.memset(zero[:], 0.0).then_inc(S["zeroed"], 1)
                send_edges(pool, sender, *SENT_BY_SLICES)

            @block.vector
            def _(dve):
                step = Steps(dve, S["dve_step"])
                emit_norm(k, dve, st, mv, S["stats_ready"], S["sqrt_ready"], step)
                dve.wait_ge(S["loaded"], 16 * 15)
                step(nc.vector.tensor_scalar(temp[:], temp[:], 0.1, 5.0, ALU.max, ALU.min))
                step(nc.vector.reciprocal(temp[:], temp[:]))
                dve.wait_ge(S["fused"], 1)
                nc.vector.tensor_tensor(sl_row[:], k.ps[0:SH, 2, 0:SD], b_slice[:], ALU.add).then_inc(S["copied"], 1)
                for c in range(KC):
                    last = nc.vector.tensor_tensor(
                        w_sl[:, c, :].rearrange("p (h g) -> p h g", g=SD),
                        k.ps[:, c, :].rearrange("p (h g) -> p h g", g=SD),
                        temp[:].unsqueeze(2).to_broadcast([P, SH, SD]), ALU.mult)
                last.then_inc(S["w_ready"], 1)
                nc.vector.memset(fx[:, :, :, PD:], 1.0).then_inc(S["fixed"], 1)
                nc.vector.memset(token[:], 0.0).then_inc(S["fixed"], 1)
                nc.vector.memset(att[:], 0.0).then_inc(S["fixed"], 1)
                dve.wait_ge(S["fixed"], 3)
                dve.wait_ge(S["bias_in"], 16)
                step(nc.vector.tensor_tensor(
                    b_sl[:].rearrange("p (h g) -> p h g", g=SD), b_sl[:].rearrange("p (h g) -> p h g", g=SD),
                    temp[:].unsqueeze(2).to_broadcast([P, SH, SD]), ALU.mult))

                def norm_row(i, o):
                    if not isinstance(i, int) or i >= 4:
                        dve.wait_ge(S["turned"], i - 3)
                    nc.vector.tensor_scalar(xn[:, o, :], k.xs[:, bass.ts(i, D)], mv[:, 0, bass.ds(i, 1)],
                                            mv[:, 4, bass.ds(i, 1)], ALU.subtract, ALU.mult).then_inc(S["normed"], 1)

                def raise_scores(i, o):
                    s3, bank = soft[:, o, :].rearrange("p (h g) -> p h g", g=SD), 2 + o % 2 * 4
                    dve.wait_ge(S["product"], i + 1)
                    if not isinstance(i, int) or i >= 4:
                        dve.wait_ge(S["tokens"], i - 3)
                    nc.vector.tensor_tensor(soft[:, o, :], k.ps[:, bank + 1, :], b_sl[:], ALU.add).then_inc(S["peaked"], 1)
                    nc.vector.tensor_tensor(fx[:, o, :, 0:PD],
                                            k.ps[:, bank, :].rearrange("p (a b) -> p a b", b=PD),
                                            b_fx[:].rearrange("p (a b) -> p a b", b=PD), ALU.add).then_inc(S["scored"], 1)
                    dve.wait_ge(S["peaked"], 2 * i + 1)
                    nc.vector.tensor_reduce(peak[:, o, :], s3, AX, ALU.max).then_inc(S["peaked"], 1)
                    dve.wait_ge(S["peaked"], 2 * i + 2)
                    nc.vector.tensor_tensor(s3, s3, peak[:, o, :].unsqueeze(2).to_broadcast([P, SH, SD]),
                                            ALU.subtract).then_inc(S["raised"], 1)

                def divide(i, o):
                    s3 = soft[:, o, :].rearrange("p (h g) -> p h g", g=SD)
                    dve.wait_ge(S["weighed"], i + 1)
                    nc.vector.tensor_reduce(total[:, o, :], s3, AX, ALU.add).then_inc(S["summed"], 1)
                    dve.wait_ge(S["summed"], 2 * i + 1)
                    nc.vector.reciprocal(total[:, o, :], total[:, o, :]).then_inc(S["summed"], 1)
                    dve.wait_ge(S["summed"], 2 * i + 2)
                    nc.vector.scalar_tensor_tensor(
                        out=s3, in0=s3, scalar=k.mask[:, bass.ds(i, 1)],
                        in1=total[:, o, :].unsqueeze(2).to_broadcast([P, SH, SD]),
                        op0=ALU.mult, op1=ALU.mult).then_inc(S["cut"], 1)

                staggered(dve, [(norm_row, 0), (divide, 3), (raise_scores, 2)])
                step = Steps(dve, S["mid_dve"])
                dve.wait_ge(S["tokens"], NT)
                sums = k.ps[:, 4:6, 0:2 * (PD + 1)].rearrange("p b (r c) -> p b r c", c=PD + 1)
                step(nc.vector.tensor_scalar(norm[:].rearrange("p (b r) -> p b r", r=2), sums[:, :, :, PD], 1e-5, None,
                                             ALU.add))
                step(nc.vector.reciprocal(norm[:], norm[:]))
                for r in range(PAIRS):
                    for a, b in HALVES:
                        last = nc.vector.tensor_scalar(token[a:b, r, a:b], sums[a:b, r // 2, r % 2, a:b],
                                                       norm[a:b, r:r + 1], None, ALU.mult)
                step(last)

                def leave(n, out, bank):
                    dve.wait_ge(S["mid_pe"], n)
                    step(nc.vector.tensor_copy(out[:].rearrange("p a b -> p (a b)"), k.ps[:, bank, :]))

                leave(1, token_t, 0)
                dve.wait_ge(S["mid_pe"], 2)
                for out, bank in ((q_t, 1), (k_t, 2), (v, 3)):
                    step(nc.vector.tensor_copy(out[:].rearrange("p a b -> p (a b)"), k.ps[:, bank, :]))
                dve.wait_ge(S["mid_pe"], 3)
                scale = float(SD) ** -0.5
                for a, b in HALVES:
                    last = nc.vector.tensor_reduce(high[a:b, :], k.ps[a:b, 0, :].rearrange(
                        "p (r c) -> p r c", c=PD)[:, :, a:b], AX, ALU.max)
                step(last)
                for a, b in HALVES:
                    last = nc.vector.tensor_tensor(
                        att[a:b, :, a:b], k.ps[a:b, 0, :].rearrange("p (r c) -> p r c", c=PD)[:, :, a:b],
                        high[a:b, :].unsqueeze(2).to_broadcast([SD, PAIRS, SD]), ALU.subtract)
                step(last)
                dve.wait_ge(S["mid_act"], 1)
                for a, b in HALVES:
                    last = nc.vector.tensor_reduce(mass[a:b, :], att[a:b, :, a:b], AX, ALU.add)
                step(last)
                step(nc.vector.reciprocal(mass[:], mass[:]))
                step(nc.vector.tensor_tensor(att[:], att[:], mass[:].unsqueeze(2).to_broadcast([PD, PAIRS, PD]),
                                             ALU.mult))
                leave(4, att_t, 1)
                leave(5, mix_t, 2)
                dve.wait_ge(S["mid_pe"], 6)
                step(nc.vector.tensor_copy(fold[:, 0:2, :].rearrange("p a b -> p (a b)"), k.ps[:, 4, :]))
                step(nc.vector.tensor_copy(fold[:, 2:4, :].rearrange("p a b -> p (a b)"), k.ps[:, 5, :]))
                with dve.Fori(0, GROUPS) as g:
                    for u in range(U):
                        i = g * U + u
                        dve.wait_ge(S["result"], i + 1)
                        xsl = k.xs[:, bass.ts(i, D)]
                        nc.vector.tensor_tensor(xsl, xsl, k.ps[:, u % 2, 0:D], ALU.add).then_inc(S["cut"], 1)
                        dve.wait_ge(S["cut"], NT + i + 1)
                        nc.vector.tensor_tensor(xsl, xsl, b_out[:], ALU.add).then_inc(S["added"], 1)

            @block.scalar
            def _(act):
                emit_sqrt(k, act, mv, S["stats_ready"], S["sqrt_ready"])

                def copy_turned(i, o):
                    act.wait_ge(S["turned"], i + 1)
                    if not isinstance(i, int) or i >= 4:
                        act.wait_ge(S["product"], i - 3)
                    nc.scalar.copy(xt[:, o, :], k.ps[:, 0, 0:D]).then_inc(S["turned_copied"], 1)

                def exponents(i, o):
                    act.wait_ge(S["raised"], i + 1)
                    nc.scalar.activation(soft[:, o, :], soft[:, o, :], ACT.Exp).then_inc(S["weighed"], 1)

                def keep_turned(i, o):
                    act.wait_ge(S["soft_turned"], i + 1)
                    nc.scalar.copy(soft_t[:, :, bass.ts(i, P)],
                                   k.ps[:, 1, :].rearrange("p (a b) -> p a b", b=P)).then_inc(S["soft_kept"], 1)

                staggered(act, [(keep_turned, 4), (copy_turned, 0), (exponents, 2)])
                act.wait_ge(S["mid_dve"], 9)
                for a, b in HALVES:
                    last = nc.scalar.activation(att[a:b, :, a:b], att[a:b, :, a:b], ACT.Exp, scale=float(SD) ** -0.5)
                last.then_inc(S["mid_act"], 1)
                act.wait_ge(S["soft_kept"], NT)
                with act.Fori(0, GROUPS) as g:
                    for u in range(U):
                        i = g * U + u
                        act.wait_ge(S["result"], g * U)
                        nc.scalar.copy(piece[:, u, :].rearrange("p (a b) -> p a b", b=P),
                                       soft_t[:, :, bass.ts(i, P)]).then_inc(S["act_step"], 1)

            @block.tensor
            def _(pe):
                pe.wait_ge(S["loaded"], 16 * 15)
                pe.wait_ge(S["zeroed"], 4)
                for c in range(KC):
                    for h in range(SH):
                        nc.tensor.matmul(k.ps[:, c, bass.ts(h, SD)], w_x_t[:, h, bass.ts(c, P)], w_slice[:],
                                         start=True, stop=True)
                nc.tensor.matmul(k.ps[0:SH, 2, 0:SD], b_x[:], w_slice[:], start=True, stop=True).then_inc(S["fused"], 1)
                pe.wait_ge(S["w_ready"], 1)
                for b in range(2):
                    nc.tensor.matmul(k.ps[:, 4 + b, 0:2 * (PD + 1)], k.ones[0:1, :], zero[:], start=True, stop=False,
                                     skip_group_check=True)

                def turn(i, o):
                    pe.wait_ge(S["normed"], i + 1)
                    if not isinstance(i, int) or i >= 1:
                        pe.wait_ge(S["turned_copied"], i)
                    for c in range(KC):
                        last = nc.tensor.transpose(k.ps[:, 0, bass.ts(c, P)], xn[:, o, bass.ts(c, P)], k.ident[:])
                    last.then_inc(S["turned"], 1)

                def project(i, o):
                    bank = 2 + o % 2 * 4
                    pe.wait_ge(S["turned_copied"], i + 1)
                    if not isinstance(i, int) or i >= 2:
                        pe.wait_ge(S["scored"], i - 1)
                    for b, w in ((bank, w_fx), (bank + 1, w_sl)):
                        for c in range(KC):
                            last = nc.tensor.matmul(k.ps[:, b, :], xt[:, o, bass.ts(c, P)], w[:, c, :],
                                                    start=c == 0, stop=c == KC - 1)
                    last.then_inc(S["product"], 1)

                def sum_tokens(i, o):
                    pe.wait_ge(S["cut"], i + 1)
                    if not isinstance(i, int) or i >= 1:
                        pe.wait_ge(S["soft_kept"], i)
                    for r in range(PAIRS):
                        last = nc.tensor.transpose(k.ps[:, 1, bass.ts(r, P)], soft[:, o, bass.ts(r, P)], k.ident[:])
                    last.then_inc(S["soft_turned"], 1)
                    for r in range(PAIRS):
                        last = nc.tensor.matmul(k.ps[:, 4 + r // 2, bass.ts(r % 2, PD + 1)], soft[:, o, bass.ts(r, PD)],
                                                fx[:, o, r, :], start=False, stop=False, skip_group_check=True)
                    last.then_inc(S["tokens"], 1)

                staggered(pe, [(turn, 0), (project, 1), (sum_tokens, 3)])
                pe.wait_ge(S["soft_kept"], NT)
                pe.wait_ge(S["mid_dve"], 3)
                for r in range(PAIRS):
                    last = nc.tensor.transpose(k.ps[:, 0, bass.ts(r, PD)], token[:, r, :], k.ident[:])
                last.then_inc(S["mid_pe"], 1)
                pe.wait_ge(S["mid_dve"], 4)
                for r in range(PAIRS):
                    nc.tensor.matmul(k.ps[:, 1, bass.ts(r, PD)], w_two[0][:], token_t[:, r, :], start=True, stop=True)
                    nc.tensor.matmul(k.ps[:, 2, bass.ts(r, PD)], w_two[1][:], token_t[:, r, :], start=True, stop=True)
                    last = nc.tensor.matmul(k.ps[:, 3, bass.ts(r, PD)], token_t[:, r, :], w_two[2][:], start=True,
                                            stop=True)
                last.then_inc(S["mid_pe"], 1)
                pe.wait_ge(S["mid_dve"], 7)
                for r in range(PAIRS):
                    last = nc.tensor.matmul(k.ps[:, 0, bass.ts(r, PD)], q_t[:, r, :], k_t[:, r, :], start=True,
                                            stop=True)
                last.then_inc(S["mid_pe"], 1)
                pe.wait_ge(S["mid_dve"], 12)
                for r in range(PAIRS):
                    last = nc.tensor.transpose(k.ps[:, 1, bass.ts(r, PD)], att[:, r, :], k.ident[:])
                last.then_inc(S["mid_pe"], 1)
                pe.wait_ge(S["mid_dve"], 13)
                for r in range(PAIRS):
                    last = nc.tensor.matmul(k.ps[:, 2, bass.ts(r, PD)], v[:, r, :], att_t[:, r, :], start=True,
                                            stop=True)
                last.then_inc(S["mid_pe"], 1)
                pe.wait_ge(S["mid_dve"], 14)
                for r in range(PAIRS):
                    last = nc.tensor.matmul(k.ps[:, 4 + r // 2, bass.ts(r % 2, D)], mix_t[:, r, :], w_out[:, r, :],
                                            start=True, stop=True)
                last.then_inc(S["mid_pe"], 1)
                pe.wait_ge(S["mid_dve"], 16)
                with pe.Fori(0, GROUPS) as g:
                    for u in range(U):
                        i = g * U + u
                        pe.wait_ge(S["act_step"], i + 1)
                        pe.wait_ge(S["added"], i - 1 if u >= 2 else g * U)
                        for r in range(PAIRS):
                            last = nc.tensor.matmul(k.ps[:, u % 2, 0:D], piece[:, u, bass.ts(r, P)], fold[:, r, :],
                                                    start=r == 0, stop=r == PAIRS - 1)
                        last.then_inc(S["result"], 1)


def message_tables(k):
    nc, t = k.nc, k.t
    ctx, sb, sem = phase(k)
    with ctx:
        w, b1 = sb("w", [P, KC, 2 * D]), sb("b1", [P, D])
        st, mv = sb("st", [P, NT * 6]), sb("mv", [P, 5, NT])
        xn, xt, out = sb("xn", [P, U, D]), sb("xt", [P, U, D]), sb("out", [P, U, D])
        sender = Sender(k, sb, sem)
        loaded, dve_step, stats_ready, sqrt_ready = (sem(s) for s in ("loaded", "dve_step", "stats_ready", "sqrt_ready"))
        normed, turned, turned_copied, product, left = (
            sem(s) for s in ("normed", "turned", "turned_copied", "product", "left"))
        stored = [sem(f"stored{u}") for u in range(U)]

        with nc.Block() as block:
            @block.sync
            def _(sp):
                load_weights(k, sp, loaded, [(w[:, :, 0:D], chunks(t["w1_t"][0:D, :])),
                                             (w[:, :, D:], chunks(t["w1_t"][D:, :])), (b1[:], across(t["b1"]))])
                with sp.Fori(0, GROUPS) as g:
                    for u in range(U):
                        i = g * U + u
                        sp.wait_ge(left, i + 1)
                        sp.dma_start(t["msg_rows"][bass.ts(i, P), :], out[:, u, :]).then_inc(stored[u], 16)
                for u in range(U):
                    sp.wait_ge(stored[u], 16 * GROUPS)

            @block.gpsimd
            def _(pool):
                send_edges(pool, sender, *SENT_BY_MESSAGES)

            @block.vector
            def _(dve):
                step = Steps(dve, dve_step)
                emit_norm(k, dve, st, mv, stats_ready, sqrt_ready, step)
                dve.wait_ge(loaded, 48)
                with dve.Fori(0, GROUPS) as g:
                    for u in range(U):
                        i = g * U + u
                        dve.wait_ge(turned, i + 1)
                        nc.vector.tensor_scalar(xn[:, u, :], k.xs[:, bass.ts(i, D)], mv[:, 0, bass.ds(i, 1)],
                                                mv[:, 4, bass.ds(i, 1)], ALU.subtract, ALU.mult).then_inc(normed, 1)
                    for u in range(U):
                        i = g * U + u
                        dve.wait_ge(product, i + 1)
                        dve.wait_ge(stored[u], 16 * g)
                        nc.vector.tensor_tensor(k.source_part[:, bass.ts(i, D)], k.ps[:, 2 + u % 2, 0:D], b1[:], ALU.add)
                        nc.vector.tensor_copy(out[:, u, :], k.ps[:, 2 + u % 2, D:]).then_inc(left, 1)

            @block.scalar
            def _(act):
                emit_sqrt(k, act, mv, stats_ready, sqrt_ready)
                with act.Fori(0, GROUPS) as g:
                    for u in range(U):
                        i = g * U + u
                        act.wait_ge(turned, i + U + 1)
                        nc.scalar.copy(xt[:, u, :], k.ps[:, u % 2, 0:D]).then_inc(turned_copied, 1)

            @block.tensor
            def _(pe):
                pe.sem_inc(turned, U)
                pe.wait_ge(loaded, 48)
                with pe.Fori(0, GROUPS) as g:
                    for u in range(U):
                        i = g * U + u
                        pe.wait_ge(normed, i + 1)
                        pe.wait_ge(turned_copied, i - 1 if u >= 2 else g * U)
                        for c in range(KC):
                            last = nc.tensor.transpose(k.ps[:, u % 2, bass.ts(c, P)], xn[:, u, bass.ts(c, P)],
                                                       k.ident[:])
                        last.then_inc(turned, 1)
                    for u in range(U):
                        i = g * U + u
                        pe.wait_ge(turned_copied, i + 1)
                        pe.wait_ge(left, i - 1 if u >= 2 else g * U)
                        for c in range(KC):
                            last = nc.tensor.matmul(k.ps[:, 2 + u % 2, :], xt[:, u, bass.ts(c, P)], w[:, c, :],
                                                    start=c == 0, stop=c == KC - 1)
                        last.then_inc(product, 1)


def message_edges(k):
    nc, t = k.nc, k.t
    ctx, sb, sem = phase(k)
    W = D + 1
    with ctx:
        acc = k.sums
        rec, rows = sb("rec", [P, SLOTS, 2], I32), sb("rows", [P, SLOTS, D])
        hot, hot_t = sb("hot", [P, SLOTS, P]), sb("hot_t", [P, 2, BATCH, P])
        msg = sb("msg", [P, 2, BATCH, W])
        started = sem("started")
        rec_landed = [sem(f"rec_landed{s}") for s in range(SLOTS)]
        row_landed = [sem(f"row_landed{s}") for s in range(SLOTS)]
        hot_made, hot_turned, hot_copied, expanded, raised, silu_done, multiplied, added, prepared = (
            sem(s) for s in ("hot_made", "hot_turned", "hot_copied", "expanded", "raised", "silu_done", "multiplied",
                             "added", "prepared"))

        with nc.Block() as block:
            @block.sync
            def _(sp):
                with sp.Fori(0, BODIES) as g:
                    for half in range(2):
                        _, start = nc.values_load_multi_w_load_instructions(
                            k.start_src[0:1, bass.ds(g * SLOTS + half * 8, 8)], engines=(SP,), min_val=0, max_val=EP)
                        for n in range(8):
                            s = half * 8 + n
                            sp.wait_ge(raised, g * BSETS + s // BATCH + 1)
                            sp.dma_start(rec[:, s, :], t["rec_src"][bass.ds(start[n], P), :]).then_inc(rec_landed[s], 16)

            @block.gpsimd
            def _(pool):
                with pool.Fori(0, BODIES) as g:
                    for s in range(SLOTS):
                        pool.wait_ge(rec_landed[s], 16 * (g + 1))
                        pool.sem_inc(started, 1)
                        nc.gpsimd.indirect_dma_start(
                            rows[:, s, :], None, t["msg_rows"][:, :],
                            bass.IndirectOffsetOnAxis(ap=rec[:, s, 0:1], axis=0)).then_inc(row_landed[s], 16)

            @block.vector
            def _(dve):
                dve.sem_inc(raised, BSETS)
                nc.vector.memset(msg[:, :, :, D:], 1.0).then_inc(prepared, 1)
                nc.vector.memset(acc[:], 0.0).then_inc(prepared, 1)
                dve.wait_ge(prepared, 2)

                def one_hot(g, c, n):
                    s = c * BATCH + n
                    q = g * SLOTS + s
                    if not (isinstance(g, int) and g == 0):
                        dve.wait_ge(multiplied, q - SLOTS + 1)
                    dve.wait_ge(rec_landed[s], 16 * (g + 1))
                    nc.vector.tensor_scalar(hot[:, s, :], k.iota[:], k.base_src[:, bass.ds(q, 1)],
                                            rec[:, s, 1:2].bitcast(F32), ALU.add, ALU.is_equal).then_inc(hot_made, 1)

                def add_rows(g, c):
                    B = g * BSETS + c
                    dve.wait_ge(expanded, B + 1)
                    if not (isinstance(g, int) and g == 0 and c < 2):
                        dve.wait_ge(multiplied, (B - 1) * BATCH)
                    for h in range(2):
                        s0 = c * BATCH + 2 * h
                        for s in (s0, s0 + 1):
                            dve.wait_ge(row_landed[s], 16 * (g + 1))
                        last = nc.vector.tensor_tensor(
                            msg[:, c % 2, 2 * h:2 * h + 2, 0:D], k.ps[:, 2 + h, :].rearrange("p (a b) -> p a b", b=D),
                            rows[:, s0:s0 + 2, :], ALU.add)
                    last.then_inc(raised, 1)

                def add_sum(g, c, n, tile):
                    q = g * SLOTS + c * BATCH + n
                    dve.wait_ge(multiplied, q + 1)
                    dve.wait_ge(added, q)
                    sums = acc[:, bass.ds(tile[n] * W, W)]
                    nc.vector.tensor_tensor(sums, sums, k.ps[:, 4 + n, 0:W], ALU.add).then_inc(added, 1)

                def tiles(q):
                    return nc.values_load_multi_w_load_instructions(
                        k.tile_src[0:1, bass.ds(q, BATCH)], engines=(DVE,), min_val=0, max_val=NT - 1)[1]

                def body(g, first, last):
                    if first:
                        for c in range(2):
                            for n in range(BATCH):
                                one_hot(0, c, n)
                    for c in range(BSETS):
                        before = (g, c - 2) if c >= 2 else None if first else (g - 1, c + 2)
                        ahead = (g, c + 2) if c < 2 else None if last else (g + 1, c - 2)
                        if before:
                            tile = tiles(before[0] * SLOTS + before[1] * BATCH)
                        for n in range(BATCH):
                            if before:
                                add_sum(*before, n, tile)
                            if ahead:
                                one_hot(*ahead, n)
                        add_rows(g, c)
                    if last:
                        for c in (BSETS - 2, BSETS - 1):
                            tile = tiles(g * SLOTS + c * BATCH)
                            for n in range(BATCH):
                                add_sum(g, c, n, tile)

                bodies(dve, body)

            @block.scalar
            def _(act):
                def copy_turned(g, c):
                    B = g * BSETS + c
                    act.wait_ge(hot_turned, B + 1)
                    if not (isinstance(g, int) and g == 0 and c < 2):
                        act.wait_ge(expanded, B - 1)
                    nc.scalar.copy(hot_t[:, c % 2, :, :], k.ps[:, c % 2, :].rearrange(
                        "p (a b) -> p a b", b=P)).then_inc(hot_copied, 1)

                def body(g, first, last):
                    if first:
                        copy_turned(0, 0)
                    for c in range(BSETS):
                        if c < BSETS - 1:
                            copy_turned(g, c + 1)
                        elif not last:
                            copy_turned(g + 1, 0)
                        act.wait_ge(raised, g * BSETS + c + 1 + BSETS)
                        nc.scalar.activation(msg[:, c % 2, :, 0:D], msg[:, c % 2, :, 0:D],
                                             ACT.Silu).then_inc(silu_done, 1)

                bodies(act, body)

            @block.tensor
            def _(pe):
                pe.wait_ge(prepared, 1)

                def turn(g, c):
                    B = g * BSETS + c
                    pe.wait_ge(hot_made, (B + 1) * BATCH)
                    if not (isinstance(g, int) and g == 0 and c < 2):
                        pe.wait_ge(hot_copied, B - 1)
                    for n in range(BATCH):
                        last = nc.tensor.transpose(k.ps[:, c % 2, bass.ts(n, P)], hot[:, c * BATCH + n, :], k.ident[:])
                    last.then_inc(hot_turned, 1)

                def expand(g, c, tile):
                    B = g * BSETS + c
                    pe.wait_ge(hot_copied, B + 1)
                    pe.wait_ge(raised, B + BSETS)
                    for n in range(BATCH):
                        last = nc.tensor.matmul(k.ps[:, 2 + n // 2, bass.ts(n % 2, D)], hot_t[:, c % 2, n, :],
                                                k.source_part[:, bass.ds(tile[n] * D, D)], start=True, stop=True)
                    last.then_inc(expanded, 1)

                def multiply(g, c):
                    B = g * BSETS + c
                    pe.wait_ge(silu_done, B + 1)
                    for n in range(BATCH):
                        if not (isinstance(g, int) and g == 0 and c == 0):
                            pe.wait_ge(added, (B - 1) * BATCH + n + 1)
                        nc.tensor.matmul(k.ps[:, 4 + n, 0:W], hot[:, c * BATCH + n, :], msg[:, c % 2, n, :],
                                         start=True, stop=True).then_inc(multiplied, 1)

                def tiles(q):
                    return nc.values_load_multi_w_load_instructions(
                        k.tile_src[0:1, bass.ds(q, BATCH)], engines=(PE,), min_val=0, max_val=NT - 1)[1]

                def body(g, first, last):
                    if first:
                        turn(0, 0)
                    for c in range(BSETS):
                        expand(g, c, tiles(g * SLOTS + c * BATCH))
                        if c < BSETS - 1:
                            turn(g, c + 1)
                        elif not last:
                            turn(g + 1, 0)
                        if c:
                            multiply(g, c - 1)
                        elif not first:
                            multiply(g - 1, BSETS - 1)
                    if last:
                        multiply(g, BSETS - 1)

                bodies(pe, body)


def gated_update(k):
    nc, t = k.nc, k.t
    ctx, sb, sem = phase(k)
    W, G = D + 1, 3 * D
    with ctx:
        w_hh, w_ih = sb("w_hh", [P, KC, G]), sb("w_ih", [P, KC, G])
        w2, b2 = sb("w2", [P, KC, D]), sb("b2", [P, KC])
        w_in = sb("w_in", [P, KC, G])
        bias = sb("bias", [3, 4 * D])
        gamma, beta = sb("gamma", [P, D]), sb("beta", [P, D])
        inv, full = sb("inv", [P, NT]), sb("full", [P, NT])
        st, mv = sb("st", [P, NT * 6]), sb("mv", [P, 5, NT])
        both = sb("both", [P, 4, 2 * D + 3])
        both_t = sb("both_t", [P, 2, 4, P])
        ones_t = sb("ones_t", [3, 2, P])
        rz, new = sb("rz", [P, 2, 2 * D]), sb("new", [P, 2, D])
        nst = sb("nst", [P, 2, 6])
        names = ("loaded", "zeroed", "dve_step", "stats_ready", "sqrt_ready", "fused", "w_ready", "normed", "turned",
                 "turned_copied", "product", "gates", "candidate", "tanh_done", "chain", "tile_var", "tile_sqrt",
                 "finished")
        S = {n: sem(n) for n in names}
        sums3 = k.sums[:].rearrange("p (i c) -> p i c", c=W)
        outv = k.new_rows

        with nc.Block() as block:
            @block.sync
            def _(sp):
                sp.wait_ge(S["zeroed"], 1)
                load_weights(k, sp, S["loaded"], [
                    (w_hh[:], chunks(t["w_hh_t"])), (w_ih[:], chunks(t["w_ih_t"])), (w2[:], chunks(t["w2"])),
                    (b2[:], t["b2_cols"]), (gamma[:], across(t["gamma"])), (beta[:], across(t["beta"])),
                    (bias[1:2, 0:3 * D], row(t["b_ih"])), (bias[2:3, 0:2 * D], row(t["b_hh"][0:2 * D])),
                    (bias[2:3, 3 * D:], row(t["b_hh"][2 * D:]))])

            @block.gpsimd
            def _(pool):
                nc.gpsimd.memset(bias[:], 0.0).then_inc(S["zeroed"], 1)
                nc.gpsimd.memset(both[:, :, 2 * D + 1:], 1.0).then_inc(S["zeroed"], 1)

            @block.vector
            def _(dve):
                step = Steps(dve, S["dve_step"])
                emit_norm(k, dve, st, mv, S["stats_ready"], S["sqrt_ready"], step)
                step(nc.vector.tensor_scalar(inv[:], sums3[:, :, D], 1e-8, None, ALU.add))
                step(nc.vector.reciprocal(inv[:], inv[:]))
                step(nc.vector.tensor_tensor(full[:], sums3[:, :, D], inv[:], ALU.mult))
                dve.wait_ge(S["fused"], 1)
                for m in range(KC):
                    step(nc.vector.tensor_copy(w_in[:, m, 0:2 * D], k.ps[:, 2 * m, :]))
                    step(nc.vector.tensor_copy(w_in[:, m, 2 * D:], k.ps[:, 2 * m + 1, 0:D]))
                dve.wait_ge(S["loaded"], 16 * 9)
                step(nc.vector.tensor_copy(bias[0:1, 0:2 * D], k.ps[0:1, 4, :]))
                nc.vector.tensor_copy(bias[0:1, 2 * D:3 * D], k.ps[0:1, 5, 0:D]).then_inc(S["w_ready"], 1)
                dve.wait_ge(S["zeroed"], 2)
                dve.wait_ge(S["w_ready"], 1)
                CH = 5

                def prepare(i, o):
                    if not isinstance(i, int) or i >= 4:
                        dve.wait_ge(S["turned"], i - 3)
                    nc.vector.tensor_scalar(both[:, o, 0:D], k.xs[:, bass.ts(i, D)], mv[:, 0, bass.ds(i, 1)],
                                            mv[:, 4, bass.ds(i, 1)], ALU.subtract, ALU.mult)
                    nc.vector.tensor_copy(both[:, o, 2 * D:2 * D + 1], full[:, bass.ds(i, 1)])
                    nc.vector.tensor_scalar(both[:, o, D:2 * D], k.sums[:, bass.ds(i * W, D)], inv[:, bass.ds(i, 1)],
                                            None, ALU.mult).then_inc(S["normed"], 1)

                def update(i, slot):
                    o = slot % 2
                    xn = both[:, slot, 0:D]

                    def link(n, ins):
                        ins.then_inc(S["chain"], 1)
                        dve.wait_ge(S["chain"], i * CH + n)

                    dve.wait_ge(S["gates"], i + 1)
                    link(1, nc.vector.tensor_tensor(new[:, o, :], rz[:, o, 0:D], k.ps[:, 4 + o, D:], ALU.mult))
                    nc.vector.tensor_tensor(new[:, o, :], new[:, o, :], k.ps[:, 4 + o, 0:D],
                                            ALU.add).then_inc(S["candidate"], 1)
                    dve.wait_ge(S["tanh_done"], i + 1)
                    link(2, nc.vector.tensor_tensor(xn, xn, new[:, o, :], ALU.subtract))
                    link(3, nc.vector.tensor_tensor(xn, xn, rz[:, o, D:], ALU.mult))
                    link(4, nc.vector.tensor_tensor(new[:, o, :], new[:, o, :], xn, ALU.add))
                    link(5, nc.vector.bn_stats(nst[:, o, :], new[:, o, :]))
                    nc.vector.tensor_scalar(st[:, bass.ts(i, 6)], nst[:, o, :], 1.0, None, ALU.mult)
                    nc.vector.tensor_scalar(outv[:, bass.ts(i, D)], new[:, o, :], 1.0, None,
                                            ALU.mult).then_inc(S["finished"], 1)

                staggered(dve, [(prepare, 0), (update, 2)])
                dve.wait_ge(S["finished"], NT)
                emit_moments(k, dve, st, mv, S["tile_var"], S["tile_sqrt"], step)
                start = step.n
                with dve.Fori(0, GROUPS) as g:
                    for n in range(4):
                        for u in range(U):
                            i = g * U + u
                            y, xsl = outv[:, bass.ts(i, D)], k.xs[:, bass.ts(i, D)]
                            if n == 0:
                                last = nc.vector.tensor_scalar(y, y, mv[:, 0, bass.ds(i, 1)],
                                                               mv[:, 4, bass.ds(i, 1)], ALU.subtract, ALU.mult)
                            elif n == 1:
                                last = nc.vector.tensor_tensor(y, y, gamma[:], ALU.mult)
                            elif n == 2:
                                last = nc.vector.tensor_tensor(xsl, xsl, beta[:], ALU.add)
                            else:
                                last = nc.vector.tensor_tensor(xsl, xsl, y, ALU.add)
                        last.then_inc(S["dve_step"], 1)
                        dve.wait_ge(S["dve_step"], start + 4 * g + n + 1)

            @block.scalar
            def _(act):
                emit_sqrt(k, act, mv, S["stats_ready"], S["sqrt_ready"])

                def copy_turned(i, slot):
                    o = slot % 2
                    act.wait_ge(S["turned"], i + 1)
                    if not isinstance(i, int) or i >= 2:
                        act.wait_ge(S["product"], i - 1)
                    nc.scalar.copy(both_t[:, o, :, :], k.ps[:, o, :].rearrange("p (a b) -> p a b", b=P))
                    nc.scalar.copy(ones_t[:, o, :], k.ps[0:3, 6, 0:P]).then_inc(S["turned_copied"], 1)

                def gates(i, slot):
                    o = slot % 2
                    act.wait_ge(S["product"], i + 1)
                    if not isinstance(i, int) or i >= 2:
                        act.wait_ge(S["finished"], i - 1)
                    nc.scalar.activation(rz[:, o, :], k.ps[:, 2 + o, :], ACT.Sigmoid).then_inc(S["gates"], 1)
                    act.wait_ge(S["candidate"], i + 1)
                    nc.scalar.activation(new[:, o, :], new[:, o, :], ACT.Tanh).then_inc(S["tanh_done"], 1)

                staggered(act, [(copy_turned, 0), (gates, 1)])
                emit_sqrt(k, act, mv, S["tile_var"], S["tile_sqrt"])

            @block.tensor
            def _(pe):
                pe.wait_ge(S["loaded"], 16 * 9)
                for m in range(KC):
                    for c in range(KC):
                        nc.tensor.matmul(k.ps[:, 2 * m, :], w2[:, c, bass.ts(m, P)], w_ih[:, c, 0:2 * D],
                                         start=c == 0, stop=c == KC - 1)
                    for c in range(KC):
                        nc.tensor.matmul(k.ps[:, 2 * m + 1, 0:D], w2[:, c, bass.ts(m, P)], w_ih[:, c, 2 * D:],
                                         start=c == 0, stop=c == KC - 1)
                for c in range(KC):
                    nc.tensor.matmul(k.ps[0:1, 4, :], b2[:, c:c + 1], w_ih[:, c, 0:2 * D], start=c == 0,
                                     stop=c == KC - 1)
                for c in range(KC):
                    last = nc.tensor.matmul(k.ps[0:1, 5, 0:D], b2[:, c:c + 1], w_ih[:, c, 2 * D:], start=c == 0,
                                            stop=c == KC - 1)
                last.then_inc(S["fused"], 1)
                pe.wait_ge(S["w_ready"], 1)

                def turn(i, slot):
                    o = slot % 2
                    pe.wait_ge(S["normed"], i + 1)
                    pe.wait_ge(S["turned_copied"], i)
                    for c in range(4):
                        nc.tensor.transpose(k.ps[:, o, bass.ts(c, P)], both[:, slot, bass.ts(c, P)], k.ident[:])
                    nc.tensor.transpose(k.ps[0:3, 6, 0:P], both[:, slot, 2 * D:], k.ident[:]).then_inc(S["turned"], 1)

                def products(i, slot):
                    o = slot % 2
                    pe.wait_ge(S["turned_copied"], i + 1)
                    if not isinstance(i, int) or i > 1:
                        pe.wait_ge(S["candidate"], i - 1)
                    rz_p, i_n, h_n = k.ps[:, 2 + o, :], k.ps[:, 4 + o, 0:D], k.ps[:, 4 + o, D:]
                    x_t, m_t, one = both_t[:, o, 0:2, :], both_t[:, o, 2:4, :], ones_t[:, o, :]
                    for c in range(KC):
                        nc.tensor.matmul(rz_p, x_t[:, c, :], w_hh[:, c, 0:2 * D], start=c == 0, stop=False)
                    for c in range(KC):
                        nc.tensor.matmul(rz_p, m_t[:, c, :], w_in[:, c, 0:2 * D], start=False, stop=False)
                    nc.tensor.matmul(rz_p, one, bias[:, 0:2 * D], start=False, stop=True)
                    for c in range(KC):
                        nc.tensor.matmul(i_n, m_t[:, c, :], w_in[:, c, 2 * D:], start=c == 0, stop=False)
                    nc.tensor.matmul(i_n, one, bias[:, 2 * D:3 * D], start=False, stop=True)
                    for c in range(KC):
                        nc.tensor.matmul(h_n, x_t[:, c, :], w_hh[:, c, 2 * D:], start=c == 0, stop=False)
                    nc.tensor.matmul(h_n, one, bias[:, 3 * D:], start=False, stop=True).then_inc(S["product"], 1)

                staggered(pe, [(turn, 0), (products, 1)])


def experts(k):
    nc, t = k.nc, k.t
    ctx, sb, sem = phase(k)
    TOK = U * P
    HALF = TOK // 2
    with ctx:
        w1, w2 = sb("w1", [P, NE, KC, ED]), sb("w2", [P, NE, EK, D])
        b1, b2 = sb("b1", [P, NE, EK]), sb("b2", [NE, D])
        w_gate, b_gate, g_bias = sb("w_gate", [P, KC, NE]), sb("b_gate", [P, NE]), sb("g_bias", [P, NE])
        rank = sb("rank", [P, U, NE])
        st, mv = sb("st", [P, NT * 6]), sb("mv", [P, 5, NT])
        xn, xt = sb("xn", [P, U, D]), sb("xt", [P, KC, TOK])
        hid = sb("hid", [P, 2, EK, TOK])
        y = sb("y", [P, U, D])
        logit, eq, one, two, mix = (sb(n, [P, U, NE]) for n in ("logit", "eq", "one", "two", "mix"))
        best = sb("best", [P, 6, U])
        mix_t = sb("mix_t", [NE, U, P])
        names = ("loaded", "gate_loaded", "dve_step", "stats_ready", "sqrt_ready", "ranked", "normed", "turned",
                 "turned_copied", "gated", "chain", "gap", "gap_exp", "mix_ready", "mix_turned", "mix_copied", "based",
                 "filled", "based_mix", "hidden", "active", "projected", "mixed")
        S = {n: sem(n) for n in names}
        stored = [sem(f"stored{u}") for u in range(U)]

        def groups(engine, group):
            with engine.Fori(0, GROUPS - 1) as g:
                group(g, False)
            group(GROUPS - 1, True)

        with nc.Block() as block:
            @block.sync
            def _(sp):
                load_weights(k, sp, S["gate_loaded"], [
                    (w_gate[:], chunks(t["w_gate"])), (b_gate[:], across(t["b_gate"])), (g_bias[:], across(t["gate_bias"]))])
                load_weights(k, sp, S["loaded"], [(b1[:], t["e_b1_cols"]), (b2[:], t["e_b2"])])
                for e in range(NE):
                    sp.dma_start(w1[:, e, :, :], chunks(t["e_w1"][e])).then_inc(S["loaded"], 16)
                    sp.dma_start(w2[:, e, :, :], chunks(t["e_w2"][e])).then_inc(S["loaded"], 16)

                def group(g, last):
                    for u in range(U):
                        i = g * U + u
                        sp.wait_ge(S["mixed"], (g * NE + NE - 1) * U + u + 1)
                        if last and u == U - 1:
                            sp.dma_start(t["out"][(NT - 1) * P:N, :], y[0:TAIL, u, :]).then_inc(stored[u], 16)
                        else:
                            sp.dma_start(t["out"][bass.ts(i, P), :], y[:, u, :]).then_inc(stored[u], 16)

                groups(sp, group)
                for u in range(U):
                    sp.wait_ge(stored[u], 16 * GROUPS)

            @block.vector
            def _(dve):
                step = Steps(dve, S["dve_step"])
                emit_norm(k, dve, st, mv, S["stats_ready"], S["sqrt_ready"], step)
                for u in range(U):
                    last = nc.vector.tensor_scalar(rank[:, u, :], k.iota[:, 0:NE], -1.0, float(NE), ALU.mult, ALU.add)
                step(last)
                dve.wait_ge(S["gate_loaded"], 48)
                CH = 18

                def group(g, final):
                    def link(n, ins):
                        ins.then_inc(S["chain"], 1)
                        dve.wait_ge(S["chain"], g * CH + n)

                    for u in range(U):
                        i = g * U + u
                        dve.wait_ge(S["turned"], i + 1)
                        nc.vector.tensor_scalar(xn[:, u, :], k.xs[:, bass.ts(i, D)], mv[:, 0, bass.ds(i, 1)],
                                                mv[:, 4, bass.ds(i, 1)], ALU.subtract, ALU.mult).then_inc(S["normed"], 1)
                    for u in range(U):
                        i = g * U + u
                        dve.wait_ge(stored[u], 16 * g)
                        last = nc.vector.tensor_scalar(y[:, u, :], k.xs[:, bass.ts(i, D)], 1.0, None, ALU.mult)
                    last.then_inc(S["filled"], 1)
                    dve.wait_ge(S["gated"], g + 1)

                    def spread(v):
                        return v.unsqueeze(2).to_broadcast([P, U, NE])

                    def same(v):
                        return v[:].unsqueeze(1).to_broadcast([P, U, NE])

                    link(1, nc.vector.tensor_tensor(logit[:], k.ps[:, 7, 0:U * NE].rearrange(
                        "p (u e) -> p u e", e=NE), same(b_gate), ALU.add))
                    link(2, nc.vector.tensor_tensor(logit[:], logit[:], same(g_bias), ALU.add))
                    n = 2
                    for hot, top in ((one, best[:, 0, :]), (two, best[:, 1, :])):
                        link(n + 1, nc.vector.tensor_reduce(top, logit[:], AX, ALU.max))
                        link(n + 2, nc.vector.tensor_tensor(eq[:], logit[:], spread(top), ALU.is_equal))
                        link(n + 3, nc.vector.tensor_tensor(eq[:], eq[:], rank[:], ALU.mult))
                        link(n + 4, nc.vector.tensor_reduce(best[:, 2, :], eq[:], AX, ALU.max))
                        link(n + 5, nc.vector.tensor_tensor(hot[:], eq[:], spread(best[:, 2, :]), ALU.is_equal))
                        if hot is one:
                            link(n + 6, nc.vector.scalar_tensor_tensor(out=logit[:], in0=one[:], scalar=-BIG,
                                                                       in1=logit[:], op0=ALU.mult, op1=ALU.add))
                            n += 6
                    nc.vector.tensor_tensor(best[:, 3, :], best[:, 1, :], best[:, 0, :], ALU.subtract).then_inc(S["gap"], 1)
                    dve.wait_ge(S["gap_exp"], g + 1)
                    link(14, nc.vector.tensor_scalar(best[:, 4, :], best[:, 3, :], 1.0, None, ALU.add))
                    link(15, nc.vector.reciprocal(best[:, 4, :], best[:, 4, :]))
                    link(16, nc.vector.tensor_tensor(best[:, 5, :], best[:, 3, :], best[:, 4, :], ALU.mult))
                    link(17, nc.vector.tensor_tensor(one[:], one[:], spread(best[:, 4, :]), ALU.mult))
                    link(18, nc.vector.tensor_tensor(two[:], two[:], spread(best[:, 5, :]), ALU.mult))
                    nc.vector.tensor_tensor(mix[:], one[:], two[:], ALU.add).then_inc(S["mix_ready"], 1)
                    dve.wait_ge(S["mix_ready"], g + 1)
                    dve.wait_ge(S["filled"], g + 1)
                    for u in range(U):
                        i = g * U + u
                        dve.wait_ge(S["based"], i + 1)
                        nc.vector.tensor_tensor(y[:, u, :], y[:, u, :], k.ps[:, 4 + u % 2, 0:D],
                                                ALU.add).then_inc(S["based_mix"], 1)
                    for e in range(NE):
                        for u in range(U):
                            n = (g * NE + e) * U + u
                            dve.wait_ge(S["projected"], n + 1)
                            if e:
                                dve.wait_ge(S["mixed"], n - U + 1)
                            else:
                                dve.wait_ge(S["based_mix"], g * U + u + 1)
                            nc.vector.scalar_tensor_tensor(
                                out=y[:, u, :], in0=k.ps[:, 4 + u % 2, 0:D], scalar=mix[:, u, e:e + 1],
                                in1=y[:, u, :], op0=ALU.mult, op1=ALU.add).then_inc(S["mixed"], 1)

                groups(dve, group)

            @block.scalar
            def _(act):
                emit_sqrt(k, act, mv, S["stats_ready"], S["sqrt_ready"])
                act.wait_ge(S["loaded"], 16 * (2 + 2 * NE))

                def relu(g, e):
                    for m in range(EK):
                        n = (g * NE + e) * EK + m
                        act.wait_ge(S["hidden"], n + 1)
                        if e >= 2:
                            act.wait_ge(S["projected"], (g * NE + e - 1) * U)
                        else:
                            act.wait_ge(S["projected"], g * NE * U)
                        nc.scalar.activation(
                            hid[:, e % 2, m, :].rearrange("p (a b) -> p a b", b=HALF),
                            k.ps[:, 2 * (m % 2):2 * (m % 2) + 2, 0:HALF], ACT.Relu,
                            bias=b1[:, e, m:m + 1]).then_inc(S["active"], 1)

                def group(g, last):
                    act.wait_ge(S["hidden"], g * NE * EK)
                    for u in range(U):
                        i = g * U + u
                        act.wait_ge(S["turned"], i + U + 1)
                        nc.scalar.copy(xt[:, :, bass.ts(u, P)],
                                       k.ps[:, 6, 0:D].rearrange("p (c n) -> p c n", n=P)).then_inc(S["turned_copied"], 1)
                    act.wait_ge(S["gap"], g + 1)
                    nc.scalar.activation(best[:, 3, :], best[:, 3, :], ACT.Exp).then_inc(S["gap_exp"], 1)
                    relu(g, 0)
                    act.wait_ge(S["mix_turned"], g + 1)
                    nc.scalar.copy(mix_t[:], k.ps[0:NE, 6:8, :].rearrange("p a b -> p (a b)")[:, 0:TOK].rearrange(
                        "p (u n) -> p u n", n=P)).then_inc(S["mix_copied"], 1)
                    for e in range(1, NE):
                        relu(g, e)

                groups(act, group)

            @block.tensor
            def _(pe):
                pe.sem_inc(S["turned"], U)

                def hidden(g, e):
                    for m in range(EK):
                        n = (g * NE + e) * EK + m
                        if e or m >= 2:
                            pe.wait_ge(S["active"], n - 1)
                        else:
                            pe.wait_ge(S["active"], g * NE * EK)
                        for h in range(2):
                            for c in range(KC):
                                last = nc.tensor.matmul(k.ps[:, 2 * (m % 2) + h, 0:HALF], w1[:, e, c, bass.ts(m, P)],
                                                        xt[:, c, bass.ts(h, HALF)], start=c == 0, stop=c == KC - 1)
                        last.then_inc(S["hidden"], 1)

                def project(g, e):
                    pe.wait_ge(S["active"], (g * NE + e + 1) * EK)
                    for u in range(U):
                        n = (g * NE + e) * U + u
                        if u >= 2:
                            pe.wait_ge(S["mixed"], n - 1)
                        elif e:
                            pe.wait_ge(S["mixed"], n - u)
                        else:
                            pe.wait_ge(S["based_mix"], (g + 1) * U)
                        for m in range(EK):
                            last = nc.tensor.matmul(k.ps[:, 4 + u % 2, 0:D], hid[:, e % 2, m, bass.ts(u, P)],
                                                    w2[:, e, m, :], start=m == 0, stop=m == EK - 1)
                        last.then_inc(S["projected"], 1)

                def group(g, last_group):
                    for u in range(U):
                        i = g * U + u
                        pe.wait_ge(S["normed"], i + 1)
                        pe.wait_ge(S["turned_copied"], i)
                        pe.wait_ge(S["mix_copied"], g)
                        for c in range(KC):
                            last = nc.tensor.transpose(k.ps[:, 6, bass.ts(c, P)], xn[:, u, bass.ts(c, P)], k.ident[:])
                        last.then_inc(S["turned"], 1)
                    pe.wait_ge(S["turned_copied"], (g + 1) * U)
                    pe.wait_ge(S["gate_loaded"], 48)
                    for u in range(U):
                        for c in range(KC):
                            last = nc.tensor.matmul(k.ps[:, 7, bass.ts(u, NE)], xt[:, c, bass.ts(u, P)],
                                                    w_gate[:, c, :], start=c == 0, stop=c == KC - 1)
                    last.then_inc(S["gated"], 1)
                    pe.wait_ge(S["loaded"], 16 * (2 + 2 * NE))
                    hidden(g, 0)
                    pe.wait_ge(S["mix_ready"], g + 1)
                    for u in range(U):
                        bank, at = 6 + u // 4, (u % 4) * P
                        last = nc.tensor.transpose(k.ps[0:NE, bank, at:at + P], mix[:, u, :], k.ident[:])
                    last.then_inc(S["mix_turned"], 1)
                    hidden(g, 1)
                    pe.wait_ge(S["mix_copied"], g + 1)
                    for u in range(U):
                        i = g * U + u
                        if u >= 2:
                            pe.wait_ge(S["based_mix"], i - 1)
                        else:
                            pe.wait_ge(S["mixed"], g * NE * U)
                        nc.tensor.matmul(k.ps[:, 4 + u % 2, 0:D], mix_t[:, u, :], b2[:], start=True,
                                         stop=True).then_inc(S["based"], 1)
                    project(g, 0)
                    for e in range(2, NE):
                        hidden(g, e)
                        project(g, e - 1)
                    project(g, NE - 1)

                groups(pe, group)


def build(nc, t):
    ctx = ExitStack()
    with ctx:
        def sb(name, shape, dtype=F32):
            return ctx.enter_context(nc.sbuf_tensor(name, shape, dtype))

        k = Kept(nc, t)
        k.ps = ctx.enter_context(nc.psum_tensor("banks", [P, 8, 512], F32))
        k.xs = sb("xs", [P, NT * D])
        k.er = sb("er", [P, NT * H1])
        k.ident, k.ones = sb("ident", [P, P]), sb("ones", [P, P])
        k.tri_incl, k.tri_strict = sb("tri_incl", [P, P]), sb("tri_strict", [P, P])
        k.iota, k.mask = sb("iota", [P, P]), sb("mask", [P, NT])
        k.dst_i, k.src_i = sb("dst_i", [P, EC], I32), sb("src_i", [P, EC], I32)
        k.dst_f = sb("dst_f", [P, EC])
        k.pos_i, k.edge_rec = sb("pos_i", [P, EC], I32), sb("edge_rec", [P, EC * 2], I32)
        k.base_dst, k.base_src = sb("base_dst", [P, ST]), sb("base_src", [P, ST])
        k.start_dst, k.start_src = sb("start_dst", [1, ST], I32), sb("start_src", [1, ST], I32)
        k.tile_dst, k.tile_src = sb("tile_dst", [1, ST], I32), sb("tile_src", [1, ST], I32)
        k.large = sb("large", [P, NT * (2 * D + 1)])
        k.source_part, k.sums = k.large[:, 0:NT * D], k.large[:, NT * D:]
        k.new_rows = k.source_part
        phases = [setup, gat_tables, gat_scores, gat_edges, slice_attention, message_tables, message_edges, gated_update, experts]
        for f in phases:
            f(k)
            nc.clear_and_free_semaphores(k.semaphores)
            k.semaphores = []
            nc.all_engine_barrier()


_LAYOUT = {
    "x": ("x", lambda a: a), "src": ("src", lambda a: a), "dst": ("dst", lambda a: a),
    "w_lin": ("L0_gnn_W_lin", lambda a: a), "w_lin_t": ("L0_gnn_W_lin", lambda a: a.T),
    "b_lin": ("L0_gnn_b_lin", lambda a: a), "b_lin_cols": ("L0_gnn_b_lin", lambda a: a.reshape(KC, P).T),
    "w_gat": ("L0_gnn_W_gat", lambda a: a),
    "attn_l": ("L0_gnn_attn_l", lambda a: a), "attn_r": ("L0_gnn_attn_r", lambda a: a),
    "gat_bias": ("L0_gnn_gat_bias", lambda a: a),
    "w_fx": ("L0_ffn_W_fx", lambda a: a), "b_fx": ("L0_ffn_b_fx", lambda a: a),
    "w_x_t": ("L0_ffn_W_x", lambda a: a.T), "b_x_cols": ("L0_ffn_b_x", lambda a: a.reshape(SH, SD).T),
    "w_slice": ("L0_ffn_W_slice", lambda a: a), "b_slice": ("L0_ffn_b_slice", lambda a: a),
    "w_q": ("L0_ffn_W_q", lambda a: a), "w_k": ("L0_ffn_W_k", lambda a: a), "w_v": ("L0_ffn_W_v", lambda a: a),
    "w_out": ("L0_ffn_W_out", lambda a: a), "b_out": ("L0_ffn_b_out", lambda a: a),
    "temp": ("L0_ffn_temperature", lambda a: a.reshape(-1)),
    "w1_t": ("L1_gnn_W1", lambda a: a.T), "b1": ("L1_gnn_b1", lambda a: a),
    "w2": ("L1_gnn_W2", lambda a: a), "b2_cols": ("L1_gnn_b2", lambda a: a.reshape(KC, P).T),
    "w_ih_t": ("L1_gnn_w_ih", lambda a: a.T), "w_hh_t": ("L1_gnn_w_hh", lambda a: a.T),
    "b_ih": ("L1_gnn_b_ih", lambda a: a), "b_hh": ("L1_gnn_b_hh", lambda a: a),
    "gamma": ("L1_gnn_gamma", lambda a: a), "beta": ("L1_gnn_beta", lambda a: a),
    "w_gate": ("L1_ffn_Wg", lambda a: a), "b_gate": ("L1_ffn_bg", lambda a: a),
    "gate_bias": ("L1_ffn_bias", lambda a: a),
    "e_w1": ("L1_ffn_W1", lambda a: a), "e_b1_cols": ("L1_ffn_b1", lambda a: a.reshape(NE, EK, P).transpose(2, 0, 1)),
    "e_w2": ("L1_ffn_W2", lambda a: a), "e_b2": ("L1_ffn_b2", lambda a: a),
}
_TABLES = {
    "gat_rows": ((NP, D), F32), "el_rows": ((NP, H1), F32),
    "rec_gat": ((ER, RW), I32), "rec_src": ((ER, 2), I32), "msg_rows": ((NP, D), F32),
    "slice_bias": ((SH, SD), F32),
}


def kernel(**inputs):
    import numpy as np
    import concourse.bacc as bacc
    from concourse.bass_utils import run_bass_kernel_spmd as run

    nc = bacc.Bacc("TRN2", target_bir_lowering=False, num_devices=1)
    tables, arrays = {}, {}
    for name, (source, lay) in _LAYOUT.items():
        a = np.ascontiguousarray(lay(np.asarray(inputs[source])))
        arrays["in_" + name] = a
        tables[name] = nc.dram_tensor("in_" + name, a.shape, mybir.dt.from_np(a.dtype), kind="ExternalInput").ap()
    for name, (shape, dtype) in _TABLES.items():
        tables[name] = nc.dram_tensor("tab_" + name, list(shape), dtype, kind="Internal").ap()
    tables["out"] = nc.dram_tensor("out_0_dram", (N, D), F32, kind="ExternalOutput").ap()
    build(nc, tables)
    return run(nc, [arrays], core_ids=[0]).results[0]["out_0_dram"]
```

```python
from contextlib import ExitStack

import concourse.bass as bass
from concourse import mybir
from concourse.alu_op_type import AluOpType as ALU

ACT = mybir.ActivationFunctionType
F32 = mybir.dt.float32
I32 = mybir.dt.int32
AX = mybir.AxisListType.X
DVE, SP = mybir.EngineType.DVE, mybir.EngineType.SP
PE = mybir.EngineType.PE

P = 128
N = 3125
NT = -(-N // P)
NP = NT * P
TAIL = N - (NT - 1) * P
D = 256
KC = D // P
E = 50000
EC = 392
EP = P * EC
EFULL = E // EC
EREST = E - EFULL * EC
ST = (EP + NT * (P - 1)) // P
ER = EP + P
H1 = 8
HD = D // H1
SH, SD = 8, 64
SI = SH * SD
PAIRS = SH // 2
NE, ED = 8, 512
EK = ED // P
U = 5
GROUPS = NT // U
BIG = 1.0e30
EPS = 1e-5
RW = 2 + 2 * H1
SEND = 14
PART = 7
SENT_BY_GAT, SENT_BY_SLICES, SENT_BY_MESSAGES = (0, 8), (8, 24), (24, EC // SEND)
assert EC % SEND == 0 and all(a % 2 == 0 == b % 2 for a, b in (SENT_BY_GAT, SENT_BY_SLICES, SENT_BY_MESSAGES))
assert NT % U == 0 and EC % 28 == 0 and EREST < EC


class Kept:

    def __init__(self, nc, tables):
        self.nc, self.t, self.count, self.semaphores = nc, tables, 0, []


class Steps:

    def __init__(self, engine, semaphore, start=0):
        self.engine, self.semaphore, self.n = engine, semaphore, start

    def __call__(self, instruction):
        instruction.then_inc(self.semaphore, 1)
        self.n = self.n + 1
        self.engine.wait_ge(self.semaphore, self.n)


def phase(k):
    ctx = ExitStack()
    nc = k.nc
    k.count += 1
    tag = f"p{k.count}_"

    def sb(name, shape, dtype=F32):
        return ctx.enter_context(nc.sbuf_tensor(tag + name, shape, dtype))

    def sem(name):
        handle = nc.alloc_semaphore(name=tag + name)
        k.semaphores.append(handle)
        return handle

    return ctx, sb, sem


def do(k, emit, *args):
    emit(k, *args)
    k.nc.clear_and_free_semaphores(k.semaphores)
    k.semaphores = []
    k.nc.all_engine_barrier()


def emit_norm(k, dve, st, mv, stats_ready, sqrt_ready, steps):
    nc = k.nc
    with dve.Fori(0, GROUPS) as g:
        for u in range(U):
            last = nc.vector.bn_stats(st[:, bass.ts(g * U + u, 6)], k.xs[:, bass.ts(g * U + u, D)])
        last.then_inc(steps.semaphore, 1)
    steps.n += GROUPS
    dve.wait_ge(steps.semaphore, steps.n)
    emit_moments(k, dve, st, mv, stats_ready, sqrt_ready, steps)


def emit_moments(k, dve, st, mv, stats_ready, sqrt_ready, steps):
    nc = k.nc
    s = st[:].rearrange("p (i c) -> p i c", c=6)
    mean, var, dif = mv[:, 0, :], mv[:, 1, :], mv[:, 2, :]
    steps(nc.vector.tensor_tensor(dif, s[:, :, 1], s[:, :, 4], ALU.subtract))
    steps(nc.vector.tensor_tensor(var, s[:, :, 2], s[:, :, 5], ALU.add))
    steps(nc.vector.tensor_tensor(dif, dif, dif, ALU.mult))
    steps(nc.vector.tensor_scalar(dif, dif, 0.25, None, ALU.mult))
    steps(nc.vector.scalar_tensor_tensor(out=var, in0=var, scalar=1.0 / D, in1=dif, op0=ALU.mult, op1=ALU.add))
    steps(nc.vector.tensor_tensor(mean, s[:, :, 1], s[:, :, 4], ALU.add))
    steps(nc.vector.tensor_scalar(mean, mean, 0.5, None, ALU.mult))
    nc.vector.tensor_scalar(mv[:, 3, :], var, EPS, None, ALU.add).then_inc(stats_ready, 1)
    rstd = mv[:, 4, :]
    dve.wait_ge(sqrt_ready, 1)
    steps(nc.vector.reciprocal(rstd, rstd))
    steps(nc.vector.tensor_tensor(dif, rstd, rstd, ALU.mult))
    steps(nc.vector.tensor_tensor(dif, dif, mv[:, 3, :], ALU.mult))
    steps(nc.vector.tensor_scalar(dif, dif, -0.5, 1.5, ALU.mult, ALU.add))
    steps(nc.vector.tensor_tensor(rstd, rstd, dif, ALU.mult))


def emit_sqrt(k, act, mv, stats_ready, sqrt_ready):
    act.wait_ge(stats_ready, 1)
    k.nc.scalar.activation(mv[:, 4, :], mv[:, 3, :], ACT.Sqrt).then_inc(sqrt_ready, 1)


def load_weights(k, sp, sem, pairs):
    for dst, src in pairs:
        sp.dma_start(dst, src).then_inc(sem, 16)
    return 16 * len(pairs)


class Sender:

    def __init__(self, k, sb, sem):
        self.k = k
        self.place, self.pair = sb("place", [P, 2, SEND], I32), sb("pair", [P, 2, SEND, 2], I32)
        self.placed, self.scattering, self.sent = sem("send_placed"), sem("scattering"), [sem("sent0"), sem("sent1")]


def send_edges(pool, sender, table, first, last):
    nc, k, placed, sent = sender.k.nc, sender.k, sender.placed, sender.sent
    place, pair = sender.place, sender.pair
    with pool.Fori(0, (last - first) // 2) as g:
        for s in range(2):
            c = 2 * g + (first + s)
            pool.wait_ge(sent[s], 16 * SEND * g)
            nc.gpsimd.tensor_copy(place[:, s, :], k.pos_i[:, bass.ts(c, SEND)]).then_inc(placed, 1)
            nc.gpsimd.tensor_copy(pair[:, s, :, :].rearrange("p j c -> p (j c)"),
                                  k.edge_rec[:, bass.ts(c, 2 * SEND)]).then_inc(placed, 1)
            pool.wait_ge(placed, 4 * g + (2 * s + 2))
            pool.sem_inc(sender.scattering, 1)
            for j in range(SEND):
                nc.gpsimd.indirect_dma_start(
                    table[0:EP, :], bass.IndirectOffsetOnAxis(ap=place[:, s, j:j + 1], axis=0),
                    pair[:, s, j, :], None).then_inc(sent[s], 16)
    for s in range(2):
        pool.wait_ge(sent[s], 16 * SEND * (last - first) // 2)


def send_part(pool, sender, table, g):
    nc, k, placed, sent = sender.k.nc, sender.k, sender.placed, sender.sent[0]
    place, pair = sender.place, sender.pair
    pool.wait_ge(sent, 16 * PART * g)
    nc.gpsimd.tensor_copy(place[:, 0, 0:PART], k.pos_i[:, bass.ts(g, PART)]).then_inc(placed, 1)
    nc.gpsimd.tensor_copy(pair[:, 0, 0:PART, :].rearrange("p j c -> p (j c)"),
                          k.edge_rec[:, bass.ts(g, 2 * PART)]).then_inc(placed, 1)
    pool.wait_ge(placed, 2 * g + 2)
    pool.sem_inc(sender.scattering, 1)
    for j in range(PART):
        nc.gpsimd.indirect_dma_start(
            table[0:EP, :], bass.IndirectOffsetOnAxis(ap=place[:, 0, j:j + 1], axis=0),
            pair[:, 0, j, :], None).then_inc(sent, 16)


def staggered(engine, stages):
    deepest = max(lag for _, lag in stages)
    first = deepest + 4 + (NT - deepest) % 4

    def one(base, n):
        for stage, lag in stages:
            if not (isinstance(base, int) and (n < lag or n - lag >= NT)):
                stage(base + (n - lag), (n - lag) % 4)

    for n in range(first):
        one(0, n)
    with engine.Fori(0, (NT - first) // 4) as g:
        for n in range(4):
            one(g * 4, first + n)
    for n in range(NT, NT + deepest):
        one(0, n)


def row(v):
    return v.rearrange("(a d) -> a d", a=1)


def across(v):
    return row(v).to_broadcast([P, v.shape[0]])


def chunks(w):
    return w.rearrange("(c p) n -> p c n", p=P)


def setup(k):
    nc, t = k.nc, k.t
    ctx, sb, sem = phase(k)
    with ctx:
        loaded, made, made2, dve_step = sem("loaded"), sem("made"), sem("made2"), sem("dve_step")
        pad_gat, pad2 = sb("pad_gat", [P, RW], I32), sb("pad2", [P, 2], I32)
        pad_f = sb("pad_f", [P, 1])
        following, follow_f = sb("following", [P, 1], I32), sb("follow_f", [P, 1])
        falls, fall_count = sb("falls", [P, EC]), sb("fall_count", [P, 2])
        pads_made, pads_stored = sem("pads_made"), sem("pads_stored")
        edges_filled, x_filled, compared, totalled = (
            sem(s) for s in ("edges_filled", "x_filled", "compared", "totalled"))

        with nc.Block() as block:
            @block.sync
            def _(sp):
                sp.wait_ge(edges_filled, 3)
                for dst, src in ((k.dst_i, t["dst"]), (k.src_i, t["src"])):
                    sp.dma_start(dst[0:EFULL, :], src[0:EFULL * EC].rearrange("(p j) -> p j", j=EC)).then_inc(loaded, 16)
                    sp.dma_start(dst[EFULL:EFULL + 1, 0:EREST], row(src[EFULL * EC:E])).then_inc(loaded, 16)
                sp.dma_start(following[0:EFULL, :], t["dst_following"]).then_inc(loaded, 16)
                sp.wait_ge(x_filled, 1)
                sp.dma_start(k.xs[:, 0:(NT - 1) * D].rearrange("p (i d) -> p i d", d=D),
                             t["x"][0:(NT - 1) * P, :].rearrange("(i p) d -> p i d", p=P)).then_inc(pads_stored, 16)
                sp.dma_start(k.xs[0:TAIL, (NT - 1) * D:NT * D], t["x"][(NT - 1) * P:N, :]).then_inc(pads_stored, 16)
                sp.wait_ge(pads_made, 5)
                sp.dma_start(t["rec_gat"][EP:ER, :], pad_gat[:]).then_inc(pads_stored, 16)
                sp.dma_start(t["rec_src"][EP:ER, :], pad2[:]).then_inc(pads_stored, 16)
                sp.wait_ge(pads_stored, 64)

            @block.gpsimd
            def _(pool):
                nc.gpsimd.memset(k.dst_i[:], NP - 1).then_inc(edges_filled, 1)
                nc.gpsimd.memset(k.src_i[:], NP - 1).then_inc(edges_filled, 1)
                nc.gpsimd.memset(following[:], NP - 1).then_inc(edges_filled, 1)
                nc.gpsimd.memset(k.xs[:, (NT - 1) * D:NT * D], 0.0).then_inc(x_filled, 1)
                nc.gpsimd.memset(k.ones[:], 1.0).then_inc(made, 1)
                nc.gpsimd.memset(pad_f[:], float(NP - 1)).then_inc(pads_made, 1)
                nc.gpsimd.memset(pad_gat[:], 0).then_inc(pads_made, 1)
                pool.wait_ge(pads_made, 2)
                nc.gpsimd.memset(pad_gat[:, 0:1], NP - 1).then_inc(pads_made, 1)
                nc.gpsimd.memset(pad2[:, 0:1], NP - 1).then_inc(pads_made, 1)
                nc.gpsimd.memset(k.ident[:], 0.0).then_inc(made, 1)
                nc.gpsimd.memset(k.tri_incl[:], 1.0).then_inc(made, 1)
                nc.gpsimd.memset(k.tri_strict[:], 1.0).then_inc(made, 1)
                nc.gpsimd.memset(k.mask[:], 1.0).then_inc(made, 1)
                nc.gpsimd.iota(k.iota[:], pattern=[[1, P]], base=0, channel_multiplier=0,
                               allow_small_or_imprecise_dtypes=True).then_inc(made, 1)
                pool.wait_ge(made, 6)
                nc.gpsimd.affine_select(out=k.ident[:], in_=k.ident[:], compare_op=ALU.not_equal, fill=1.0,
                                        base=0, pattern=[[-1, P]], channel_multiplier=1).then_inc(made2, 1)
                nc.gpsimd.affine_select(out=k.tri_incl[:], in_=k.tri_incl[:], compare_op=ALU.is_ge, fill=0.0,
                                        base=0, pattern=[[1, P]], channel_multiplier=-1).then_inc(made2, 1)
                nc.gpsimd.affine_select(out=k.tri_strict[:], in_=k.tri_strict[:], compare_op=ALU.is_ge, fill=0.0,
                                        base=-1, pattern=[[1, P]], channel_multiplier=-1).then_inc(made2, 1)
                nc.gpsimd.affine_select(out=k.mask[:, NT - 1:NT], in_=k.mask[:, NT - 1:NT], compare_op=ALU.is_ge,
                                        fill=0.0, base=TAIL - 1, pattern=[[0, 1]],
                                        channel_multiplier=-1).then_inc(made2, 1)

            @block.vector
            def _(dve):
                step = Steps(dve, dve_step)
                step(nc.vector.memset(k.ones_e[:], 1.0))
                dve.wait_ge(pads_made, 4)
                step(nc.vector.tensor_copy(pad_gat[:, 1:2].bitcast(F32), pad_f[:]))
                nc.vector.tensor_copy(pad2[:, 1:2].bitcast(F32), pad_f[:]).then_inc(pads_made, 1)
                dve.wait_ge(loaded, 80)
                step(nc.vector.tensor_copy(k.dst_f[:], k.dst_i[:]))
                step(nc.vector.tensor_copy(follow_f[:], following[:]))
                step(nc.vector.tensor_tensor(falls[:, 0:EC - 1], k.dst_f[:, 0:EC - 1], k.dst_f[:, 1:EC], ALU.is_gt))
                step(nc.vector.tensor_tensor(falls[:, EC - 1:EC], k.dst_f[:, EC - 1:EC], follow_f[:], ALU.is_gt))
                nc.vector.tensor_reduce(fall_count[:, 0:1], falls[:], AX, ALU.add).then_inc(compared, 1)
                dve.wait_ge(totalled, 1)
                step(nc.vector.tensor_copy(k.unsorted[:], k.ps[0:1, 0, 0:1]))

            @block.tensor
            def _(pe):
                pe.wait_ge(made, 1)
                pe.wait_ge(compared, 1)
                nc.tensor.matmul(k.ps[0:1, 0, 0:1], fall_count[:, 0:1], k.ones[:, 0:1], start=True,
                                 stop=True).then_inc(totalled, 1)


def sort_pass(k, shift, buckets):
    nc, t = k.nc, k.t
    ctx, sb, sem = phase(k)
    with ctx:
        bkt_i, bkt = sb("bucket_i", [P, EC], I32), sb("bucket", [P, EC])
        scan, part, pos = sb("scan", [P, EC]), sb("part", [P, EC]), sb("pos", [P, EC])
        counts, total, before = sb("counts", [P, P]), sb("total", [P, P]), sb("before", [P, P])
        sender = Sender(k, sb, sem)
        dve_step, source_set, counted, summed, placed, tallied, scanned, scattered, reloaded = (
            sem(s) for s in ("dve_step", "source_set", "counted", "summed", "placed", "tallied", "scanned", "scattered", "reloaded"))
        rec = k.edge_rec[:].rearrange("p (j c) -> p j c", c=2)

        with nc.Block() as block:
            @block.vector
            def _(dve):
                step = Steps(dve, dve_step)
                step(nc.vector.tensor_scalar(bkt_i[:], k.dst_i[:], shift, P - 1, ALU.arith_shift_right,
                                             ALU.bitwise_and))
                step(nc.vector.tensor_copy(bkt[:], bkt_i[:]))
                step(nc.vector.memset(counts[:], 0.0))
                step(nc.vector.memset(pos[:], 0.0))
                with dve.Fori(0, buckets) as b:
                    dve.wait_ge(tallied, 2 * b)
                    nc.vector.tensor_scalar(part[:], bkt[:], k.iota[:, bass.ds(b, 1)], None,
                                            ALU.is_equal).then_inc(tallied, 1)
                    dve.wait_ge(tallied, 2 * b + 1)
                    nc.vector.tensor_reduce(counts[:, bass.ds(b, 1)], part[:], AX, ALU.add).then_inc(tallied, 1)
                dve.wait_ge(tallied, 2 * buckets)
                step(nc.vector.tensor_copy(total[:], counts[:]))
                dve.sem_inc(counted, 1)
                dve.wait_ge(summed, 1)
                step(nc.vector.tensor_copy(total[:], k.ps[:, 0, 0:P]))
                step(nc.vector.tensor_tensor_scan(before[:], k.ones_e[:, 0:P], total[:], -1.0, ALU.mult, ALU.add))
                step(nc.vector.tensor_tensor(before[:], before[:], total[:], ALU.subtract))
                step(nc.vector.tensor_tensor(before[:], before[:], k.ps[:, 1, 0:P], ALU.add))
                with dve.Fori(0, buckets) as b:
                    dve.wait_ge(placed, 4 * b)
                    nc.vector.tensor_scalar(part[:], bkt[:], k.iota[:, bass.ds(b, 1)], None,
                                            ALU.is_equal).then_inc(placed, 1)
                    dve.wait_ge(placed, 4 * b + 1)
                    dve.sem_inc(scanned, 1)
                    nc.vector.tensor_tensor_scan(scan[:], k.ones_e[:], part[:], 0.0, ALU.mult,
                                                 ALU.add).then_inc(placed, 1)
                    dve.wait_ge(placed, 4 * b + 2)
                    nc.vector.scalar_tensor_tensor(out=part[:], in0=scan[:], scalar=before[:, bass.ds(b, 1)],
                                                   in1=part[:], op0=ALU.add, op1=ALU.mult).then_inc(placed, 1)
                    dve.wait_ge(placed, 4 * b + 3)
                    nc.vector.tensor_tensor(pos[:], pos[:], part[:], ALU.add).then_inc(placed, 1)
                dve.wait_ge(placed, 4 * buckets)
                step(nc.vector.tensor_copy(k.pos_i[:], pos[:]))
                step(nc.vector.tensor_copy(rec[:, :, 0], k.dst_i[:]))
                dve.wait_ge(source_set, 1)
                dve.sem_inc(counted, 1)
                dve.wait_ge(reloaded, 16)
                step(nc.vector.tensor_copy(k.dst_i[:], rec[:, :, 0]))
                step(nc.vector.tensor_copy(k.src_i[:], rec[:, :, 1]))

            @block.scalar
            def _(act):
                nc.scalar.copy(rec[:, :, 1], k.src_i[:]).then_inc(source_set, 1)

            @block.tensor
            def _(pe):
                pe.wait_ge(counted, 1)
                nc.tensor.matmul(k.ps[:, 0, 0:P], k.ones[:], counts[:], start=True, stop=True)
                nc.tensor.matmul(k.ps[:, 1, 0:P], k.tri_strict[:], counts[:], start=True, stop=True).then_inc(summed, 1)

            @block.gpsimd
            def _(pool):
                pool.wait_ge(counted, 2)
                send_edges(pool, sender, t["rec_sort"], 0, EC // SEND)
                pool.sem_inc(scattered, 1)

            @block.sync
            def _(sp):
                sp.wait_ge(scattered, 1)
                sp.dma_start(k.edge_rec[:], t["rec_sort"][:, :].rearrange("(p j) c -> p (j c)", p=P)).then_inc(
                    reloaded, 16)


def edge_tables(k, sb, sem):
    nc = k.nc
    made, dve_step = sem("made"), sem("dve_step")
    bkt_i, bkt = sb("bucket_i", [P, EC], I32), sb("bucket", [P, EC])
    junk, scan, part = sb("junk", [P, EC]), sb("scan", [P, EC]), sb("part", [P, EC])
    pos = sb("pos", [P, EC])
    counts = sb("counts", [P, NT])
    src_f = sb("src_f", [P, EC])
    small = sb("small", [P, 8])
    small_i = sb("small_i", [P, 8], I32)
    tot, off = sb("tot", [P, NT]), sb("off", [P, NT])
    grid, vrow = sb("grid", [NT, ST]), sb("vrow", [NT, P])
    starts = sb("starts", [P, ST])
    iota_q = sb("iota_q", [P, ST])
    counted, summed, tiles_ready, cum_ready, grid_ready, table_ready = (
        sem(s) for s in ("counted", "summed", "tiles_ready", "cum_ready", "grid_ready", "table_ready"))

    def number(pool):
        nc.gpsimd.iota(iota_q[:], pattern=[[1, ST]], base=0, channel_multiplier=0,
                       allow_small_or_imprecise_dtypes=True).then_inc(made, 1)

    def count(dve):
        step = Steps(dve, dve_step)
        step(nc.vector.tensor_copy(k.dst_f[:], k.dst_i[:]))
        step(nc.vector.tensor_copy(src_f[:], k.src_i[:]))
        dve.wait_ge(made, 1)
        for n, (key, base, start, tile) in enumerate(((k.dst_i, k.base_dst, k.start_dst, k.tile_dst),
                                                      (k.src_i, k.base_src, k.start_src, k.tile_src))):
            step(nc.vector.tensor_scalar(bkt_i[:], key[:], 7, None, ALU.arith_shift_right))
            step(nc.vector.tensor_copy(bkt[:], bkt_i[:]))
            for b in range(NT):
                last = nc.vector.tensor_scalar(junk[:], bkt[:], float(b), 0.0, ALU.is_equal, ALU.add,
                                               accum_out=counts[:, b:b + 1])
                if b < NT - 1:
                    step(last)
            last.then_inc(counted, 1)
            dve.wait_ge(summed, n + 1)
            step(nc.vector.tensor_scalar(small[0:NT, 0:1], k.ps[0:NT, 0, 0:1], float(P - 1), None, ALU.add))
            step(nc.vector.tensor_copy(small_i[0:NT, 0:1], small[0:NT, 0:1]))
            step(nc.vector.tensor_scalar(small_i[0:NT, 1:2], small_i[0:NT, 0:1], 7, None,
                                         ALU.arith_shift_right))
            step(nc.vector.tensor_copy(small[0:NT, 1:2], small_i[0:NT, 1:2]))
            step(nc.vector.scalar_tensor_tensor(out=small[0:NT, 2:3], in0=small[0:NT, 1:2], scalar=-float(P),
                                                in1=k.ps[0:NT, 0, 0:1], op0=ALU.mult, op1=ALU.add))
            nc.vector.tensor_scalar(vrow[:], k.ones[0:NT, :], small[0:NT, 2:3], None,
                                    ALU.mult).then_inc(tiles_ready, 1)
            dve.wait_ge(cum_ready, n + 1)
            nc.vector.tensor_scalar(grid[:], iota_q[0:NT, :], k.ps[0:NT, 3, 0:1], None,
                                    ALU.is_ge).then_inc(grid_ready, 1)
            dve.wait_ge(table_ready, n + 1)
            step(nc.vector.tensor_scalar(base[:], k.ps[:, 4, 0:ST], float(NT - 1), None, ALU.min))
            step(nc.vector.tensor_copy(tile[:], base[0:1, :]))
            step(nc.vector.tensor_scalar(base[:], base[:], float(P), None, ALU.mult))
            step(nc.vector.scalar_tensor_tensor(out=starts[:], in0=iota_q[:], scalar=float(P),
                                                in1=k.ps[:, 5, 0:ST], op0=ALU.mult, op1=ALU.add))
            step(nc.vector.tensor_scalar(starts[:], starts[:], float(EP), None, ALU.min))
            step(nc.vector.tensor_copy(start[:], starts[0:1, :]))
        step(nc.vector.tensor_copy(tot[:], k.ps[:, 1, 0:NT]))
        step(nc.vector.tensor_tensor_scan(off[:], k.ones_e[:, 0:NT], tot[:], -1.0, ALU.mult, ALU.add))
        step(nc.vector.tensor_tensor(off[:], off[:], tot[:], ALU.subtract))
        step(nc.vector.tensor_tensor(off[:], off[:], k.ps[:, 2, 0:NT], ALU.add))
        step(nc.vector.memset(pos[:], 0.0))
        for b in range(NT):
            step(nc.vector.tensor_scalar(part[:], bkt[:], float(b), None, ALU.is_equal))
            step(nc.vector.tensor_tensor_scan(scan[:], k.ones_e[:], part[:], off[:, b:b + 1], ALU.mult, ALU.add))
            step(nc.vector.tensor_tensor(part[:], part[:], scan[:], ALU.mult))
            step(nc.vector.tensor_tensor(pos[:], pos[:], part[:], ALU.add))
        step(nc.vector.tensor_copy(k.pos_i[:], pos[:]))
        rec = k.edge_rec[:].rearrange("p (j c) -> p j c", c=2)
        step(nc.vector.tensor_copy(rec[:, :, 0], k.dst_i[:]))
        step(nc.vector.tensor_copy(rec[:, :, 1].bitcast(F32), src_f[:]))

    def total(pe):
        for n in range(2):
            pe.wait_ge(counted, n + 1)
            if n:
                pe.wait_ge(table_ready, 1)
            nc.tensor.matmul(k.ps[0:NT, 0, 0:1], counts[:], k.ones[:, 0:1], start=True, stop=True)
            nc.tensor.matmul(k.ps[:, 1, 0:NT], k.ones[:], counts[:], start=True, stop=True)
            nc.tensor.matmul(k.ps[:, 2, 0:NT], k.tri_strict[:], counts[:], start=True,
                             stop=True).then_inc(summed, 1)
            pe.wait_ge(tiles_ready, n + 1)
            nc.tensor.matmul(k.ps[0:NT, 3, 0:1], k.tri_incl[0:NT, 0:NT], small[0:NT, 1:2], start=True,
                             stop=True).then_inc(cum_ready, 1)
            pe.wait_ge(grid_ready, n + 1)
            nc.tensor.matmul(k.ps[:, 4, 0:ST], k.ones[0:NT, :], grid[:], start=True, stop=True)
            nc.tensor.matmul(k.ps[:, 5, 0:ST], vrow[:], grid[:], start=True,
                             stop=True).then_inc(table_ready, 1)

    return number, count, total


def gat_tables(k):
    nc, t = k.nc, k.t
    ctx, sb, sem = phase(k)
    C = 2 * D + 2 * H1
    with ctx:
        w_lin_t, w_gat = sb("w_lin_t", [P, KC, D]), sb("w_gat", [P, KC, D])
        b_col = sb("b_col", [P, KC])
        att = sb("att", [P, KC, 2 * H1])
        fused_t = sb("fused_t", [P, KC, D])
        w_all = sb("w_all", [P, KC, C])
        bias_row = sb("bias_row", [1, C])
        bias_col = sb("bias_col", [P, KC])
        bias = sb("bias", [P, C])
        st, mv = sb("st", [P, NT * 6]), sb("mv", [P, 5, NT])
        xn, xt = sb("xn", [P, 4, D]), sb("xt", [P, 4, D])
        out = sb("out", [P, 4, D + H1])
        loaded, zeroed = sem("loaded"), sem("zeroed")
        dve_step, stats_ready, sqrt_ready = sem("dve_step"), sem("stats_ready"), sem("sqrt_ready")
        fused, copied, w_ready = sem("fused"), sem("copied"), sem("w_ready")
        normed, turned, turned_copied, product, summed, added = (
            sem(s) for s in ("normed", "turned", "turned_copied", "product", "summed", "added"))
        stored = [sem(f"stored{o}") for o in range(4)]
        sender = Sender(k, sb, sem)

        with nc.Block() as block:
            @block.sync
            def _(sp):
                load_weights(k, sp, loaded, [
                    (w_lin_t[:], chunks(t["w_lin_t"])), (w_gat[:], chunks(t["w_gat"])),
                    (b_col[:], t["b_lin_cols"]),
                    (w_all[:, :, 0:D], chunks(t["w_lin"])), (bias_row[:, 0:D], row(t["b_lin"]))])
                sp.wait_ge(zeroed, 1)
                for n, a in enumerate((t["attn_l"], t["attn_r"])):
                    for h in range(H1):
                        p0 = (h * HD) % P
                        sp.dma_start(att[p0:p0 + HD, h * HD // P, n * H1 + h:n * H1 + h + 1],
                                     a[h, :].rearrange("(d a) -> d a", a=1)).then_inc(loaded, 16)

                def store(i, o):
                    sp.wait_ge(added, i + 1)
                    sp.dma_start(t["gat_rows"][bass.ts(i, P), :], out[:, o, 0:D]).then_inc(stored[o], 16)
                    sp.dma_start(t["el_rows"][bass.ts(i, P), :], out[:, o, D:]).then_inc(stored[o], 16)

                staggered(sp, [(store, 0)])
                for o in range(4):
                    sp.wait_ge(stored[o], 32 * len(range(o, NT, 4)))

            @block.gpsimd
            def _(pool):
                nc.gpsimd.memset(att[:], 0.0).then_inc(zeroed, 1)

            @block.vector
            def _(dve):
                step = Steps(dve, dve_step)
                emit_norm(k, dve, st, mv, stats_ready, sqrt_ready, step)
                dve.wait_ge(fused, 1)
                nc.vector.tensor_copy(fused_t[:], k.ps[:, 0:KC, 0:D]).then_inc(copied, 1)
                nc.vector.tensor_copy(w_all[:, :, D:2 * D], k.ps[:, 2:2 + KC, 0:D]).then_inc(copied, 1)
                nc.vector.tensor_copy(bias_row[:, D:2 * D], k.ps[0:1, 4, 0:D]).then_inc(copied, 1)
                nc.vector.tensor_copy(bias_col[:], k.ps[:, 5:5 + KC, 0]).then_inc(copied, 1)
                dve.wait_ge(fused, 2)
                nc.vector.tensor_copy(w_all[:, :, 2 * D:], k.ps[:, 0:KC, 0:2 * H1]).then_inc(copied, 1)
                nc.vector.tensor_copy(bias_row[:, 2 * D:], k.ps[0:1, 4, 0:2 * H1]).then_inc(copied, 1)
                dve.wait_ge(fused, 3)
                nc.vector.tensor_copy(bias[:, 0:ED], k.ps[:, 0, :]).then_inc(copied, 1)
                nc.vector.tensor_copy(bias[:, ED:C], k.ps[:, 1, 0:C - ED]).then_inc(w_ready, 1)
                dve.wait_ge(w_ready, 1)
                dve.wait_ge(copied, 7)

                def norm_row(i, o):
                    if not isinstance(i, int) or i >= 4:
                        dve.wait_ge(turned, i - 3)
                    nc.vector.tensor_scalar(xn[:, o, :], k.xs[:, bass.ts(i, D)], mv[:, 0, bass.ds(i, 1)],
                                            mv[:, 4, bass.ds(i, 1)], ALU.subtract, ALU.mult).then_inc(normed, 1)

                def leave(i, o):
                    bank, xsl = 2 + 2 * (o % 2), k.xs[:, bass.ts(i, D)]
                    dve.wait_ge(product, i + 1)
                    nc.vector.tensor_tensor(xsl, xsl, k.ps[:, bank, 0:D], ALU.add).then_inc(summed, 1)
                    if not isinstance(i, int) or i >= 4:
                        dve.wait_ge(stored[o], (i - o) * 8)
                    nc.vector.tensor_tensor(out[:, o, 0:D], k.ps[:, bank, D:2 * D], bias[:, D:2 * D], ALU.add)
                    nc.vector.tensor_tensor(out[:, o, D:], k.ps[:, bank + 1, 0:H1], bias[:, 2 * D:2 * D + H1], ALU.add)
                    nc.vector.tensor_tensor(k.er[:, bass.ts(i, H1)], k.ps[:, bank + 1, H1:2 * H1],
                                            bias[:, 2 * D + H1:], ALU.add)
                    dve.wait_ge(summed, i + 1)
                    nc.vector.tensor_tensor(xsl, xsl, bias[:, 0:D], ALU.add).then_inc(added, 1)

                staggered(dve, [(norm_row, 0), (leave, 2)])

            @block.scalar
            def _(act):
                emit_sqrt(k, act, mv, stats_ready, sqrt_ready)

                def keep_turned(i, o):
                    act.wait_ge(turned, i + 1)
                    if not isinstance(i, int) or i >= 4:
                        act.wait_ge(product, i - 3)
                    nc.scalar.copy(xt[:, o, :], k.ps[:, o % 2, 0:D]).then_inc(turned_copied, 1)

                staggered(act, [(keep_turned, 0)])

            @block.tensor
            def _(pe):
                pe.wait_ge(loaded, 16 * (5 + 2 * H1))
                for m in range(KC):
                    for c in range(KC):
                        nc.tensor.matmul(k.ps[:, m, 0:D], w_gat[:, c, bass.ts(m, P)], w_lin_t[:, c, :],
                                         start=c == 0, stop=c == KC - 1)
                for m in range(KC):
                    for c in range(KC):
                        nc.tensor.matmul(k.ps[:, 2 + m, 0:D], w_lin_t[:, c, bass.ts(m, P)], w_gat[:, c, :],
                                         start=c == 0, stop=c == KC - 1)
                for c in range(KC):
                    nc.tensor.matmul(k.ps[0:1, 4, 0:D], b_col[:, c:c + 1], w_gat[:, c, :],
                                     start=c == 0, stop=c == KC - 1)
                for m in range(KC):
                    for c in range(KC):
                        last = nc.tensor.matmul(k.ps[:, 5 + m, 0:1], w_gat[:, c, bass.ts(m, P)], b_col[:, c:c + 1],
                                                start=c == 0, stop=c == KC - 1)
                last.then_inc(fused, 1)
                pe.wait_ge(copied, 4)
                for m in range(KC):
                    for c in range(KC):
                        nc.tensor.matmul(k.ps[:, m, 0:2 * H1], fused_t[:, c, bass.ts(m, P)], att[:, c, :],
                                         start=c == 0, stop=c == KC - 1)
                for c in range(KC):
                    last = nc.tensor.matmul(k.ps[0:1, 4, 0:2 * H1], bias_col[:, c:c + 1], att[:, c, :],
                                            start=c == 0, stop=c == KC - 1)
                last.then_inc(fused, 1)
                pe.wait_ge(copied, 6)
                nc.tensor.matmul(k.ps[:, 0, :], k.ones[0:1, :], bias_row[:, 0:ED], start=True, stop=True)
                nc.tensor.matmul(k.ps[:, 1, 0:C - ED], k.ones[0:1, :], bias_row[:, ED:C], start=True,
                                 stop=True).then_inc(fused, 1)
                pe.wait_ge(w_ready, 1)

                def turn(i, o):
                    pe.wait_ge(normed, i + 1)
                    if not isinstance(i, int) or i >= 2:
                        pe.wait_ge(turned_copied, i - 1)
                    for c in range(KC):
                        last = nc.tensor.transpose(k.ps[:, o % 2, bass.ts(c, P)], xn[:, o, bass.ts(c, P)], k.ident[:])
                    last.then_inc(turned, 1)

                def project(i, o):
                    bank = 2 + 2 * (o % 2)
                    pe.wait_ge(turned_copied, i + 1)
                    if not isinstance(i, int) or i >= 2:
                        pe.wait_ge(added, i - 1)
                    for c in range(KC):
                        nc.tensor.matmul(k.ps[:, bank, :], xt[:, o, bass.ts(c, P)], w_all[:, c, 0:2 * D],
                                         start=c == 0, stop=c == KC - 1)
                    for c in range(KC):
                        last = nc.tensor.matmul(k.ps[:, bank + 1, 0:2 * H1], xt[:, o, bass.ts(c, P)],
                                                w_all[:, c, 2 * D:], start=c == 0, stop=c == KC - 1)
                    last.then_inc(product, 1)

                staggered(pe, [(turn, 0), (project, 1)])


def gat_scores(k):
    nc, t = k.nc, k.t
    ctx, sb, sem = phase(k)
    W = 14
    with ctx:
        number, count, total = edge_tables(k, sb, sem)
        el = sb("el", [P, EC * H1])
        fwd, bwd = sb("fwd", [P, EC * H1]), sb("bwd", [P, EC * H1])
        rec = sb("rec", [P, EC * RW], I32)
        cut = sb("cut", [P, EC + 1])
        index, got = sb("index", [P, 2, W], I32), sb("got", [P, 2, W, H1])
        ends = sb("ends", [P, 4, H1])
        turned = sb("turned", [H1, 4, P])
        line = sb("line", [H1, 6, P])
        carry = sb("carry", [P, 2, H1])
        staged, unloaded, step_sem, started = sem("staged"), sem("unloaded"), sem("step"), sem("started")
        landed = [sem("landed0"), sem("landed1")]
        ends_ready, ends_turned, line_ready, line_turned = (
            sem(s) for s in ("ends_ready", "ends_turned", "line_ready", "line_turned"))
        rec_ready, stored = sem("rec_ready"), sem("stored")

        with nc.Block() as block:
            @block.gpsimd
            def _(pool):
                number(pool)
                with pool.Fori(0, EC // W // 2) as g:
                    for s in range(2):
                        c = 2 * g + s
                        pool.wait_ge(unloaded, c + 1)
                        nc.gpsimd.tensor_copy(index[:, s, :], k.src_i[:, bass.ts(c, W)]).then_inc(staged, 1)
                        pool.wait_ge(staged, c + 1)
                        pool.sem_inc(started, 1)
                        for j in range(W):
                            nc.gpsimd.indirect_dma_start(
                                got[:, s, j, :], None, t["el_rows"][:, :],
                                bass.IndirectOffsetOnAxis(ap=index[:, s, j:j + 1], axis=0)).then_inc(landed[s], 16)

            @block.scalar
            def _(act):
                act.sem_inc(unloaded, 2)
                with act.Fori(0, EC // W // 2) as g:
                    for s in range(2):
                        c = 2 * g + s
                        act.wait_ge(landed[s], 16 * W * (g + 1))
                        nc.scalar.copy(el[:, bass.ts(c, W * H1)],
                                       got[:, s, :, :].rearrange("p j h -> p (j h)")).then_inc(unloaded, 1)
                act.wait_ge(unloaded, 2 + EC // W)
                nc.scalar.copy(rec[:].rearrange("p (j c) -> p j c", c=RW)[:, :, 2:2 + H1].bitcast(F32),
                               el[:].rearrange("p (j h) -> p j h", h=H1)).then_inc(rec_ready, 1)

            @block.vector
            def _(dve):
                count(dve)
                step = Steps(dve, step_sem)
                rec3 = rec[:].rearrange("p (j c) -> p j c", c=RW)
                nc.vector.tensor_copy(rec3[:, :, 0], k.src_i[:]).then_inc(rec_ready, 1)
                nc.vector.tensor_copy(rec3[:, :, 1].bitcast(F32), k.dst_f[:]).then_inc(rec_ready, 1)
                step(nc.vector.memset(cut[:], 0.0))
                step(nc.vector.tensor_tensor(cut[:, 1:EC], k.dst_f[:, 1:EC], k.dst_f[:, 0:EC - 1], ALU.is_equal))
                step(nc.vector.tensor_scalar(cut[:], cut[:], -1.0, BIG, ALU.add, ALU.mult))
                for n, j in ((2, 0), (3, EC - 1)):
                    step(nc.vector.tensor_scalar(ends[:, n, :], k.ones[:, 0:H1], k.dst_f[:, j:j + 1], None, ALU.mult))
                dve.wait_ge(unloaded, 2 + EC // W)
                f3, b3, e3 = (a[:].rearrange("p (j h) -> p j h", h=H1) for a in (fwd, bwd, el))

                def scans(first, second):
                    for h in range(H1):
                        nc.vector.tensor_tensor_scan(f3[:, :, h], cut[:, 0:EC], e3[:, :, h], first(h), ALU.add, ALU.max)
                        last = nc.vector.tensor_tensor_scan(b3[:, ::-1, h], cut[:, 1:EC + 1][:, ::-1],
                                                            e3[:, ::-1, h], second(h), ALU.add, ALU.max)
                    step(last)

                scans(lambda h: -BIG, lambda h: -BIG)
                nc.vector.tensor_copy(ends[:, 0, :], f3[:, EC - 1, :])
                nc.vector.tensor_copy(ends[:, 1, :], b3[:, 0, :]).then_inc(ends_ready, 1)
                dve.wait_ge(ends_turned, 1)
                step(nc.vector.tensor_copy(turned[:], k.ps[0:H1, 0:4, 0:P]))
                tail, head, first, final = (turned[:, n, :] for n in range(4))
                linked, reach, back, run, cin, cout = (line[:, n, :] for n in range(6))
                step(nc.vector.memset(line[:], 0.0))
                step(nc.vector.tensor_tensor(linked[:, 1:P], final[:, 0:P - 1], first[:, 1:P], ALU.is_equal))
                step(nc.vector.tensor_tensor(run, first, final, ALU.is_equal))
                step(nc.vector.tensor_tensor(reach, run, linked, ALU.mult))
                step(nc.vector.tensor_tensor(back[:, 0:P - 1], run[:, 0:P - 1], linked[:, 1:P], ALU.mult))
                step(nc.vector.tensor_scalar(line[:, 0:3, :], line[:, 0:3, :], -1.0, BIG, ALU.add, ALU.mult))
                step(nc.vector.tensor_tensor_scan(run, reach, tail, -BIG, ALU.add, ALU.max))
                step(nc.vector.memset(cin, -BIG))
                step(nc.vector.tensor_tensor(cin[:, 1:P], run[:, 0:P - 1], linked[:, 1:P], ALU.add))
                step(nc.vector.tensor_tensor_scan(run[:, ::-1], back[:, ::-1], head[:, ::-1], -BIG, ALU.add, ALU.max))
                step(nc.vector.memset(cout, -BIG))
                nc.vector.tensor_tensor(cout[:, 0:P - 1], run[:, 1:P], linked[:, 1:P], ALU.add).then_inc(line_ready, 1)
                dve.wait_ge(line_turned, 1)
                step(nc.vector.tensor_copy(carry[:], k.ps[:, 4:6, 0:H1]))
                step(nc.vector.memset(cut[:, 0:1], 0.0))
                step(nc.vector.memset(cut[:, EC:EC + 1], 0.0))
                scans(lambda h: carry[:, 0, h:h + 1], lambda h: carry[:, 1, h:h + 1])
                nc.vector.tensor_tensor(rec3[:, :, 2 + H1:].bitcast(F32), f3, b3, ALU.max).then_inc(rec_ready, 1)

            @block.tensor
            def _(pe):
                total(pe)
                pe.wait_ge(ends_ready, 1)
                for n in range(4):
                    last = nc.tensor.transpose(k.ps[0:H1, n, 0:P], ends[:, n, :], k.ident[:])
                last.then_inc(ends_turned, 1)
                pe.wait_ge(line_ready, 1)
                for n in range(2):
                    last = nc.tensor.transpose(k.ps[:, 4 + n, 0:H1], line[:, 4 + n, :], k.ident[0:H1, 0:H1])
                last.then_inc(line_turned, 1)

            @block.sync
            def _(sp):
                sp.wait_ge(rec_ready, 4)
                sp.dma_start(t["rec_gat"][0:EP, :].rearrange("(p j) c -> p (j c)", p=P), rec[:]).then_inc(stored, 16)
                sp.wait_ge(stored, 16)


BATCH = 4
BSETS = 8
SLOTS = BATCH * BSETS
BODIES = ST // SLOTS
assert BODIES * SLOTS == ST and BODIES > 2


def bodies(engine, body):
    body(0, True, False)
    with engine.Fori(1, BODIES - 1) as g:
        body(g, False, False)
    body(BODIES - 1, False, True)


def gat_edges(k):
    nc, t = k.nc, k.t
    ctx, sb, sem = phase(k)
    W = D + H1
    with ctx:
        acc = sb("acc", [P, NT * W])
        rec, rows = sb("rec", [P, SLOTS, RW], I32), sb("rows", [P, SLOTS, D])
        hot, hot_t = sb("hot", [P, SLOTS, P]), sb("hot_t", [P, 2, BATCH, P])
        places = sb("places", [P, 2, BATCH])
        score = sb("score", [P, 2, BATCH, 2, H1])
        msg = sb("msg", [P, BSETS, BATCH, W])
        bias, top = sb("bias", [P, D]), sb("top", [P, 2, D])
        den = sb("den", [P, NT * H1])
        sender = Sender(k, sb, sem)
        rec_landed = [sem(f"rec_landed{s}") for s in range(SLOTS)]
        row_landed = [sem(f"row_landed{s}") for s in range(SLOTS)]
        started, loaded, step_sem = sem("started"), sem("loaded"), sem("step")
        placed, hot_made, hot_turned, hot_copied, expanded, scored, shifted, raised, weighted, exp_done, multiplied, added = (
            sem(s) for s in ("placed", "hot_made", "hot_turned", "hot_copied", "expanded", "scored", "shifted", "raised",
                             "weighted", "exp_done", "multiplied", "added"))

        with nc.Block() as block:
            @block.sync
            def _(sp):
                sp.dma_start(bias[:], across(t["gat_bias"])).then_inc(loaded, 16)
                with sp.Fori(0, BODIES) as g:
                    for part in range(SLOTS // 8):
                        _, start = nc.values_load_multi_w_load_instructions(
                            k.start_dst[0:1, bass.ds(g * SLOTS + part * 8, 8)], engines=(SP,), min_val=0, max_val=EP)
                        for n in range(8):
                            s = part * 8 + n
                            sp.wait_ge(weighted, g * SLOTS + s + 1)
                            sp.dma_start(rec[:, s, :], t["rec_gat"][bass.ds(start[n], P), :]).then_inc(rec_landed[s], 16)

            @block.gpsimd
            def _(pool):
                with pool.Fori(0, BODIES) as g:
                    for s in range(SLOTS):
                        pool.wait_ge(rec_landed[s], 16 * (g + 1))
                        pool.sem_inc(started, 1)
                        nc.gpsimd.indirect_dma_start(
                            rows[:, s, :], None, t["gat_rows"][:, :],
                            bass.IndirectOffsetOnAxis(ap=rec[:, s, 0:1], axis=0)).then_inc(row_landed[s], 16)
                    send_part(pool, sender, t["rec_src"], g)
                parts = (SENT_BY_GAT[1] - SENT_BY_GAT[0]) * SEND // PART
                with pool.Fori(BODIES, parts) as g:
                    send_part(pool, sender, t["rec_src"], g)
                pool.wait_ge(sender.sent[0], 16 * PART * parts)

            @block.vector
            def _(dve):
                step = Steps(dve, step_sem)
                dve.sem_inc(weighted, SLOTS)
                step(nc.vector.memset(acc[:], 0.0))

                def find_places(g, c):
                    B, s0 = g * BSETS + c, c * BATCH
                    for s in range(s0, s0 + BATCH):
                        dve.wait_ge(rec_landed[s], 16 * (g + 1))
                    nc.vector.tensor_tensor(places[:, c % 2, :], rec[:, s0:s0 + BATCH, 1].bitcast(F32),
                                            k.base_dst[:, bass.ds(B * BATCH, BATCH)], ALU.subtract).then_inc(placed, 1)

                def one_hots(g, c):
                    B, s0 = g * BSETS + c, c * BATCH
                    if not (isinstance(g, int) and g == 0):
                        dve.wait_ge(multiplied, (B - BSETS + 1) * BATCH)
                    dve.wait_ge(placed, B + 1)
                    nc.vector.tensor_tensor(hot[:, s0:s0 + BATCH, :],
                                            k.iota[:].unsqueeze(1).to_broadcast([P, BATCH, P]),
                                            places[:, c % 2, :].unsqueeze(2).to_broadcast([P, BATCH, P]),
                                            ALU.is_equal).then_inc(hot_made, 1)

                def scores(g, c, part):
                    B = g * BSETS + c
                    now, s0 = score[:, c % 2], c * BATCH
                    if part == 0:
                        dve.wait_ge(expanded, B + 1)
                        nc.vector.tensor_tensor(
                            now, rec[:, s0:s0 + BATCH, 2:].bitcast(F32).rearrange("p a (b h) -> p a b h", h=H1),
                            k.ps[:, 2 + c % 2, 0:BATCH * H1].rearrange(
                                "p (a h) -> p a h", h=H1).unsqueeze(2).to_broadcast([P, BATCH, 2, H1]),
                            ALU.add).then_inc(scored, 1)
                    elif part == 1:
                        dve.wait_ge(scored, B + 1)
                        nc.vector.scalar_tensor_tensor(out=now, in0=now, scalar=0.2, in1=now, op0=ALU.mult,
                                                       op1=ALU.max).then_inc(raised, 1)
                    elif part == 2:
                        dve.wait_ge(raised, B + 1)
                        nc.vector.tensor_tensor(now[:, :, 0, :], now[:, :, 0, :], now[:, :, 1, :],
                                                ALU.subtract).then_inc(shifted, 1)

                def weigh_rows(g, c, n):
                    s = c * BATCH + n
                    if n == 0:
                        dve.wait_ge(exp_done, g * BSETS + c + 1)
                    dve.wait_ge(row_landed[s], 16 * (g + 1))
                    dve.wait_ge(row_landed[s + 1], 16 * (g + 1))
                    nc.vector.tensor_tensor(
                        msg[:, c, n:n + 2, 0:D].rearrange("p a (h d) -> p a h d", d=HD),
                        rows[:, s:s + 2, :].rearrange("p a (h d) -> p a h d", d=HD),
                        msg[:, c, n:n + 2, D:].unsqueeze(3).to_broadcast([P, 2, H1, HD]), ALU.mult).then_inc(weighted, 2)

                def add_sum(g, c, n, tile):
                    q = g * SLOTS + c * BATCH + n
                    dve.wait_ge(multiplied, q + 1)
                    dve.wait_ge(added, q)
                    sums = acc[:, bass.ds(tile[n] * W, W)]
                    nc.vector.tensor_tensor(sums, sums, k.ps[:, 4 + n, 0:W], ALU.add).then_inc(added, 1)

                def tiles(q):
                    return nc.values_load_multi_w_load_instructions(
                        k.tile_dst[0:1, bass.ds(q, BATCH)], engines=(DVE,), min_val=0, max_val=NT - 1)[1]

                def body(g, first, last):
                    if first:
                        for c in range(2):
                            find_places(0, c)
                            one_hots(0, c)
                        find_places(0, 2)
                        for part in range(3):
                            scores(0, 0, part)
                    for c in range(BSETS):
                        before = (g, c - 2) if c >= 2 else None if first else (g - 1, c + BSETS - 2)
                        ahead = (g, c + 2) if c < BSETS - 2 else None if last else (g + 1, c + 2 - BSETS)
                        scored_next = (g, c + 1) if c < BSETS - 1 else None if last else (g + 1, 0)
                        placed_next = (g, c + 3) if c < BSETS - 3 else None if last else (g + 1, c + 3 - BSETS)
                        if before:
                            tile = tiles(before[0] * SLOTS + before[1] * BATCH)
                        if ahead:
                            one_hots(*ahead)
                        for n in range(BATCH):
                            if before:
                                add_sum(*before, n, tile)
                            if scored_next:
                                scores(*scored_next, n)
                        weigh_rows(g, c, 0)
                        if placed_next:
                            find_places(*placed_next)
                        weigh_rows(g, c, 2)
                    if last:
                        for c in (BSETS - 2, BSETS - 1):
                            tile = tiles(g * SLOTS + c * BATCH)
                            for n in range(BATCH):
                                add_sum(g, c, n, tile)

                bodies(dve, body)
                dve.wait_ge(added, ST)
                dve.wait_ge(loaded, 16)
                acc3 = acc[:].rearrange("p (i c) -> p i c", c=W)
                den3 = den[:].rearrange("p (i h) -> p i h", h=H1)
                step(nc.vector.tensor_scalar(den3, acc3[:, :, D:], 1e-30, None, ALU.max))
                step(nc.vector.reciprocal(den[:], den[:]))
                base = step.n
                for i in range(NT):
                    a, xsl, y = acc3[:, i, 0:D], k.xs[:, bass.ts(i, D)], top[:, i % 2, :]
                    step(nc.vector.tensor_tensor(
                        a.rearrange("p (h d) -> p h d", d=HD), a.rearrange("p (h d) -> p h d", d=HD),
                        den3[:, i, :].unsqueeze(2).to_broadcast([P, H1, HD]), ALU.mult))
                    step(nc.vector.tensor_tensor(a, a, bias[:], ALU.add))
                    step(nc.vector.scalar_tensor_tensor(out=y, in0=a, scalar=0.01, in1=a, op0=ALU.mult, op1=ALU.max))
                    step(nc.vector.tensor_tensor(xsl, xsl, y, ALU.add))

            @block.scalar
            def _(act):
                def copy_turned(g, c):
                    B = g * BSETS + c
                    act.wait_ge(hot_turned, B + 1)
                    if not (isinstance(g, int) and g == 0 and c < 2):
                        act.wait_ge(expanded, B - 1)
                    nc.scalar.copy(hot_t[:, c % 2, :, :], k.ps[:, c % 2, :].rearrange(
                        "p (a b) -> p a b", b=P)).then_inc(hot_copied, 1)

                def weights(g, c):
                    B = g * BSETS + c
                    act.wait_ge(shifted, B + 1)
                    if not (isinstance(g, int) and g == 0):
                        act.wait_ge(multiplied, (B - BSETS + 1) * BATCH)
                    nc.scalar.activation(msg[:, c, :, D:], score[:, c % 2, :, 0, :], ACT.Exp).then_inc(exp_done, 1)

                def body(g, first, last):
                    if first:
                        copy_turned(0, 0)
                        copy_turned(0, 1)
                        weights(0, 0)
                    for c in range(BSETS):
                        if c < BSETS - 2:
                            copy_turned(g, c + 2)
                        elif not last:
                            copy_turned(g + 1, c + 2 - BSETS)
                        if c < BSETS - 1:
                            weights(g, c + 1)
                        elif not last:
                            weights(g + 1, 0)

                bodies(act, body)

            @block.tensor
            def _(pe):
                def turn(g, c):
                    B = g * BSETS + c
                    pe.wait_ge(hot_made, B + 1)
                    if not (isinstance(g, int) and g == 0 and c < 2):
                        pe.wait_ge(hot_copied, B - 1)
                    for n in range(BATCH):
                        last = nc.tensor.transpose(k.ps[:, c % 2, bass.ts(n, P)], hot[:, c * BATCH + n, :], k.ident[:])
                    last.then_inc(hot_turned, 1)

                def expand(g, c, tile):
                    B = g * BSETS + c
                    pe.wait_ge(hot_copied, B + 1)
                    if not (isinstance(g, int) and g == 0 and c < 2):
                        pe.wait_ge(scored, B - 1)
                    for n in range(BATCH):
                        last = nc.tensor.matmul(k.ps[:, 2 + c % 2, bass.ts(n, H1)], hot_t[:, c % 2, n, :],
                                                k.er[:, bass.ds(tile[n] * H1, H1)], start=True, stop=True)
                    last.then_inc(expanded, 1)

                def multiply(g, c):
                    B = g * BSETS + c
                    pe.wait_ge(weighted, (B + 1) * BATCH + SLOTS)
                    for n in range(BATCH):
                        if not (isinstance(g, int) and g == 0 and c == 0):
                            pe.wait_ge(added, (B - 1) * BATCH + n + 1)
                        nc.tensor.matmul(k.ps[:, 4 + n, 0:W], hot[:, c * BATCH + n, :], msg[:, c, n, :],
                                         start=True, stop=True).then_inc(multiplied, 1)

                def tiles(q):
                    return nc.values_load_multi_w_load_instructions(
                        k.tile_dst[0:1, bass.ds(q, BATCH)], engines=(PE,), min_val=0, max_val=NT - 1)[1]

                def body(g, first, last):
                    if first:
                        turn(0, 0)
                        turn(0, 1)
                        expand(0, 0, tiles(0))
                    for c in range(BSETS):
                        if c < BSETS - 1:
                            expand(g, c + 1, tiles(g * SLOTS + (c + 1) * BATCH))
                        elif not last:
                            expand(g + 1, 0, tiles(g * SLOTS + SLOTS))
                        if c < BSETS - 2:
                            turn(g, c + 2)
                        elif not last:
                            turn(g + 1, c + 2 - BSETS)
                        if c:
                            multiply(g, c - 1)
                        elif not first:
                            multiply(g - 1, BSETS - 1)
                    if last:
                        multiply(g, BSETS - 1)

                bodies(pe, body)


def slice_attention(k):
    nc, t = k.nc, k.t
    ctx, sb, sem = phase(k)
    PD = 2 * SD
    with ctx:
        w_fx, w_sl = sb("w_fx", [P, KC, SI]), sb("w_sl", [P, KC, SI])
        w_x_t = sb("w_x_t", [SD, SH, D])
        w_slice, b_x = sb("w_slice", [SD, SD]), sb("b_x", [SD, SH])
        w_two = [sb(f"w_{n}2", [PD, PD]) for n in ("q", "k", "v")]
        w_out, fold = sb("w_out", [PD, PAIRS, D]), sb("fold", [PD, PAIRS, D])
        b_fx, b_out, b_sl = sb("b_fx", [P, SI]), sb("b_out", [P, D]), sb("b_sl", [P, SI])
        b_slice = sb("b_slice", [SH, SD])
        sl_row = sb("sl_row", [SH, SD])
        temp = sb("temp", [P, SH])
        st, mv = sb("st", [P, NT * 6]), sb("mv", [P, 5, NT])
        xn, xt = sb("xn", [P, 4, D]), sb("xt", [P, 4, D])
        soft, fx = sb("soft", [P, 4, SI]), sb("fx", [P, 4, PAIRS, PD + 1])
        peak, total = sb("peak", [P, 4, SH]), sb("total", [P, 4, SH])
        soft_t = k.large[:, 0:PAIRS * NP].rearrange("p (a n) -> p a n", n=NP)
        piece = sb("piece", [P, U, SI])
        zero = sb("zero", [1, 2 * (PD + 1)])
        token, norm = sb("token", [PD, PAIRS, PD]), sb("norm", [PD, PAIRS])
        token_t, q_t, k_t, v = (sb(n, [PD, PAIRS, PD]) for n in ("token_t", "q_t", "k_t", "v"))
        att, att_t, mix_t = (sb(n, [PD, PAIRS, PD]) for n in ("att", "att_t", "mix_t"))
        high, mass = sb("high", [PD, PAIRS]), sb("mass", [PD, PAIRS])
        sender = Sender(k, sb, sem)
        S = {n: sem(n) for n in (
            "loaded", "zeroed", "dve_step", "act_step", "stats_ready", "sqrt_ready", "fused", "copied", "bias_out",
            "bias_in", "w_ready", "normed", "turned", "turned_copied", "product", "scored", "raised", "weighed",
            "tokens", "soft_turned", "soft_kept", "fixed", "mid_pe", "mid_dve", "mid_act", "cut", "result",
            "added", "peaked", "summed")}
        HALVES = ((0, SD), (SD, PD))

        with nc.Block() as block:
            @block.sync
            def _(sp):
                n = load_weights(k, sp, S["loaded"], [
                    (w_fx[:], chunks(t["w_fx"])), (w_x_t[:], t["w_x_t"].rearrange("(h c) n -> c h n", c=SD)),
                    (w_slice[:], t["w_slice"]), (b_x[:], t["b_x_cols"]), (w_out[:], chunks(t["w_out"])),
                    (b_fx[:], across(t["b_fx"])), (b_out[:], across(t["b_out"])),
                    (b_slice[:], row(t["b_slice"]).to_broadcast([SH, SD])), (temp[:], across(t["temp"]))])
                sp.wait_ge(S["zeroed"], 4)
                for w2, w in zip(w_two, (t["w_q"], t["w_k"], t["w_v"])):
                    for a, b in HALVES:
                        sp.dma_start(w2[a:b, a:b], w).then_inc(S["loaded"], 16)
                sp.wait_ge(S["copied"], 1)
                sp.dma_start(t["slice_bias"], sl_row[:]).then_inc(S["bias_out"], 16)
                sp.wait_ge(S["bias_out"], 16)
                sp.dma_start(b_sl[:], row(t["slice_bias"].rearrange("h g -> (h g)")).to_broadcast(
                    [P, SI])).then_inc(S["bias_in"], 16)

            @block.gpsimd
            def _(pool):
                for w2 in w_two:
                    nc.gpsimd.memset(w2[:], 0.0).then_inc(S["zeroed"], 1)
                nc.gpsimd.memset(zero[:], 0.0).then_inc(S["zeroed"], 1)
                send_edges(pool, sender, t["rec_src"], *SENT_BY_SLICES)

            @block.vector
            def _(dve):
                step = Steps(dve, S["dve_step"])
                emit_norm(k, dve, st, mv, S["stats_ready"], S["sqrt_ready"], step)
                dve.wait_ge(S["loaded"], 16 * 15)
                step(nc.vector.tensor_scalar(temp[:], temp[:], 0.1, 5.0, ALU.max, ALU.min))
                step(nc.vector.reciprocal(temp[:], temp[:]))
                dve.wait_ge(S["fused"], 1)
                nc.vector.tensor_tensor(sl_row[:], k.ps[0:SH, 2, 0:SD], b_slice[:], ALU.add).then_inc(S["copied"], 1)
                for c in range(KC):
                    last = nc.vector.tensor_tensor(
                        w_sl[:, c, :].rearrange("p (h g) -> p h g", g=SD),
                        k.ps[:, c, :].rearrange("p (h g) -> p h g", g=SD),
                        temp[:].unsqueeze(2).to_broadcast([P, SH, SD]), ALU.mult)
                last.then_inc(S["w_ready"], 1)
                nc.vector.memset(fx[:, :, :, PD:], 1.0).then_inc(S["fixed"], 1)
                nc.vector.memset(token[:], 0.0).then_inc(S["fixed"], 1)
                nc.vector.memset(att[:], 0.0).then_inc(S["fixed"], 1)
                dve.wait_ge(S["fixed"], 3)
                dve.wait_ge(S["bias_in"], 16)
                step(nc.vector.tensor_tensor(
                    b_sl[:].rearrange("p (h g) -> p h g", g=SD), b_sl[:].rearrange("p (h g) -> p h g", g=SD),
                    temp[:].unsqueeze(2).to_broadcast([P, SH, SD]), ALU.mult))

                def norm_row(i, o):
                    if not isinstance(i, int) or i >= 4:
                        dve.wait_ge(S["turned"], i - 3)
                    nc.vector.tensor_scalar(xn[:, o, :], k.xs[:, bass.ts(i, D)], mv[:, 0, bass.ds(i, 1)],
                                            mv[:, 4, bass.ds(i, 1)], ALU.subtract, ALU.mult).then_inc(S["normed"], 1)

                def raise_scores(i, o):
                    s3, bank = soft[:, o, :].rearrange("p (h g) -> p h g", g=SD), 2 + o % 2 * 4
                    dve.wait_ge(S["product"], i + 1)
                    if not isinstance(i, int) or i >= 4:
                        dve.wait_ge(S["tokens"], i - 3)
                    nc.vector.tensor_tensor(soft[:, o, :], k.ps[:, bank + 1, :], b_sl[:], ALU.add).then_inc(S["peaked"], 1)
                    nc.vector.tensor_tensor(fx[:, o, :, 0:PD],
                                            k.ps[:, bank, :].rearrange("p (a b) -> p a b", b=PD),
                                            b_fx[:].rearrange("p (a b) -> p a b", b=PD), ALU.add).then_inc(S["scored"], 1)
                    dve.wait_ge(S["peaked"], 2 * i + 1)
                    nc.vector.tensor_reduce(peak[:, o, :], s3, AX, ALU.max).then_inc(S["peaked"], 1)
                    dve.wait_ge(S["peaked"], 2 * i + 2)
                    nc.vector.tensor_tensor(s3, s3, peak[:, o, :].unsqueeze(2).to_broadcast([P, SH, SD]),
                                            ALU.subtract).then_inc(S["raised"], 1)

                def divide(i, o):
                    s3 = soft[:, o, :].rearrange("p (h g) -> p h g", g=SD)
                    dve.wait_ge(S["weighed"], i + 1)
                    nc.vector.tensor_reduce(total[:, o, :], s3, AX, ALU.add).then_inc(S["summed"], 1)
                    dve.wait_ge(S["summed"], 2 * i + 1)
                    nc.vector.reciprocal(total[:, o, :], total[:, o, :]).then_inc(S["summed"], 1)
                    dve.wait_ge(S["summed"], 2 * i + 2)
                    nc.vector.scalar_tensor_tensor(
                        out=s3, in0=s3, scalar=k.mask[:, bass.ds(i, 1)],
                        in1=total[:, o, :].unsqueeze(2).to_broadcast([P, SH, SD]),
                        op0=ALU.mult, op1=ALU.mult).then_inc(S["cut"], 1)

                staggered(dve, [(norm_row, 0), (divide, 3), (raise_scores, 2)])
                step = Steps(dve, S["mid_dve"])
                dve.wait_ge(S["tokens"], NT)
                sums = k.ps[:, 4:6, 0:2 * (PD + 1)].rearrange("p b (r c) -> p b r c", c=PD + 1)
                step(nc.vector.tensor_scalar(norm[:].rearrange("p (b r) -> p b r", r=2), sums[:, :, :, PD], 1e-5, None,
                                             ALU.add))
                step(nc.vector.reciprocal(norm[:], norm[:]))
                for r in range(PAIRS):
                    for a, b in HALVES:
                        last = nc.vector.tensor_scalar(token[a:b, r, a:b], sums[a:b, r // 2, r % 2, a:b],
                                                       norm[a:b, r:r + 1], None, ALU.mult)
                step(last)

                def leave(n, out, bank):
                    dve.wait_ge(S["mid_pe"], n)
                    step(nc.vector.tensor_copy(out[:].rearrange("p a b -> p (a b)"), k.ps[:, bank, :]))

                leave(1, token_t, 0)
                dve.wait_ge(S["mid_pe"], 2)
                for out, bank in ((q_t, 1), (k_t, 2), (v, 3)):
                    step(nc.vector.tensor_copy(out[:].rearrange("p a b -> p (a b)"), k.ps[:, bank, :]))
                dve.wait_ge(S["mid_pe"], 3)
                scale = float(SD) ** -0.5
                for a, b in HALVES:
                    last = nc.vector.tensor_reduce(high[a:b, :], k.ps[a:b, 0, :].rearrange(
                        "p (r c) -> p r c", c=PD)[:, :, a:b], AX, ALU.max)
                step(last)
                for a, b in HALVES:
                    last = nc.vector.tensor_tensor(
                        att[a:b, :, a:b], k.ps[a:b, 0, :].rearrange("p (r c) -> p r c", c=PD)[:, :, a:b],
                        high[a:b, :].unsqueeze(2).to_broadcast([SD, PAIRS, SD]), ALU.subtract)
                step(last)
                dve.wait_ge(S["mid_act"], 1)
                for a, b in HALVES:
                    last = nc.vector.tensor_reduce(mass[a:b, :], att[a:b, :, a:b], AX, ALU.add)
                step(last)
                step(nc.vector.reciprocal(mass[:], mass[:]))
                step(nc.vector.tensor_tensor(att[:], att[:], mass[:].unsqueeze(2).to_broadcast([PD, PAIRS, PD]),
                                             ALU.mult))
                leave(4, att_t, 1)
                leave(5, mix_t, 2)
                dve.wait_ge(S["mid_pe"], 6)
                step(nc.vector.tensor_copy(fold[:, 0:2, :].rearrange("p a b -> p (a b)"), k.ps[:, 4, :]))
                step(nc.vector.tensor_copy(fold[:, 2:4, :].rearrange("p a b -> p (a b)"), k.ps[:, 5, :]))
                with dve.Fori(0, GROUPS) as g:
                    for u in range(U):
                        i = g * U + u
                        dve.wait_ge(S["result"], i + 1)
                        xsl = k.xs[:, bass.ts(i, D)]
                        nc.vector.tensor_tensor(xsl, xsl, k.ps[:, u % 2, 0:D], ALU.add).then_inc(S["cut"], 1)
                        dve.wait_ge(S["cut"], NT + i + 1)
                        nc.vector.tensor_tensor(xsl, xsl, b_out[:], ALU.add).then_inc(S["added"], 1)

            @block.scalar
            def _(act):
                emit_sqrt(k, act, mv, S["stats_ready"], S["sqrt_ready"])

                def copy_turned(i, o):
                    act.wait_ge(S["turned"], i + 1)
                    if not isinstance(i, int) or i >= 4:
                        act.wait_ge(S["product"], i - 3)
                    nc.scalar.copy(xt[:, o, :], k.ps[:, 0, 0:D]).then_inc(S["turned_copied"], 1)

                def exponents(i, o):
                    act.wait_ge(S["raised"], i + 1)
                    nc.scalar.activation(soft[:, o, :], soft[:, o, :], ACT.Exp).then_inc(S["weighed"], 1)

                def keep_turned(i, o):
                    act.wait_ge(S["soft_turned"], i + 1)
                    nc.scalar.copy(soft_t[:, :, bass.ts(i, P)],
                                   k.ps[:, 1, :].rearrange("p (a b) -> p a b", b=P)).then_inc(S["soft_kept"], 1)

                staggered(act, [(keep_turned, 4), (copy_turned, 0), (exponents, 2)])
                act.wait_ge(S["mid_dve"], 9)
                for a, b in HALVES:
                    last = nc.scalar.activation(att[a:b, :, a:b], att[a:b, :, a:b], ACT.Exp, scale=float(SD) ** -0.5)
                last.then_inc(S["mid_act"], 1)
                act.wait_ge(S["soft_kept"], NT)
                with act.Fori(0, GROUPS) as g:
                    for u in range(U):
                        i = g * U + u
                        act.wait_ge(S["result"], g * U)
                        nc.scalar.copy(piece[:, u, :].rearrange("p (a b) -> p a b", b=P),
                                       soft_t[:, :, bass.ts(i, P)]).then_inc(S["act_step"], 1)

            @block.tensor
            def _(pe):
                pe.wait_ge(S["loaded"], 16 * 15)
                pe.wait_ge(S["zeroed"], 4)
                for c in range(KC):
                    for h in range(SH):
                        nc.tensor.matmul(k.ps[:, c, bass.ts(h, SD)], w_x_t[:, h, bass.ts(c, P)], w_slice[:],
                                         start=True, stop=True)
                nc.tensor.matmul(k.ps[0:SH, 2, 0:SD], b_x[:], w_slice[:], start=True, stop=True).then_inc(S["fused"], 1)
                pe.wait_ge(S["w_ready"], 1)
                for b in range(2):
                    nc.tensor.matmul(k.ps[:, 4 + b, 0:2 * (PD + 1)], k.ones[0:1, :], zero[:], start=True, stop=False,
                                     skip_group_check=True)

                def turn(i, o):
                    pe.wait_ge(S["normed"], i + 1)
                    if not isinstance(i, int) or i >= 1:
                        pe.wait_ge(S["turned_copied"], i)
                    for c in range(KC):
                        last = nc.tensor.transpose(k.ps[:, 0, bass.ts(c, P)], xn[:, o, bass.ts(c, P)], k.ident[:])
                    last.then_inc(S["turned"], 1)

                def project(i, o):
                    bank = 2 + o % 2 * 4
                    pe.wait_ge(S["turned_copied"], i + 1)
                    if not isinstance(i, int) or i >= 2:
                        pe.wait_ge(S["scored"], i - 1)
                    for b, w in ((bank, w_fx), (bank + 1, w_sl)):
                        for c in range(KC):
                            last = nc.tensor.matmul(k.ps[:, b, :], xt[:, o, bass.ts(c, P)], w[:, c, :],
                                                    start=c == 0, stop=c == KC - 1)
                    last.then_inc(S["product"], 1)

                def sum_tokens(i, o):
                    pe.wait_ge(S["cut"], i + 1)
                    if not isinstance(i, int) or i >= 1:
                        pe.wait_ge(S["soft_kept"], i)
                    for r in range(PAIRS):
                        last = nc.tensor.transpose(k.ps[:, 1, bass.ts(r, P)], soft[:, o, bass.ts(r, P)], k.ident[:])
                    last.then_inc(S["soft_turned"], 1)
                    for r in range(PAIRS):
                        last = nc.tensor.matmul(k.ps[:, 4 + r // 2, bass.ts(r % 2, PD + 1)], soft[:, o, bass.ts(r, PD)],
                                                fx[:, o, r, :], start=False, stop=False, skip_group_check=True)
                    last.then_inc(S["tokens"], 1)

                staggered(pe, [(turn, 0), (project, 1), (sum_tokens, 3)])
                pe.wait_ge(S["soft_kept"], NT)
                pe.wait_ge(S["mid_dve"], 3)
                for r in range(PAIRS):
                    last = nc.tensor.transpose(k.ps[:, 0, bass.ts(r, PD)], token[:, r, :], k.ident[:])
                last.then_inc(S["mid_pe"], 1)
                pe.wait_ge(S["mid_dve"], 4)
                for r in range(PAIRS):
                    nc.tensor.matmul(k.ps[:, 1, bass.ts(r, PD)], w_two[0][:], token_t[:, r, :], start=True, stop=True)
                    nc.tensor.matmul(k.ps[:, 2, bass.ts(r, PD)], w_two[1][:], token_t[:, r, :], start=True, stop=True)
                    last = nc.tensor.matmul(k.ps[:, 3, bass.ts(r, PD)], token_t[:, r, :], w_two[2][:], start=True,
                                            stop=True)
                last.then_inc(S["mid_pe"], 1)
                pe.wait_ge(S["mid_dve"], 7)
                for r in range(PAIRS):
                    last = nc.tensor.matmul(k.ps[:, 0, bass.ts(r, PD)], q_t[:, r, :], k_t[:, r, :], start=True,
                                            stop=True)
                last.then_inc(S["mid_pe"], 1)
                pe.wait_ge(S["mid_dve"], 12)
                for r in range(PAIRS):
                    last = nc.tensor.transpose(k.ps[:, 1, bass.ts(r, PD)], att[:, r, :], k.ident[:])
                last.then_inc(S["mid_pe"], 1)
                pe.wait_ge(S["mid_dve"], 13)
                for r in range(PAIRS):
                    last = nc.tensor.matmul(k.ps[:, 2, bass.ts(r, PD)], v[:, r, :], att_t[:, r, :], start=True,
                                            stop=True)
                last.then_inc(S["mid_pe"], 1)
                pe.wait_ge(S["mid_dve"], 14)
                for r in range(PAIRS):
                    last = nc.tensor.matmul(k.ps[:, 4 + r // 2, bass.ts(r % 2, D)], mix_t[:, r, :], w_out[:, r, :],
                                            start=True, stop=True)
                last.then_inc(S["mid_pe"], 1)
                pe.wait_ge(S["mid_dve"], 16)
                with pe.Fori(0, GROUPS) as g:
                    for u in range(U):
                        i = g * U + u
                        pe.wait_ge(S["act_step"], i + 1)
                        pe.wait_ge(S["added"], i - 1 if u >= 2 else g * U)
                        for r in range(PAIRS):
                            last = nc.tensor.matmul(k.ps[:, u % 2, 0:D], piece[:, u, bass.ts(r, P)], fold[:, r, :],
                                                    start=r == 0, stop=r == PAIRS - 1)
                        last.then_inc(S["result"], 1)


def message_tables(k):
    nc, t = k.nc, k.t
    ctx, sb, sem = phase(k)
    with ctx:
        w, b1 = sb("w", [P, KC, 2 * D]), sb("b1", [P, D])
        st, mv = sb("st", [P, NT * 6]), sb("mv", [P, 5, NT])
        xn, xt, out = (sb(n, [P, 4, D]) for n in ("xn", "xt", "out"))
        sender = Sender(k, sb, sem)
        loaded, dve_step, stats_ready, sqrt_ready = (sem(s) for s in ("loaded", "dve_step", "stats_ready", "sqrt_ready"))
        normed, turned, turned_copied, product, left = (
            sem(s) for s in ("normed", "turned", "turned_copied", "product", "left"))
        stored = [sem(f"stored{o}") for o in range(4)]

        with nc.Block() as block:
            @block.sync
            def _(sp):
                load_weights(k, sp, loaded, [(w[:, :, 0:D], chunks(t["w1_t"][0:D, :])),
                                             (w[:, :, D:], chunks(t["w1_t"][D:, :])), (b1[:], across(t["b1"]))])

                def store(i, o):
                    sp.wait_ge(left, i + 1)
                    sp.dma_start(t["msg_rows"][bass.ts(i, P), :], out[:, o, :]).then_inc(stored[o], 16)

                staggered(sp, [(store, 0)])
                for o in range(4):
                    sp.wait_ge(stored[o], 16 * len(range(o, NT, 4)))

            @block.gpsimd
            def _(pool):
                send_edges(pool, sender, t["rec_src"], *SENT_BY_MESSAGES)

            @block.vector
            def _(dve):
                step = Steps(dve, dve_step)
                emit_norm(k, dve, st, mv, stats_ready, sqrt_ready, step)
                dve.wait_ge(loaded, 48)

                def norm_row(i, o):
                    if not isinstance(i, int) or i >= 4:
                        dve.wait_ge(turned, i - 3)
                    nc.vector.tensor_scalar(xn[:, o, :], k.xs[:, bass.ts(i, D)], mv[:, 0, bass.ds(i, 1)],
                                            mv[:, 4, bass.ds(i, 1)], ALU.subtract, ALU.mult).then_inc(normed, 1)

                def leave(i, o):
                    dve.wait_ge(product, i + 1)
                    nc.vector.tensor_tensor(k.source_part[:, bass.ts(i, D)], k.ps[:, 2 + o % 2, 0:D], b1[:], ALU.add)
                    if not isinstance(i, int) or i >= 4:
                        dve.wait_ge(stored[o], (i - o) * 4)
                    nc.vector.tensor_copy(out[:, o, :], k.ps[:, 2 + o % 2, D:]).then_inc(left, 1)

                staggered(dve, [(norm_row, 0), (leave, 2)])

            @block.scalar
            def _(act):
                emit_sqrt(k, act, mv, stats_ready, sqrt_ready)

                def keep_turned(i, o):
                    act.wait_ge(turned, i + 1)
                    if not isinstance(i, int) or i >= 4:
                        act.wait_ge(product, i - 3)
                    nc.scalar.copy(xt[:, o, :], k.ps[:, o % 2, 0:D]).then_inc(turned_copied, 1)

                staggered(act, [(keep_turned, 0)])

            @block.tensor
            def _(pe):
                pe.wait_ge(loaded, 48)

                def turn(i, o):
                    pe.wait_ge(normed, i + 1)
                    if not isinstance(i, int) or i >= 2:
                        pe.wait_ge(turned_copied, i - 1)
                    for c in range(KC):
                        last = nc.tensor.transpose(k.ps[:, o % 2, bass.ts(c, P)], xn[:, o, bass.ts(c, P)], k.ident[:])
                    last.then_inc(turned, 1)

                def project(i, o):
                    pe.wait_ge(turned_copied, i + 1)
                    if not isinstance(i, int) or i >= 2:
                        pe.wait_ge(left, i - 1)
                    for c in range(KC):
                        last = nc.tensor.matmul(k.ps[:, 2 + o % 2, :], xt[:, o, bass.ts(c, P)], w[:, c, :],
                                                start=c == 0, stop=c == KC - 1)
                    last.then_inc(product, 1)

                staggered(pe, [(turn, 0), (project, 1)])


def message_edges(k):
    nc, t = k.nc, k.t
    ctx, sb, sem = phase(k)
    W = D + 1
    with ctx:
        acc = k.sums
        rec, rows = sb("rec", [P, SLOTS, 2], I32), sb("rows", [P, SLOTS, D])
        hot, hot_t = sb("hot", [P, SLOTS, P]), sb("hot_t", [P, 2, BATCH, P])
        places = sb("places", [P, 2, BATCH])
        msg = sb("msg", [P, 2, BATCH, W])
        started = sem("started")
        rec_landed = [sem(f"rec_landed{s}") for s in range(SLOTS)]
        row_landed = [sem(f"row_landed{s}") for s in range(SLOTS)]
        placed, hot_made, hot_turned, hot_copied, expanded, raised, silu_done, multiplied, added, prepared = (
            sem(s) for s in ("placed", "hot_made", "hot_turned", "hot_copied", "expanded", "raised", "silu_done", "multiplied",
                             "added", "prepared"))

        with nc.Block() as block:
            @block.sync
            def _(sp):
                with sp.Fori(0, BODIES) as g:
                    for part in range(SLOTS // 8):
                        _, start = nc.values_load_multi_w_load_instructions(
                            k.start_src[0:1, bass.ds(g * SLOTS + part * 8, 8)], engines=(SP,), min_val=0, max_val=EP)
                        for n in range(8):
                            s = part * 8 + n
                            sp.wait_ge(raised, g * BSETS + s // BATCH + 1)
                            sp.dma_start(rec[:, s, :], t["rec_src"][bass.ds(start[n], P), :]).then_inc(rec_landed[s], 16)

            @block.gpsimd
            def _(pool):
                with pool.Fori(0, BODIES) as g:
                    for s in range(SLOTS):
                        pool.wait_ge(rec_landed[s], 16 * (g + 1))
                        pool.sem_inc(started, 1)
                        nc.gpsimd.indirect_dma_start(
                            rows[:, s, :], None, t["msg_rows"][:, :],
                            bass.IndirectOffsetOnAxis(ap=rec[:, s, 0:1], axis=0)).then_inc(row_landed[s], 16)

            @block.vector
            def _(dve):
                dve.sem_inc(raised, BSETS)
                nc.vector.memset(msg[:, :, :, D:], 1.0).then_inc(prepared, 1)
                nc.vector.memset(acc[:], 0.0).then_inc(prepared, 1)
                dve.wait_ge(prepared, 2)

                def find_places(g, c):
                    B, s0 = g * BSETS + c, c * BATCH
                    for s in range(s0, s0 + BATCH):
                        dve.wait_ge(rec_landed[s], 16 * (g + 1))
                    nc.vector.tensor_tensor(places[:, c % 2, :], rec[:, s0:s0 + BATCH, 1].bitcast(F32),
                                            k.base_src[:, bass.ds(B * BATCH, BATCH)], ALU.subtract).then_inc(placed, 1)

                def one_hots(g, c, n):
                    B, s = g * BSETS + c, c * BATCH + n
                    if not (isinstance(g, int) and g == 0):
                        dve.wait_ge(multiplied, (B - BSETS + 1) * BATCH)
                    dve.wait_ge(placed, B + 1)
                    nc.vector.tensor_tensor(hot[:, s:s + 2, :], k.iota[:].unsqueeze(1).to_broadcast([P, 2, P]),
                                            places[:, c % 2, n:n + 2].unsqueeze(2).to_broadcast([P, 2, P]),
                                            ALU.is_equal).then_inc(hot_made, 1)

                def add_rows(g, c):
                    B = g * BSETS + c
                    dve.wait_ge(expanded, B + 1)
                    if not (isinstance(g, int) and g == 0 and c < 2):
                        dve.wait_ge(multiplied, (B - 1) * BATCH)
                    for h in range(2):
                        s0 = c * BATCH + 2 * h
                        for s in (s0, s0 + 1):
                            dve.wait_ge(row_landed[s], 16 * (g + 1))
                        last = nc.vector.tensor_tensor(
                            msg[:, c % 2, 2 * h:2 * h + 2, 0:D], k.ps[:, 2 + h, :].rearrange("p (a b) -> p a b", b=D),
                            rows[:, s0:s0 + 2, :], ALU.add)
                    last.then_inc(raised, 1)

                def add_sum(g, c, n, tile):
                    q = g * SLOTS + c * BATCH + n
                    dve.wait_ge(multiplied, q + 1)
                    dve.wait_ge(added, q)
                    sums = acc[:, bass.ds(tile[n] * W, W)]
                    nc.vector.tensor_tensor(sums, sums, k.ps[:, 4 + n, 0:W], ALU.add).then_inc(added, 1)

                def tiles(q):
                    return nc.values_load_multi_w_load_instructions(
                        k.tile_src[0:1, bass.ds(q, BATCH)], engines=(DVE,), min_val=0, max_val=NT - 1)[1]

                def body(g, first, last):
                    if first:
                        for c in range(2):
                            find_places(0, c)
                            one_hots(0, c, 0)
                            one_hots(0, c, 2)
                        find_places(0, 2)
                    for c in range(BSETS):
                        before = (g, c - 2) if c >= 2 else None if first else (g - 1, c + BSETS - 2)
                        ahead = (g, c + 2) if c < BSETS - 2 else None if last else (g + 1, c + 2 - BSETS)
                        placed_next = (g, c + 3) if c < BSETS - 3 else None if last else (g + 1, c + 3 - BSETS)
                        if before:
                            tile = tiles(before[0] * SLOTS + before[1] * BATCH)
                        for n in range(BATCH):
                            if before:
                                add_sum(*before, n, tile)
                            if n < 2 and ahead:
                                one_hots(*ahead, 2 * n)
                            if n == 2 and placed_next:
                                find_places(*placed_next)
                        add_rows(g, c)
                    if last:
                        for c in (BSETS - 2, BSETS - 1):
                            tile = tiles(g * SLOTS + c * BATCH)
                            for n in range(BATCH):
                                add_sum(g, c, n, tile)

                bodies(dve, body)

            @block.scalar
            def _(act):
                def copy_turned(g, c):
                    B = g * BSETS + c
                    act.wait_ge(hot_turned, B + 1)
                    if not (isinstance(g, int) and g == 0 and c < 2):
                        act.wait_ge(expanded, B - 1)
                    nc.scalar.copy(hot_t[:, c % 2, :, :], k.ps[:, c % 2, :].rearrange(
                        "p (a b) -> p a b", b=P)).then_inc(hot_copied, 1)

                def body(g, first, last):
                    if first:
                        copy_turned(0, 0)
                    for c in range(BSETS):
                        if c < BSETS - 1:
                            copy_turned(g, c + 1)
                        elif not last:
                            copy_turned(g + 1, 0)
                        act.wait_ge(raised, g * BSETS + c + 1 + BSETS)
                        nc.scalar.activation(msg[:, c % 2, :, 0:D], msg[:, c % 2, :, 0:D],
                                             ACT.Silu).then_inc(silu_done, 1)

                bodies(act, body)

            @block.tensor
            def _(pe):
                pe.wait_ge(prepared, 1)

                def turn(g, c):
                    B = g * BSETS + c
                    pe.wait_ge(hot_made, (B + 1) * 2)
                    if not (isinstance(g, int) and g == 0 and c < 2):
                        pe.wait_ge(hot_copied, B - 1)
                    for n in range(BATCH):
                        last = nc.tensor.transpose(k.ps[:, c % 2, bass.ts(n, P)], hot[:, c * BATCH + n, :], k.ident[:])
                    last.then_inc(hot_turned, 1)

                def expand(g, c, tile):
                    B = g * BSETS + c
                    pe.wait_ge(hot_copied, B + 1)
                    pe.wait_ge(raised, B + BSETS)
                    for n in range(BATCH):
                        last = nc.tensor.matmul(k.ps[:, 2 + n // 2, bass.ts(n % 2, D)], hot_t[:, c % 2, n, :],
                                                k.source_part[:, bass.ds(tile[n] * D, D)], start=True, stop=True)
                    last.then_inc(expanded, 1)

                def multiply(g, c):
                    B = g * BSETS + c
                    pe.wait_ge(silu_done, B + 1)
                    for n in range(BATCH):
                        if not (isinstance(g, int) and g == 0 and c == 0):
                            pe.wait_ge(added, (B - 1) * BATCH + n + 1)
                        nc.tensor.matmul(k.ps[:, 4 + n, 0:W], hot[:, c * BATCH + n, :], msg[:, c % 2, n, :],
                                         start=True, stop=True).then_inc(multiplied, 1)

                def tiles(q):
                    return nc.values_load_multi_w_load_instructions(
                        k.tile_src[0:1, bass.ds(q, BATCH)], engines=(PE,), min_val=0, max_val=NT - 1)[1]

                def body(g, first, last):
                    if first:
                        turn(0, 0)
                    for c in range(BSETS):
                        expand(g, c, tiles(g * SLOTS + c * BATCH))
                        if c < BSETS - 1:
                            turn(g, c + 1)
                        elif not last:
                            turn(g + 1, 0)
                        if c:
                            multiply(g, c - 1)
                        elif not first:
                            multiply(g - 1, BSETS - 1)
                    if last:
                        multiply(g, BSETS - 1)

                bodies(pe, body)


def gated_update(k):
    nc, t = k.nc, k.t
    ctx, sb, sem = phase(k)
    W, G = D + 1, 3 * D
    FR = mybir.dt.float32r
    with ctx:
        w_hh, w_ih = sb("w_hh", [P, KC, G]), sb("w_ih", [P, KC, G])
        w2, b2 = sb("w2", [P, KC, D]), sb("b2", [P, KC])
        w_hh_h, w_hh_l = sb("w_hh_h", [P, KC, G], FR), sb("w_hh_l", [P, KC, G], FR)
        w_in_h, w_in_l = sb("w_in_h", [P, KC, G], FR), sb("w_in_l", [P, KC, G], FR)
        bias = sb("bias", [3, 4 * D])
        bias_h, bias_l = sb("bias_h", [3, 4 * D], FR), sb("bias_l", [3, 4 * D], FR)
        gamma, beta = sb("gamma", [P, D]), sb("beta", [P, D])
        inv, full = sb("inv", [P, NT]), sb("full", [P, NT])
        st, mv = sb("st", [P, NT * 6]), sb("mv", [P, 5, NT])
        both = sb("both", [P, 4, 2 * D + 3])
        both_h, both_l = sb("both_h", [P, 2, 4, P], FR), sb("both_l", [P, 2, 4, P], FR)
        ones_t = sb("ones_t", [3, 2, P], FR)
        rz, new = sb("rz", [P, 2, 2 * D]), sb("new", [P, 2, D])
        nst = sb("nst", [P, 2, 6])
        names = ("loaded", "zeroed", "dve_step", "stats_ready", "sqrt_ready", "fused", "w_high", "w_split", "bias_whole", "w_ready", "halved",
                 "adding", "layer_normed", "times_gamma", "residual_added", "normed", "turned",
                 "turned_copied", "product", "gates", "candidate", "tanh_done", "chain", "tile_var", "tile_sqrt",
                 "finished")
        S = {n: sem(n) for n in names}
        sums3 = k.sums[:].rearrange("p (i c) -> p i c", c=W)
        outv = k.new_rows

        with nc.Block() as block:
            @block.sync
            def _(sp):
                sp.wait_ge(S["zeroed"], 1)
                load_weights(k, sp, S["loaded"], [
                    (w_hh[:], chunks(t["w_hh_t"])), (w_ih[:], chunks(t["w_ih_t"])), (w2[:], chunks(t["w2"])),
                    (b2[:], t["b2_cols"]), (gamma[:], across(t["gamma"])), (beta[:], across(t["beta"])),
                    (bias[1:2, 0:3 * D], row(t["b_ih"])), (bias[2:3, 0:2 * D], row(t["b_hh"][0:2 * D])),
                    (bias[2:3, 3 * D:], row(t["b_hh"][2 * D:]))])

            @block.gpsimd
            def _(pool):
                nc.gpsimd.memset(bias[:], 0.0).then_inc(S["zeroed"], 1)
                nc.gpsimd.memset(both[:, :, 2 * D + 1:], 1.0).then_inc(S["zeroed"], 1)
                pool.wait_ge(S["loaded"], 16 * 9)
                nc.gpsimd.tensor_copy(w_hh_h[:], w_hh[:]).then_inc(S["w_split"], 1)
                pool.wait_ge(S["w_split"], 1)
                nc.gpsimd.tensor_tensor(w_hh_l[:], w_hh[:], w_hh_h[:].bitcast(F32), ALU.subtract).then_inc(S["w_split"], 1)

                def add_beta(i, o):
                    pool.wait_ge(S["normed"], i + 1)
                    pool.sem_inc(S["adding"], 1)
                    xsl = k.xs[:, bass.ts(i, D)]
                    nc.gpsimd.tensor_tensor(xsl, xsl, beta[:], ALU.add)

                staggered(pool, [(add_beta, 0)])
                with pool.Fori(0, GROUPS) as g:
                    pool.wait_ge(S["layer_normed"], g + 1)
                    pool.sem_inc(S["adding"], 1)
                    for u in range(U):
                        y = outv[:, bass.ts(g * U + u, D)]
                        last = nc.gpsimd.tensor_tensor(y, y, gamma[:], ALU.mult)
                    last.then_inc(S["times_gamma"], 1)

            @block.vector
            def _(dve):
                step = Steps(dve, S["dve_step"])
                emit_norm(k, dve, st, mv, S["stats_ready"], S["sqrt_ready"], step)
                step(nc.vector.tensor_scalar(inv[:], sums3[:, :, D], 1e-8, None, ALU.add))
                step(nc.vector.reciprocal(inv[:], inv[:]))
                step(nc.vector.tensor_tensor(full[:], sums3[:, :, D], inv[:], ALU.mult))
                dve.wait_ge(S["fused"], 1)
                dve.wait_ge(S["loaded"], 16 * 9)
                nc.vector.tensor_copy(bias[0:1, 0:2 * D], k.ps[0:1, 4, :]).then_inc(S["bias_whole"], 1)
                nc.vector.tensor_copy(bias[0:1, 2 * D:3 * D], k.ps[0:1, 5, 0:D]).then_inc(S["bias_whole"], 1)
                for n in range(2 * KC):
                    cols = slice(0, 2 * D) if n % 2 == 0 else slice(2 * D, G)
                    dve.wait_ge(S["w_high"], n + 1)
                    nc.vector.tensor_tensor(w_in_l[:, n // 2, cols], k.ps[:, n, 0:cols.stop - cols.start],
                                            w_in_h[:, n // 2, cols].bitcast(F32), ALU.subtract).then_inc(S["w_ready"], 1)
                dve.wait_ge(S["w_high"], 2 * KC + 1)
                nc.vector.tensor_tensor(bias_l[:], bias[:], bias_h[:].bitcast(F32), ALU.subtract).then_inc(S["w_ready"], 1)
                dve.wait_ge(S["zeroed"], 2)
                CH = 5

                def prepare(i, o):
                    if not isinstance(i, int) or i >= 4:
                        dve.wait_ge(S["turned"], i - 3)
                    nc.vector.tensor_scalar(both[:, o, 0:D], k.xs[:, bass.ts(i, D)], mv[:, 0, bass.ds(i, 1)],
                                            mv[:, 4, bass.ds(i, 1)], ALU.subtract, ALU.mult)
                    nc.vector.tensor_copy(both[:, o, 2 * D:2 * D + 1], full[:, bass.ds(i, 1)])
                    nc.vector.tensor_scalar(both[:, o, D:2 * D], k.sums[:, bass.ds(i * W, D)], inv[:, bass.ds(i, 1)],
                                            None, ALU.mult).then_inc(S["normed"], 1)

                def low_part(i, slot):
                    o = slot % 2
                    dve.wait_ge(S["turned_copied"], i + 1)
                    nc.vector.tensor_tensor(both_l[:, o, :, :], k.ps[:, o, :].rearrange("p (a b) -> p a b", b=P),
                                            both_h[:, o, :, :].bitcast(F32), ALU.subtract).then_inc(S["halved"], 1)

                def update(i, slot):
                    o = slot % 2
                    xn = both[:, slot, 0:D]

                    def link(n, ins):
                        ins.then_inc(S["chain"], 1)
                        dve.wait_ge(S["chain"], i * CH + n)

                    dve.wait_ge(S["gates"], i + 1)
                    link(1, nc.vector.tensor_tensor(new[:, o, :], rz[:, o, 0:D], k.ps[:, 4 + o, D:], ALU.mult))
                    nc.vector.tensor_tensor(new[:, o, :], new[:, o, :], k.ps[:, 4 + o, 0:D],
                                            ALU.add).then_inc(S["candidate"], 1)
                    dve.wait_ge(S["tanh_done"], i + 1)
                    link(2, nc.vector.tensor_tensor(xn, xn, new[:, o, :], ALU.subtract))
                    link(3, nc.vector.tensor_tensor(xn, xn, rz[:, o, D:], ALU.mult))
                    link(4, nc.vector.tensor_tensor(new[:, o, :], new[:, o, :], xn, ALU.add))
                    link(5, nc.vector.bn_stats(nst[:, o, :], new[:, o, :]))
                    nc.vector.tensor_scalar(st[:, bass.ts(i, 6)], nst[:, o, :], 1.0, None, ALU.mult)
                    nc.vector.tensor_scalar(outv[:, bass.ts(i, D)], new[:, o, :], 1.0, None,
                                            ALU.mult).then_inc(S["finished"], 1)

                staggered(dve, [(prepare, 0), (low_part, 1), (update, 2)])
                dve.wait_ge(S["finished"], NT)
                emit_moments(k, dve, st, mv, S["tile_var"], S["tile_sqrt"], step)
                with dve.Fori(0, GROUPS) as g:
                    for u in range(U):
                        i = g * U + u
                        y = outv[:, bass.ts(i, D)]
                        last = nc.vector.tensor_scalar(y, y, mv[:, 0, bass.ds(i, 1)], mv[:, 4, bass.ds(i, 1)],
                                                       ALU.subtract, ALU.mult)
                    last.then_inc(S["layer_normed"], 1)
                with dve.Fori(0, GROUPS) as g:
                    dve.wait_ge(S["times_gamma"], g + 1)
                    for u in range(U):
                        xsl = k.xs[:, bass.ts(g * U + u, D)]
                        last = nc.vector.tensor_tensor(xsl, xsl, outv[:, bass.ts(g * U + u, D)], ALU.add)
                    last.then_inc(S["residual_added"], 1)
                dve.wait_ge(S["residual_added"], GROUPS)

            @block.scalar
            def _(act):
                emit_sqrt(k, act, mv, S["stats_ready"], S["sqrt_ready"])
                act.wait_ge(S["fused"], 1)
                for n in range(2 * KC):
                    cols = slice(0, 2 * D) if n % 2 == 0 else slice(2 * D, G)
                    nc.scalar.copy(w_in_h[:, n // 2, cols], k.ps[:, n, 0:cols.stop - cols.start]).then_inc(S["w_high"], 1)
                act.wait_ge(S["bias_whole"], 2)
                nc.scalar.copy(bias_h[:], bias[:]).then_inc(S["w_high"], 1)

                def copy_turned(i, slot):
                    o = slot % 2
                    act.wait_ge(S["turned"], i + 1)
                    if not isinstance(i, int) or i >= 2:
                        act.wait_ge(S["product"], i - 1)
                    nc.scalar.copy(both_h[:, o, :, :], k.ps[:, o, :].rearrange("p (a b) -> p a b", b=P))
                    nc.scalar.copy(ones_t[:, o, :], k.ps[0:3, 6, 0:P]).then_inc(S["turned_copied"], 1)

                def gates(i, slot):
                    o = slot % 2
                    act.wait_ge(S["product"], i + 1)
                    if not isinstance(i, int) or i >= 2:
                        act.wait_ge(S["finished"], i - 1)
                    nc.scalar.activation(rz[:, o, :], k.ps[:, 2 + o, :], ACT.Sigmoid).then_inc(S["gates"], 1)
                    act.wait_ge(S["candidate"], i + 1)
                    nc.scalar.activation(new[:, o, :], new[:, o, :], ACT.Tanh).then_inc(S["tanh_done"], 1)

                staggered(act, [(copy_turned, 0), (gates, 1)])
                emit_sqrt(k, act, mv, S["tile_var"], S["tile_sqrt"])

            @block.tensor
            def _(pe):
                pe.wait_ge(S["loaded"], 16 * 9)
                for m in range(KC):
                    for c in range(KC):
                        nc.tensor.matmul(k.ps[:, 2 * m, :], w2[:, c, bass.ts(m, P)], w_ih[:, c, 0:2 * D],
                                         start=c == 0, stop=c == KC - 1)
                    for c in range(KC):
                        nc.tensor.matmul(k.ps[:, 2 * m + 1, 0:D], w2[:, c, bass.ts(m, P)], w_ih[:, c, 2 * D:],
                                         start=c == 0, stop=c == KC - 1)
                for c in range(KC):
                    nc.tensor.matmul(k.ps[0:1, 4, :], b2[:, c:c + 1], w_ih[:, c, 0:2 * D], start=c == 0,
                                     stop=c == KC - 1)
                for c in range(KC):
                    last = nc.tensor.matmul(k.ps[0:1, 5, 0:D], b2[:, c:c + 1], w_ih[:, c, 2 * D:], start=c == 0,
                                            stop=c == KC - 1)
                last.then_inc(S["fused"], 1)
                pe.wait_ge(S["w_ready"], 2 * KC + 1)
                pe.wait_ge(S["w_split"], 2)

                def turn(i, slot):
                    o = slot % 2
                    pe.wait_ge(S["normed"], i + 1)
                    pe.wait_ge(S["turned_copied"], i)
                    if not isinstance(i, int) or i > 1:
                        pe.wait_ge(S["halved"], i - 1)
                    for c in range(4):
                        nc.tensor.transpose(k.ps[:, o, bass.ts(c, P)], both[:, slot, bass.ts(c, P)], k.ident[:])
                    nc.tensor.transpose(k.ps[0:3, 6, 0:P], both[:, slot, 2 * D:], k.ident[:]).then_inc(S["turned"], 1)

                def products(i, slot):
                    o = slot % 2
                    pe.wait_ge(S["halved"], i + 1)
                    if not isinstance(i, int) or i > 1:
                        pe.wait_ge(S["candidate"], i - 1)
                    one = ones_t[:, o, :]

                    def product(out, parts, cols, bias_cols):
                        first = True
                        for at, w_h, w_l in parts:
                            for c in range(KC):
                                x_h, x_l = both_h[:, o, at + c, :], both_l[:, o, at + c, :]
                                for x, w in ((x_h, w_h), (x_h, w_l), (x_l, w_h)):
                                    nc.tensor.matmul(out, x, w[:, c, cols], start=first, stop=False)
                                    first = False
                        nc.tensor.matmul(out, one, bias_h[:, bias_cols], start=False, stop=False)
                        return nc.tensor.matmul(out, one, bias_l[:, bias_cols], start=False, stop=True)

                    own, message = (0, w_hh_h, w_hh_l), (KC, w_in_h, w_in_l)
                    product(k.ps[:, 2 + o, :], (own, message), slice(0, 2 * D), slice(0, 2 * D))
                    product(k.ps[:, 4 + o, 0:D], (message,), slice(2 * D, G), slice(2 * D, G))
                    product(k.ps[:, 4 + o, D:], (own,), slice(2 * D, G), slice(G, 4 * D)).then_inc(S["product"], 1)

                staggered(pe, [(turn, 0), (products, 1)])


def experts(k):
    nc, t = k.nc, k.t
    ctx, sb, sem = phase(k)
    TOK = U * P
    HALF = TOK // 2
    STEPS = 2 * GROUPS
    FR = mybir.dt.float32r
    with ctx:
        raw1, raw2 = sb("raw1", [P, KC, ED]), sb("raw2", [P, EK, D])
        w1_h, w1_l = sb("w1_h", [P, 2, KC, ED], FR), sb("w1_l", [P, 2, KC, ED], FR)
        w2_h, w2_l = sb("w2_h", [P, 2, EK, D], FR), sb("w2_l", [P, 2, EK, D], FR)
        b1, b2 = sb("b1", [P, 2, EK]), sb("b2", [NE, D])
        w_gate, b_gate, g_bias = sb("w_gate", [P, KC, NE]), sb("b_gate", [P, NE]), sb("g_bias", [P, NE])
        rank = sb("rank", [P, NE])
        st, mv = sb("st", [P, NT * 6]), sb("mv", [P, 5, NT])
        xn, xt = sb("xn", [P, 4, D]), sb("xt", [P, 4, KC, P])
        xt_h, xt_l = sb("xt_h", [P, KC, NP], FR), sb("xt_l", [P, KC, NP], FR)
        act_out = sb("act_out", [P, 2, TOK])
        hid_h, hid_l = sb("hid_h", [P, 2, EK, TOK], FR), sb("hid_l", [P, 2, EK, TOK], FR)
        logit, eq, one, two, mix = (sb(n, [P, NT, NE]) for n in ("logit", "eq", "one", "two", "mix"))
        best = sb("best", [P, 6, NT])
        mix_now, mix_t = sb("mix_now", [P, 4, NE]), sb("mix_t", [NE, 4, P])
        names = ("loaded", "gate_loaded", "dve_step", "stats_ready", "sqrt_ready", "normed", "turned", "turned_copied",
                 "halved", "split_x", "gated", "gap", "gap_exp", "mix_ready", "mix_staged", "mix_turned", "mix_copied", "based",
                 "base_added", "weights_loaded", "fetching", "splitting", "weights_split", "hidden", "raised", "high_ready",
                 "active", "projected", "mixed", "stored")
        S = {n: sem(n) for n in names}
        BEFORE = NT + 1
        OLD = NT

        def pairs(engine, body):
            with engine.Fori(0, NE // 2) as pair:
                body(pair)

        with nc.Block() as block:
            @block.sync
            def _(sp):
                load_weights(k, sp, S["gate_loaded"], [
                    (w_gate[:], chunks(t["w_gate"])), (b_gate[:], across(t["b_gate"])), (g_bias[:], across(t["gate_bias"])),
                    (b2[:], t["e_b2"])])

                def load(pair):
                    for a in range(2):
                        e = pair * 2 + a
                        sp.wait_ge(S["weights_split"], 4 * e + 1)
                        sp.dma_start(raw1[:], t["e_w1"][bass.ds(e, 1), :, :].rearrange("a (c p) n -> p (a c) n", p=P)
                                     ).then_inc(S["weights_loaded"], 16)
                        sp.dma_start(raw2[:], t["e_w2"][bass.ds(e, 1), :, :].rearrange("a (c p) n -> p (a c) n", p=P)
                                     ).then_inc(S["weights_loaded"], 16)
                        sp.wait_ge(S["projected"], e * NT + (BEFORE - NT))
                        sp.sem_inc(S["fetching"], 1)
                        sp.dma_start(b1[:, a, :], t["e_b1_cols"][:, bass.ts(e, EK)]).then_inc(S["weights_loaded"], 16)

                pairs(sp, load)
                for g in range(GROUPS):
                    sp.wait_ge(S["mixed"], OLD + (NE - 1) * NT + (g + 1) * U)
                    full = U if g < GROUPS - 1 else U - 1
                    a = g * U
                    sp.dma_start(t["out"][a * P:(a + full) * P, :].rearrange("(i p) d -> p i d", p=P),
                                 k.xs[:, a * D:(a + full) * D].rearrange("p (i d) -> p i d", d=D)).then_inc(
                                     S["stored"], 16)
                sp.dma_start(t["out"][(NT - 1) * P:N, :], k.xs[0:TAIL, (NT - 1) * D:]).then_inc(S["stored"], 16)
                sp.wait_ge(S["stored"], 16 * (GROUPS + 1))

            @block.gpsimd
            def _(pool):
                pool.sem_inc(S["weights_split"], 1)

                def split(pair):
                    for a in range(2):
                        e = pair * 2 + a
                        pool.wait_ge(S["weights_loaded"], e * 48 + 48)
                        pool.wait_ge(S["projected"], e * NT + (BEFORE - NT))
                        pool.sem_inc(S["splitting"], 1)
                        nc.gpsimd.tensor_copy(w1_h[:, a], raw1[:]).then_inc(S["weights_split"], 1)
                        nc.gpsimd.tensor_copy(w2_h[:, a], raw2[:]).then_inc(S["weights_split"], 1)
                        pool.wait_ge(S["weights_split"], e * 4 + 3)
                        nc.gpsimd.tensor_tensor(w1_l[:, a], raw1[:], w1_h[:, a].bitcast(F32),
                                                ALU.subtract).then_inc(S["weights_split"], 1)
                        nc.gpsimd.tensor_tensor(w2_l[:, a], raw2[:], w2_h[:, a].bitcast(F32),
                                                ALU.subtract).then_inc(S["weights_split"], 1)

                pairs(pool, split)

            @block.vector
            def _(dve):
                step = Steps(dve, S["dve_step"])
                dve.sem_inc(S["mixed"], OLD)
                emit_norm(k, dve, st, mv, S["stats_ready"], S["sqrt_ready"], step)
                step(nc.vector.tensor_scalar(rank[:], k.iota[:, 0:NE], -1.0, float(NE), ALU.mult, ALU.add))

                def norm_row(i, o):
                    if not isinstance(i, int) or i >= 4:
                        dve.wait_ge(S["turned"], i - 3)
                    nc.vector.tensor_scalar(xn[:, o, :], k.xs[:, bass.ts(i, D)], mv[:, 0, bass.ds(i, 1)],
                                            mv[:, 4, bass.ds(i, 1)], ALU.subtract, ALU.mult).then_inc(S["normed"], 1)

                def low_part(i, o):
                    dve.wait_ge(S["halved"], i + 1)
                    nc.vector.tensor_tensor(xt_l[:, :, bass.ts(i, P)], xt[:, o, :, :],
                                            xt_h[:, :, bass.ts(i, P)].bitcast(F32), ALU.subtract).then_inc(S["split_x"], 1)

                staggered(dve, [(norm_row, 0), (low_part, 2)])
                dve.wait_ge(S["gate_loaded"], 64)
                dve.wait_ge(S["gated"], NT)

                def spread(v):
                    return v.unsqueeze(2).to_broadcast([P, NT, NE])

                def same(v):
                    return v[:].unsqueeze(1).to_broadcast([P, NT, NE])

                step(nc.vector.tensor_tensor(logit[:], k.ps[:, 7, 0:NT * NE].rearrange("p (i e) -> p i e", e=NE),
                                             same(b_gate), ALU.add))
                step(nc.vector.tensor_tensor(logit[:], logit[:], same(g_bias), ALU.add))
                for hot, top in ((one, best[:, 0, :]), (two, best[:, 1, :])):
                    step(nc.vector.tensor_reduce(top, logit[:], AX, ALU.max))
                    step(nc.vector.tensor_tensor(eq[:], logit[:], spread(top), ALU.is_equal))
                    step(nc.vector.tensor_tensor(eq[:], eq[:], same(rank), ALU.mult))
                    step(nc.vector.tensor_reduce(best[:, 2, :], eq[:], AX, ALU.max))
                    step(nc.vector.tensor_tensor(hot[:], eq[:], spread(best[:, 2, :]), ALU.is_equal))
                    if hot is one:
                        step(nc.vector.scalar_tensor_tensor(out=logit[:], in0=one[:], scalar=-BIG, in1=logit[:],
                                                            op0=ALU.mult, op1=ALU.add))
                nc.vector.tensor_tensor(best[:, 3, :], best[:, 1, :], best[:, 0, :], ALU.subtract).then_inc(S["gap"], 1)
                dve.wait_ge(S["gap_exp"], 1)
                step(nc.vector.tensor_scalar(best[:, 4, :], best[:, 3, :], 1.0, None, ALU.add))
                step(nc.vector.reciprocal(best[:, 4, :], best[:, 4, :]))
                step(nc.vector.tensor_tensor(best[:, 5, :], best[:, 3, :], best[:, 4, :], ALU.mult))
                step(nc.vector.tensor_tensor(one[:], one[:], spread(best[:, 4, :]), ALU.mult))
                step(nc.vector.tensor_tensor(two[:], two[:], spread(best[:, 5, :]), ALU.mult))
                nc.vector.tensor_tensor(mix[:], one[:], two[:], ALU.add).then_inc(S["mix_ready"], 1)
                dve.wait_ge(S["mix_ready"], 1)

                def add_base(i, o):
                    dve.wait_ge(S["based"], i + 1)
                    xsl = k.xs[:, bass.ts(i, D)]
                    nc.vector.tensor_tensor(xsl, xsl, k.ps[:, 4 + o % 2, 0:D], ALU.add).then_inc(S["base_added"], 1)

                def stage_mix(i, o):
                    if not isinstance(i, int) or i >= 4:
                        dve.wait_ge(S["mix_turned"], i - 3)
                    nc.vector.tensor_scalar(mix_now[:, o, :], mix[:, bass.ds(i, 1), :].rearrange("p a e -> p (a e)"), 1.0,
                                            None, ALU.mult).then_inc(S["mix_staged"], 1)

                staggered(dve, [(stage_mix, 0), (add_base, 3)])
                dve.wait_ge(S["base_added"], NT)

                def low_hidden(pair, j):
                    for m in range(EK):
                        q = (pair * STEPS + j) * EK + m
                        dve.wait_ge(S["high_ready"], q + 1)
                        nc.vector.tensor_tensor(hid_l[:, j % 2, m, :], act_out[:, m % 2, :],
                                                hid_h[:, j % 2, m, :].bitcast(F32), ALU.subtract).then_inc(S["active"], 1)

                def add_expert(pair, j):
                    a, g = j // GROUPS, j % GROUPS
                    for u in range(U):
                        i, n = g * U + u, (pair * STEPS + j) * U + u
                        dve.wait_ge(S["projected"], n + (1 + BEFORE))
                        dve.wait_ge(S["mixed"], n + 1)
                        xsl = k.xs[:, i * D:(i + 1) * D]
                        nc.vector.scalar_tensor_tensor(
                            out=xsl, in0=k.ps[:, 4 + u % 4, 0:D], scalar=mix[:, i, bass.ds(pair * 2 + a, 1)], in1=xsl,
                            op0=ALU.mult, op1=ALU.add).then_inc(S["mixed"], 1)

                def body(pair):
                    for j in range(STEPS):
                        low_hidden(pair, j)
                        if j:
                            add_expert(pair, j - 1)
                    add_expert(pair, STEPS - 1)

                pairs(dve, body)

            @block.scalar
            def _(act):
                act.sem_inc(S["raised"], 2)
                emit_sqrt(k, act, mv, S["stats_ready"], S["sqrt_ready"])

                def keep_turned(i, o):
                    act.wait_ge(S["turned"], i + 1)
                    if not isinstance(i, int) or i >= 4:
                        act.wait_ge(S["gated"], i - 3)
                        act.wait_ge(S["split_x"], i - 3)
                    turned = k.ps[:, o % 2, 0:D].rearrange("p (c n) -> p c n", n=P)
                    nc.scalar.copy(xt[:, o, :, :], turned).then_inc(S["turned_copied"], 1)
                    nc.scalar.copy(xt_h[:, :, bass.ts(i, P)], turned).then_inc(S["halved"], 1)

                staggered(act, [(keep_turned, 0)])
                act.wait_ge(S["gap"], 1)
                nc.scalar.activation(best[:, 3, :], best[:, 3, :], ACT.Exp).then_inc(S["gap_exp"], 1)

                def copy_mix(i, o):
                    act.wait_ge(S["mix_turned"], i + 1)
                    if not isinstance(i, int) or i >= 4:
                        act.wait_ge(S["based"], i - 3)
                    nc.scalar.copy(mix_t[:, o, :], k.ps[0:NE, o, 0:P]).then_inc(S["mix_copied"], 1)

                staggered(act, [(copy_mix, 1)])

                def body(pair):
                    for j in range(STEPS):
                        n = pair * STEPS + j
                        act.wait_ge(S["projected"], n * U + (BEFORE - U))
                        for m in range(EK):
                            q = n * EK + m
                            act.wait_ge(S["hidden"], q + 1)
                            act.wait_ge(S["active"], q + 1)
                            nc.scalar.activation(
                                act_out[:, m % 2, :].rearrange("p (a b) -> p a b", b=HALF),
                                k.ps[:, 2 * (m % 2):2 * (m % 2) + 2, 0:HALF], ACT.Relu,
                                bias=b1[:, j // GROUPS, m:m + 1]).then_inc(S["raised"], 1)
                            act.wait_ge(S["raised"], q + 3)
                            nc.scalar.copy(hid_h[:, j % 2, m, :], act_out[:, m % 2, :]).then_inc(S["high_ready"], 1)

                act.sem_inc(S["active"], 2)
                pairs(act, body)

            @block.tensor
            def _(pe):
                pe.sem_inc(S["projected"], BEFORE)
                pe.wait_ge(S["gate_loaded"], 64)

                def turn(i, o):
                    pe.wait_ge(S["normed"], i + 1)
                    if not isinstance(i, int) or i >= 2:
                        pe.wait_ge(S["halved"], i - 1)
                    for c in range(KC):
                        last = nc.tensor.transpose(k.ps[:, o % 2, bass.ts(c, P)], xn[:, o, bass.ts(c, P)], k.ident[:])
                    last.then_inc(S["turned"], 1)

                def gate(i, o):
                    pe.wait_ge(S["turned_copied"], i + 1)
                    for c in range(KC):
                        last = nc.tensor.matmul(k.ps[:, 7, bass.ts(i, NE)], xt[:, o, c, :], w_gate[:, c, :],
                                                start=c == 0, stop=c == KC - 1)
                    last.then_inc(S["gated"], 1)

                staggered(pe, [(turn, 0), (gate, 1)])
                def turn_mix(i, o):
                    if not isinstance(i, int) or i >= 4:
                        pe.wait_ge(S["mix_copied"], i - 3)
                    pe.wait_ge(S["mix_staged"], i + 1)
                    nc.tensor.transpose(k.ps[0:NE, o, 0:P], mix_now[:, o, :],
                                        k.ident[:]).then_inc(S["mix_turned"], 1)

                def base(i, o):
                    pe.wait_ge(S["mix_copied"], i + 1)
                    if not isinstance(i, int) or i >= 2:
                        pe.wait_ge(S["base_added"], i - 1)
                    nc.tensor.matmul(k.ps[:, 4 + o % 2, 0:D], mix_t[:, o, :], b2[:], start=True,
                                     stop=True).then_inc(S["based"], 1)

                staggered(pe, [(turn_mix, 0), (base, 1)])
                pe.wait_ge(S["base_added"], NT)
                pe.wait_ge(S["split_x"], NT)

                def hidden(pair, j):
                    a, g = j // GROUPS, j % GROUPS
                    if g == 0:
                        pe.wait_ge(S["weights_split"], pair * 8 + (4 * a + 5))
                    for m in range(EK):
                        q = (pair * STEPS + j) * EK + m
                        pe.wait_ge(S["raised"], q + 1)
                        for h in range(2):
                            at = g * TOK + h * HALF
                            for c in range(KC):
                                w_h, w_l = (w[:, a, c, bass.ts(m, P)] for w in (w1_h, w1_l))
                                x_h, x_l = (x[:, c, at:at + HALF] for x in (xt_h, xt_l))
                                for w, x in ((w_h, x_h), (w_h, x_l), (w_l, x_h)):
                                    last = nc.tensor.matmul(k.ps[:, 2 * (m % 2) + h, 0:HALF], w, x,
                                                            start=c == 0 and x is x_h and w is w_h,
                                                            stop=c == KC - 1 and w is w_l)
                        last.then_inc(S["hidden"], 1)

                def project(pair, j):
                    a, n = j // GROUPS, pair * STEPS + j
                    pe.wait_ge(S["active"], n * EK + (EK + 2))
                    for u in range(U):
                        if u in (0, 4):
                            pe.wait_ge(S["mixed"], n * U + (OLD + u // 4))
                        for m in range(EK):
                            x_h, x_l = (x[:, j % 2, m, bass.ts(u, P)] for x in (hid_h, hid_l))
                            w_h, w_l = w2_h[:, a, m, :], w2_l[:, a, m, :]
                            for x, w in ((x_h, w_h), (x_h, w_l), (x_l, w_h)):
                                last = nc.tensor.matmul(k.ps[:, 4 + u % 4, 0:D], x, w,
                                                        start=m == 0 and x is x_h and w is w_h,
                                                        stop=m == EK - 1 and x is x_l)
                        last.then_inc(S["projected"], 1)

                def body(pair):
                    for j in range(STEPS):
                        hidden(pair, j)
                        if j:
                            project(pair, j - 1)
                    project(pair, STEPS - 1)

                pairs(pe, body)


def build(nc, t):
    ctx = ExitStack()
    with ctx:
        def sb(name, shape, dtype=F32):
            return ctx.enter_context(nc.sbuf_tensor(name, shape, dtype))

        k = Kept(nc, t)
        k.ps = ctx.enter_context(nc.psum_tensor("banks", [P, 8, 512], F32))
        k.xs = sb("xs", [P, NT * D])
        k.er = sb("er", [P, NT * H1])
        k.ident, k.ones = sb("ident", [P, P]), sb("ones", [P, P])
        k.tri_incl, k.tri_strict = sb("tri_incl", [P, P]), sb("tri_strict", [P, P])
        k.iota, k.mask = sb("iota", [P, P]), sb("mask", [P, NT])
        k.dst_i, k.src_i = sb("dst_i", [P, EC], I32), sb("src_i", [P, EC], I32)
        k.dst_f = sb("dst_f", [P, EC])
        k.ones_e, k.unsorted = sb("ones_e", [P, EC]), sb("unsorted", [1, 1], I32)
        k.pos_i, k.edge_rec = sb("pos_i", [P, EC], I32), sb("edge_rec", [P, EC * 2], I32)
        k.base_dst, k.base_src = sb("base_dst", [P, ST]), sb("base_src", [P, ST])
        k.start_dst, k.start_src = sb("start_dst", [1, ST], I32), sb("start_src", [1, ST], I32)
        k.tile_dst, k.tile_src = sb("tile_dst", [1, ST], I32), sb("tile_src", [1, ST], I32)
        do(k, setup)
        _, falls = nc.values_load_multi_w_load_instructions(k.unsorted[0:1, 0:1], min_val=0, max_val=EP)
        with nc.If(falls[0] != 0):
            do(k, sort_pass, 0, P)
            do(k, sort_pass, 7, NT)
        do(k, gat_tables)
        do(k, gat_scores)
        do(k, gat_edges)
        with nc.sbuf_tensor("large", [P, NT * (2 * D + 1)], F32) as k.large:
            k.source_part, k.sums = k.large[:, 0:NT * D], k.large[:, NT * D:]
            k.new_rows = k.source_part
            do(k, slice_attention)
            do(k, message_tables)
            do(k, message_edges)
            do(k, gated_update)
        do(k, experts)


_LAYOUT = {
    "x": ("x", lambda a: a), "src": ("src", lambda a: a), "dst": ("dst", lambda a: a),
    "dst_following": ("dst", lambda a: a[EC::EC].reshape(EFULL, 1)),
    "w_lin": ("L0_gnn_W_lin", lambda a: a), "w_lin_t": ("L0_gnn_W_lin", lambda a: a.T),
    "b_lin": ("L0_gnn_b_lin", lambda a: a), "b_lin_cols": ("L0_gnn_b_lin", lambda a: a.reshape(KC, P).T),
    "w_gat": ("L0_gnn_W_gat", lambda a: a),
    "attn_l": ("L0_gnn_attn_l", lambda a: a), "attn_r": ("L0_gnn_attn_r", lambda a: a),
    "gat_bias": ("L0_gnn_gat_bias", lambda a: a),
    "w_fx": ("L0_ffn_W_fx", lambda a: a), "b_fx": ("L0_ffn_b_fx", lambda a: a),
    "w_x_t": ("L0_ffn_W_x", lambda a: a.T), "b_x_cols": ("L0_ffn_b_x", lambda a: a.reshape(SH, SD).T),
    "w_slice": ("L0_ffn_W_slice", lambda a: a), "b_slice": ("L0_ffn_b_slice", lambda a: a),
    "w_q": ("L0_ffn_W_q", lambda a: a), "w_k": ("L0_ffn_W_k", lambda a: a), "w_v": ("L0_ffn_W_v", lambda a: a),
    "w_out": ("L0_ffn_W_out", lambda a: a), "b_out": ("L0_ffn_b_out", lambda a: a),
    "temp": ("L0_ffn_temperature", lambda a: a.reshape(-1)),
    "w1_t": ("L1_gnn_W1", lambda a: a.T), "b1": ("L1_gnn_b1", lambda a: a),
    "w2": ("L1_gnn_W2", lambda a: a), "b2_cols": ("L1_gnn_b2", lambda a: a.reshape(KC, P).T),
    "w_ih_t": ("L1_gnn_w_ih", lambda a: a.T), "w_hh_t": ("L1_gnn_w_hh", lambda a: a.T),
    "b_ih": ("L1_gnn_b_ih", lambda a: a), "b_hh": ("L1_gnn_b_hh", lambda a: a),
    "gamma": ("L1_gnn_gamma", lambda a: a), "beta": ("L1_gnn_beta", lambda a: a),
    "w_gate": ("L1_ffn_Wg", lambda a: a), "b_gate": ("L1_ffn_bg", lambda a: a),
    "gate_bias": ("L1_ffn_bias", lambda a: a),
    "e_w1": ("L1_ffn_W1", lambda a: a), "e_b1_cols": ("L1_ffn_b1", lambda a: a.reshape(NE * EK, P).T),
    "e_w2": ("L1_ffn_W2", lambda a: a), "e_b2": ("L1_ffn_b2", lambda a: a),
}
_TABLES = {
    "gat_rows": ((NP, D), F32), "el_rows": ((NP, H1), F32),
    "rec_gat": ((ER, RW), I32), "rec_src": ((ER, 2), I32), "rec_sort": ((EP, 2), I32), "msg_rows": ((NP, D), F32),
    "slice_bias": ((SH, SD), F32),
}


def kernel(**inputs):
    import numpy as np
    import concourse.bacc as bacc
    from concourse.bass_utils import run_bass_kernel_spmd as run

    nc = bacc.Bacc("TRN2", target_bir_lowering=False, num_devices=1)
    tables, arrays = {}, {}
    for name, (source, lay) in _LAYOUT.items():
        a = np.ascontiguousarray(lay(np.asarray(inputs[source])))
        arrays["in_" + name] = a
        tables[name] = nc.dram_tensor("in_" + name, a.shape, mybir.dt.from_np(a.dtype), kind="ExternalInput").ap()
    for name, (shape, dtype) in _TABLES.items():
        tables[name] = nc.dram_tensor("tab_" + name, list(shape), dtype, kind="Internal").ap()
    tables["out"] = nc.dram_tensor("out_0_dram", (N, D), F32, kind="ExternalOutput").ap()
    build(nc, tables)
    return run(nc, [arrays], core_ids=[0]).results[0]["out_0_dram"]
```
